# Optimizing a Trainium2 kernel written in Bass

```python
import numpy as np
import jax
import jax.numpy as jnp

def _softmax(x, axis=-1):
    return jax.nn.softmax(x, axis=axis)

def _gelu(x):
    return jax.nn.gelu(x, approximate=True)

def _silu(x):
    return jax.nn.silu(x)

def _sigmoid(x):
    return jax.nn.sigmoid(x)

def _layernorm(x, axis=-1, eps=1e-05):
    m = jnp.mean(x, axis=axis, keepdims=True)
    v = jnp.var(x, axis=axis, keepdims=True)
    return (x - m) / jnp.sqrt(v + eps)

def _scatter_add(tgt, idx, src, axis=0):
    return tgt.at[idx].add(src)

def _segment_sum(src, seg, n):
    return jax.ops.segment_sum(src, seg, n)
kernel_name = 'mk_gnn_preln_d4_gnn_r32_ba7d56'

def setup_inputs(seed: int=0):
    np.random.seed(seed)
    _w = jnp.asarray

    def _rec_inputs():
        import jax
        import jax.numpy as jnp
        _gk = jax.random.key(seed)
        x = -0.0005121 + 1.001 * jax.random.normal(jax.random.fold_in(_gk, 1), (3125, 64), jnp.float32)
        _s = jax.random.randint(jax.random.fold_in(_gk, 2), (25000,), 0, 3125, jnp.int32)
        _d = jax.random.randint(jax.random.fold_in(_gk, 3), (25000,), 0, 3125, jnp.int32)
        _loop = jnp.arange(3125, dtype=jnp.int32)
        src = jnp.concatenate([_s, _d, _loop])
        dst = jnp.concatenate([_d, _s, _loop])
        _o = jnp.argsort(dst, stable=True)
        src = src[_o]
        dst = dst[_o]
        edge_attr_3 = 0.00117183 + 1.0004 * jax.random.normal(jax.random.fold_in(_gk, 13), (53125, 3), jnp.float32)
        edge_attr_64 = 7.68618e-05 + 1.00005 * jax.random.normal(jax.random.fold_in(_gk, 14), (53125, 64), jnp.float32)
        edge_weight = jax.random.uniform(jax.random.fold_in(_gk, 16), (53125,), jnp.float32, 0.0, 1)
        return (x, src, dst, edge_attr_3, edge_attr_64, edge_weight)
    x, src, dst, edge_attr_3, edge_attr_64, edge_weight = _rec_inputs()

    def _L0_gnn_setup():
        import jax, jax.numpy as jnp
        import numpy as np
        N_NODES = 50000
        N_EDGES = 25000
        D_IN = 64
        D_OUT = 64
        key = jax.random.key(seed)
        ks = jax.random.split(key, 8)
        feat = jax.random.normal(ks[0], (N_NODES, D_IN), dtype=jnp.float32)
        weight = jax.random.uniform(ks[1], (N_EDGES,), dtype=jnp.float32)
        W_self = jax.random.normal(ks[2], (D_OUT, D_IN), dtype=jnp.float32) * 0.1
        b_self = jax.random.normal(ks[3], (D_OUT,), dtype=jnp.float32) * 0.1
        W_neigh = jax.random.normal(ks[4], (D_OUT, D_IN), dtype=jnp.float32) * 0.1
        b_neigh = jax.random.normal(ks[5], (D_OUT,), dtype=jnp.float32) * 0.1
        src = jax.random.randint(ks[6], (N_EDGES,), 0, N_NODES, dtype=jnp.int64)
        dst = jax.random.randint(ks[7], (N_EDGES,), 0, N_NODES, dtype=jnp.int64)
        return {'feat': feat, 'weight': weight, 'W_self': W_self, 'b_self': b_self, 'W_neigh': W_neigh, 'b_neigh': b_neigh, 'src': src, 'dst': dst}
    _L0_gnn_all = _L0_gnn_setup()
    _L0_gnn_in = {k: v for k, v in _L0_gnn_all.items() if k in ('W_self', 'b_self', 'W_neigh', 'b_neigh')}
    del _L0_gnn_all

    def _L1_gnn_setup():
        import jax, jax.numpy as jnp
        import numpy as np
        M = 50000
        E = 25000
        C_IN = 64
        C_OUT = 64
        DIM = 3
        RADIUS = 1.0
        EPS = 1e-05

        def layer_norm(x, g, b):
            mu = jnp.mean(x, axis=-1, keepdims=True)
            var = jnp.mean((x - mu) ** 2, axis=-1, keepdims=True)
            return (x - mu) * jax.lax.rsqrt(var + EPS) * g + b
        key = jax.random.key(seed)
        ks = jax.random.split(key, 12)
        inv = 1.0 / np.sqrt(C_OUT)
        return {'source': jax.random.randint(ks[0], (E,), 0, M), 'target': jax.random.randint(ks[1], (E,), 0, M), 'features': jax.random.normal(ks[2], (M, C_IN), dtype=jnp.float32), 'hood_coords': jax.random.normal(ks[3], (E, DIM), dtype=jnp.float32), 'Wd1': jax.random.normal(ks[4], (DIM, C_OUT), dtype=jnp.float32) / np.sqrt(DIM), 'bd1': jnp.zeros((C_OUT,), jnp.float32), 'g1': jnp.ones((C_OUT,), jnp.float32), 'b1': jnp.zeros((C_OUT,), jnp.float32), 'Wd2': jax.random.normal(ks[5], (C_OUT, C_OUT), dtype=jnp.float32) * inv, 'bd2': jnp.zeros((C_OUT,), jnp.float32), 'g2': jnp.ones((C_OUT,), jnp.float32), 'b2': jnp.zeros((C_OUT,), jnp.float32), 'W1': jax.random.normal(ks[6], (C_IN, C_OUT), dtype=jnp.float32) / np.sqrt(C_IN), 'W2': jax.random.normal(ks[7], (C_IN, C_OUT), dtype=jnp.float32) / np.sqrt(C_IN), 'W3': jax.random.normal(ks[8], (C_IN, C_OUT), dtype=jnp.float32) / np.sqrt(C_IN)}
    _L1_gnn_all = _L1_gnn_setup()
    _L1_gnn_in = {k: v for k, v in _L1_gnn_all.items() if k in ('Wd1', 'bd1', 'g1', 'b1', 'Wd2', 'bd2', 'g2', 'b2', 'W1', 'W2', 'W3')}
    del _L1_gnn_all

    def _L2_gnn_setup():
        import jax, jax.numpy as jnp
        import numpy as np
        EPS = 1e-05

        def _mlp(h, W, b, gamma, beta):
            h = h @ W + b
            mu = jnp.mean(h, axis=0)
            var = jnp.var(h, axis=0)
            h = (h - mu) * jax.lax.rsqrt(var + EPS) * gamma + beta
            return h * jax.nn.sigmoid(h)
        key = jax.random.key(seed)
        ks = jax.random.split(key, 10)
        N, E, D, G = (3125, 31250, 64, 16)
        x = jax.random.normal(ks[0], (N, D), dtype=jnp.float32)
        edge_index = jax.random.randint(ks[1], (2, E), 0, N, dtype=jnp.int64)
        edge_attr = jax.random.normal(ks[2], (E, D), dtype=jnp.float32)
        u = jax.random.normal(ks[3], (G, D), dtype=jnp.float32)
        batch = jax.random.randint(ks[4], (N,), 0, G, dtype=jnp.int64)
        s1 = 1.0 / np.sqrt(2 * D)
        W1 = jax.random.uniform(ks[5], (2 * D, D), jnp.float32, -s1, s1)
        b1 = jax.random.uniform(ks[6], (D,), jnp.float32, -s1, s1)
        W2 = jax.random.uniform(ks[7], (2 * D, D), jnp.float32, -s1, s1)
        b2 = jax.random.uniform(ks[8], (D,), jnp.float32, -s1, s1)
        g1 = jnp.ones((D,), jnp.float32)
        be1 = jnp.zeros((D,), jnp.float32)
        g2 = jnp.ones((D,), jnp.float32)
        be2 = jnp.zeros((D,), jnp.float32)
        return {'x': x, 'edge_attr': edge_attr, 'u': u, 'W1': W1, 'b1': b1, 'g1': g1, 'be1': be1, 'W2': W2, 'b2': b2, 'g2': g2, 'be2': be2, 'edge_index': edge_index, 'batch': batch}
    _L2_gnn_all = _L2_gnn_setup()
    _L2_gnn_in = {k: v for k, v in _L2_gnn_all.items() if k in ('u', 'W1', 'b1', 'g1', 'be1', 'W2', 'b2', 'g2', 'be2')}
    del _L2_gnn_all

    def _L3_gnn_setup():
        import jax, jax.numpy as jnp
        import numpy as np
        N_NODES = 3125
        N_EDGES = 1250000
        D_FEAT = 64
        key = jax.random.key(seed)
        k1, k2 = jax.random.split(key)
        x = jax.random.normal(k1, (N_NODES, D_FEAT), dtype=jnp.float32)
        edge_index = jax.random.randint(k2, (2, N_EDGES), 0, N_NODES, dtype=jnp.int64)
        return {'x': x, 'edge_index': edge_index}
    _L3_gnn_all = _L3_gnn_setup()
    _L3_gnn_in = {k: v for k, v in _L3_gnn_all.items() if k in ()}
    del _L3_gnn_all
    return {'x': x, 'src': src, 'dst': dst, 'edge_attr_3': edge_attr_3, 'edge_attr_64': edge_attr_64, 'edge_weight': edge_weight, 'L0_gnn_W_self': _L0_gnn_in['W_self'], 'L0_gnn_b_self': _L0_gnn_in['b_self'], 'L0_gnn_W_neigh': _L0_gnn_in['W_neigh'], 'L0_gnn_b_neigh': _L0_gnn_in['b_neigh'], 'L1_gnn_Wd1': _L1_gnn_in['Wd1'], 'L1_gnn_bd1': _L1_gnn_in['bd1'], 'L1_gnn_g1': _L1_gnn_in['g1'], 'L1_gnn_b1': _L1_gnn_in['b1'], 'L1_gnn_Wd2': _L1_gnn_in['Wd2'], 'L1_gnn_bd2': _L1_gnn_in['bd2'], 'L1_gnn_g2': _L1_gnn_in['g2'], 'L1_gnn_b2': _L1_gnn_in['b2'], 'L1_gnn_W1': _L1_gnn_in['W1'], 'L1_gnn_W2': _L1_gnn_in['W2'], 'L1_gnn_W3': _L1_gnn_in['W3'], 'L2_gnn_u': _L2_gnn_in['u'], 'L2_gnn_W1': _L2_gnn_in['W1'], 'L2_gnn_b1': _L2_gnn_in['b1'], 'L2_gnn_g1': _L2_gnn_in['g1'], 'L2_gnn_be1': _L2_gnn_in['be1'], 'L2_gnn_W2': _L2_gnn_in['W2'], 'L2_gnn_b2': _L2_gnn_in['b2'], 'L2_gnn_g2': _L2_gnn_in['g2'], 'L2_gnn_be2': _L2_gnn_in['be2']}

def reference(x, src, dst, edge_attr_3, edge_attr_64, edge_weight, L0_gnn_W_self, L0_gnn_b_self, L0_gnn_W_neigh, L0_gnn_b_neigh, L1_gnn_Wd1, L1_gnn_bd1, L1_gnn_g1, L1_gnn_b1, L1_gnn_Wd2, L1_gnn_bd2, L1_gnn_g2, L1_gnn_b2, L1_gnn_W1, L1_gnn_W2, L1_gnn_W3, L2_gnn_u, L2_gnn_W1, L2_gnn_b1, L2_gnn_g1, L2_gnn_be1, L2_gnn_W2, L2_gnn_b2, L2_gnn_g2, L2_gnn_be2):
    import jax
    import jax.numpy as jnp

    def _L0_gnn_ref(feat, weight, W_self, b_self, W_neigh, b_neigh, src, dst):
        import jax, jax.numpy as jnp
        import numpy as np
        N_NODES = 50000
        N_EDGES = 25000
        D_IN = 64
        D_OUT = 64
        n = feat.shape[0]
        msg = feat[src] * weight[:, None]
        neigh_sum = jax.ops.segment_sum(msg, dst, num_segments=n)
        deg = jax.ops.segment_sum(jnp.ones_like(weight), dst, num_segments=n)
        h_neigh = neigh_sum / jnp.maximum(deg, 1.0)[:, None]
        rst = feat @ W_self.T + b_self + (h_neigh @ W_neigh.T + b_neigh)
        return rst

    def _L1_gnn_ref(source, target, features, hood_coords, Wd1, bd1, g1, b1, Wd2, bd2, g2, b2, W1, W2, W3):
        import jax, jax.numpy as jnp
        import numpy as np
        M = 50000
        E = 25000
        C_IN = 64
        C_OUT = 64
        DIM = 3
        RADIUS = 1.0
        EPS = 1e-05

        def layer_norm(x, g, b):
            mu = jnp.mean(x, axis=-1, keepdims=True)
            var = jnp.mean((x - mu) ** 2, axis=-1, keepdims=True)
            return (x - mu) * jax.lax.rsqrt(var + EPS) * g + b
        m = features.shape[0]
        x = hood_coords / RADIUS
        d = jax.nn.gelu(layer_norm(x @ Wd1 + bd1, g1, b1), approximate=False)
        d = jax.nn.gelu(layer_norm(d @ Wd2 + bd2, g2, b2), approximate=False)
        w1 = features @ W1
        w2 = features @ W2
        w3 = features @ W3
        logits = w1[target] - w2[source] + d
        seg_max = jax.ops.segment_max(logits, target, num_segments=m)
        seg_max = jnp.where(jnp.isfinite(seg_max), seg_max, 0.0)
        e = jnp.exp(logits - seg_max[target])
        denom = jax.ops.segment_sum(e, target, num_segments=m)
        a = e / denom[target]
        out = jax.ops.segment_sum(a * (w3[source] + d), target, num_segments=m)
        return out

    def _L2_gnn_ref(x, edge_attr, u, W1, b1, g1, be1, W2, b2, g2, be2, edge_index, batch):
        import jax, jax.numpy as jnp
        import numpy as np
        EPS = 1e-05

        def _mlp(h, W, b, gamma, beta):
            h = h @ W + b
            mu = jnp.mean(h, axis=0)
            var = jnp.var(h, axis=0)
            h = (h - mu) * jax.lax.rsqrt(var + EPS) * gamma + beta
            return h * jax.nn.sigmoid(h)
        N = x.shape[0]
        row, col = (edge_index[0], edge_index[1])
        msg = _mlp(jnp.concatenate([x[row], edge_attr], axis=1), W1, b1, g1, be1)
        sums = jax.ops.segment_sum(msg, col, num_segments=N)
        cnt = jax.ops.segment_sum(jnp.ones((msg.shape[0],), msg.dtype), col, num_segments=N)
        agg = sums / jnp.maximum(cnt, 1.0)[:, None]
        return _mlp(jnp.concatenate([x, agg], axis=1), W2, b2, g2, be2)

    def _L3_gnn_ref(x, edge_index):
        import jax, jax.numpy as jnp
        import numpy as np
        N_NODES = 3125
        N_EDGES = 1250000
        D_FEAT = 64
        msgs = x[edge_index[1]]
        out = jax.ops.segment_sum(msgs, edge_index[0], num_segments=x.shape[0])
        return out
    edge_index = jnp.stack([src, dst])
    batch0 = jnp.zeros((3125,), jnp.int32)
    h = jnp.maximum(_layernorm(x, axis=-1), 0.0)
    x = x + _L0_gnn_ref(h, edge_weight, L0_gnn_W_self, L0_gnn_b_self, L0_gnn_W_neigh, L0_gnn_b_neigh, src, dst)
    h = jnp.maximum(_layernorm(x, axis=-1), 0.0)
    x = x + _L1_gnn_ref(src, dst, h, edge_attr_3, L1_gnn_Wd1, L1_gnn_bd1, L1_gnn_g1, L1_gnn_b1, L1_gnn_Wd2, L1_gnn_bd2, L1_gnn_g2, L1_gnn_b2, L1_gnn_W1, L1_gnn_W2, L1_gnn_W3)
    h = jnp.maximum(_layernorm(x, axis=-1), 0.0)
    x = x + _L2_gnn_ref(h, edge_attr_64, L2_gnn_u, L2_gnn_W1, L2_gnn_b1, L2_gnn_g1, L2_gnn_be1, L2_gnn_W2, L2_gnn_b2, L2_gnn_g2, L2_gnn_be2, edge_index, batch0)
    h = jnp.maximum(_layernorm(x, axis=-1), 0.0)
    x = x + _L3_gnn_ref(h, edge_index)
    return x

_drawn_inputs = setup_inputs


def setup_inputs(seed=0):
    import zlib

    import numpy as np

    out = dict(_drawn_inputs(seed))
    spreads = {'L1_gnn_bd1': (0.0, 0.1),
     'L1_gnn_g1': (1.0, 0.2),
     'L1_gnn_b1': (0.0, 0.1),
     'L1_gnn_bd2': (0.0, 0.1),
     'L1_gnn_g2': (1.0, 0.2),
     'L1_gnn_b2': (0.0, 0.1),
     'L2_gnn_g1': (1.0, 0.6),
     'L2_gnn_be1': (0.0, 2.0),
     'L2_gnn_g2': (1.0, 0.2),
     'L2_gnn_be2': (0.0, 0.1)}
    factors = {'edge_weight': 5.052, 'L1_gnn_W1': 64.0, 'L2_gnn_b1': 64.0, 'L2_gnn_b2': 64.0}
    for name, (base, spread) in spreads.items():
        noise = np.random.default_rng([zlib.crc32(name.encode()), seed]).standard_normal(out[name].shape)
        drawn = base * np.exp(spread * noise) if base else spread * noise
        out[name] = jnp.asarray(drawn.astype(out[name].dtype))
    for name, factor in factors.items():
        out[name] = (out[name] * factor).astype(out[name].dtype)
    return out
```

```python
import numpy as np
import concourse.bass as bass
from concourse import mybir
from contextlib import ExitStack

F32 = mybir.dt.float32
BF16 = mybir.dt.bfloat16
I32 = mybir.dt.int32
U32 = mybir.dt.uint32
ALU = mybir.AluOpType
ACT = mybir.ActivationFunctionType
AX = mybir.AxisListType.X

N, D, E = 3125, 64, 53125
CH = 512
J = CH // 128
HALF = -(-E // (2 * CH)) * CH
NCH = HALF // CH
NIT = NCH // 2
B0 = E - HALF
OVER = HALF - B0
LASTA = CH - OVER
NB = -(-N // 128)
NBP = NB + 1
NPAIR = NBP // 2
NLAST = N - (NB - 1) * 128
NW = NBP * D
NV = NB * D
HR, HC = 125, E // 125
HSTEP = 2 * 8
HPRE = HC - NIT * HSTEP
BIG = 1e30
EPS = 1e-5


def build(nc, T, out):
    ctx = ExitStack()
    with ctx:
        def sb(name, shape, dt=F32):
            return ctx.enter_context(nc.sbuf_tensor(name, shape, dt))

        sems = {}

        def S(name, slot=None):
            key = name if slot is None else f"{name} [{slot}]"
            if key not in sems:
                sems[key] = ctx.enter_context(nc.semaphore(key.replace(" ", "_").strip("]").replace("[", "")))
            return sems[key]

        ring_unit = {
            "L0 msg made": 1, "L0 weight loaded": 32, "L1 w2 transposed": 1, "d loaded": 16, "d made": 1,
            "d stored": 16, "damp made": 1, "diff made": 1, "dst loaded": 32, "ea loaded": 32,
            "ea product made": 1, "ea transposed": 1, "eaT copied": 1, "edges activated": 1, "eu made": 1,
            "evacuated": 1, "expd made": 1, "hidden made": 1, "hidden summed": 1,
            "idx loaded": 32, "in transposed": 1, "keep made": 1, "logits made": 1, "m carried": 1,
            "m scanned": 1, "mlp1 made": 1, "mlp2 made": 1, "neg made": 1, "norm1 made": 1,
            "norm1 transposed": 1, "norm2 made": 1, "norm2 transposed": 1, "out transposed": 1,
            "s scanned": 1, "scan stored": 32, "scanned": 1, "sq1 made": 1, "sq2 made": 1,
            "squares1 summed": 1, "squares2 summed": 1, "u made": 1, "x3 copied": 1, "x3 loaded": 32,
            "x3 transposed": 1, "y1 made": 1,
        }

        def past(n, each=1):
            return (n + 1) * each

        def n_chunks(before, n, each=1):
            return past(n + before * NIT, each)

        def n_idx_loaded(layer, n):
            return n_chunks(layer, n, 32)

        def n_gathered(layer, n):
            return (n + layer * NIT) * 128

        def n_scan_stored(layer, n):
            return n_chunks(layer, n, 32)

        def n_scanned(layer, n):
            return n_chunks(layer, n)

        def n_out_transposed(layer, n):
            return n_chunks(layer, n)

        def n_evacuated(layer, n):
            return n_chunks(layer, n)

        def n_in_transposed(layer, n):
            return n_chunks((0, 1, None, 2)[layer], n)

        stages = {
            "PE": ("L0 weights transposed", "h0 transposed", "self made", "first hist added",
                "prefix made", "agg0 transposed", "neigh made", "h1 transposed", "w2 made", "w3 made",
                "w1 made", "h2 transposed", "w1a made", "edge bn mean summed", "edge bn var summed",
                "agg2 transposed", "z made", "node bn mean summed", "node bn var summed", "z transposed"),
            "ACT": ("L0 weights copied", "h0T copied", "agg0T copied", "h1T copied", "w2 copied", "w3 copied",
                "w1 copied", "merge factors made", "h2T copied", "w1a copied", "agg2T copied", "z copied",
                "z activated"),
            "DVE": ("consts cleared", "h0 made", "weights ready", "x self added",
                "first onehots made", "counts copied", "rowidx made", "rows indexed", "L0 merged", "h1 made",
                "merge diffs made", "L1 merged", "h2 made", "edge bn mean part made", "edge bn var part made",
                "edge bn ready", "L2 merged", "node bn mean part made", "node bn var part made",
                "node bn ready", "x3 made", "h3 made", "x4 made"),
        }

        def stage(name):
            engine = next(e for e in stages if name in stages[e])
            return S(f"{engine} stages"), stages[engine].index(name) + 1

        def stage_of(name):
            counted.append(name)
            return stage(name)[0]

        counted = []

        def dram(name, shape):
            return nc.dram_tensor(name, shape, F32, kind="Internal").ap()

        tab = [dram("table0", (NBP * 128, D)), dram("table1", (NBP * 128, 2 * D)),
               dram("table2", (NBP * 128, D)), dram("table3", (NBP * 128, D))]
        segs = [dram("scan0", (2 * HALF, D)), dram("scan1", (2 * HALF, 3 * D)),
                dram("scan2", (2 * HALF, D)), dram("scan3", (2 * HALF, D))]
        d_dram = dram("d_mlp", (128, HALF))

        keep = sb("keep", [128, HALF], BF16)
        arena = sb("arena", [128, HALF])
        x = sb("x", [128, NBP, D])
        hT = sb("hT", [128, NPAIR * 128])
        W = sb("W", [128, 12, 128])
        WSELF, WNEIGH, WD2, W1, W2, W3, W1A, W1B, W2A, W2B, WSELF_T, WNEIGH_T = range(12)
        cols = sb("cols", [128, 12])
        BD1, G1, B1, BD2, G2, B2, LB1, LG1, LBE1, LB2, LG2, LBE2 = range(12)
        Wd1 = sb("Wd1", [3 * 2 * J, J * 2, D])
        bias0 = sb("bias0", [128, 2, D])
        ident = sb("ident", [128, 128])
        ones = sb("ones", [128, 128])
        upper = sb("upper", [128, 128])
        both = sb("both", [128, 128])
        small = sb("small", [128, 8, 32])
        rowidx = sb("rowidx", [128, NB], U32)
        degpos = sb("degpos", [128, NB])
        invdeg = sb("invdeg", [128, NB])
        span = sb("span", [128, NB])
        negspan = sb("negspan", [128, NB])
        tail = sb("tail", [128, 3 * D])
        stats = sb("stats", [128, NCH * 6])
        bnw = sb("bnw", [128, 2])
        bn = sb("bn", [128, 8])
        brow = sb("brow", [1, 2, J * 2, D])
        rs = sb("rs", [128, 3, 32])
        idx = [sb(f"idx{k}", [128, 2 * J], I32) for k in range(2)]
        Gring = [sb(f"gathered{k}", [128, J * 2 * 2 * D]) for k in range(2)]

        def Gw(k, width):
            return Gring[k][:, 0:J * 2 * width].rearrange("p (j h d) -> p j h d", h=2, d=width)

        def pair(k, j):
            return Gring[k][:, j * 2 * D:(j + 1) * 2 * D]
        scanb = [sb(f"scan_ring{k}", [128, CH]) for k in range(2)]
        ostage = [sb(f"ostage{k}", [128, 2, J, D]) for k in range(2)]

        P = ctx.enter_context(nc.psum_tensor("psum", [128, 8, 512], F32))
        PF = P[:, :, :].rearrange("p b n -> p (b n)")

        def take(start):
            at = [start]

            def f(n):
                at[0] += n
                assert at[0] <= HALF
                return arena[:, at[0] - n:at[0]]
            return f

        a = take(0)
        wgt = [a(2 * J) for _ in range(2)]
        ea3 = [a(2 * J * 3) for _ in range(2)]
        dstb = [a(CH).bitcast(I32) for _ in range(2)]
        msg = [a(CH) for _ in range(2)]
        x3t, sq1, norm1, y1, sq2, norm2 = a(128), a(CH), a(CH), a(CH), a(CH), a(CH)
        dout = [a(CH) for _ in range(2)]
        dst_pm, dst_p, dst_b, iota_i = (a(HC).bitcast(I32), a(HC), a(HC), a(128).bitcast(I32))
        iota_f = a(128)
        one_p = a(HSTEP * 128 // 2).bitcast(BF16)
        one_b = a(HSTEP * NB // 2).bitcast(BF16)
        a = take(0)
        dch = [a(CH) for _ in range(2)]
        logit, neg, u1, eu = a(CH), a(CH), a(CH), a(CH)
        diff, expd = a(2 * CH), a(2 * CH)
        damp = a(CH)
        mrun = [a(CH + 1) for _ in range(2)]
        srun = [a(CH) for _ in range(2)]
        orun = [a(CH) for _ in range(2)]
        ostage1 = [a(2 * J * 3 * D).rearrange("p (h j d) -> p h j d", h=2, j=J) for _ in range(2)]
        a = take(11800)
        h = a(NW).rearrange("p (b d) -> p b d", d=D)
        tmp = a(NW).rearrange("p (b d) -> p b d", d=D)
        agg = a(NB * 3 * D)
        tabs = a(NBP * 2 * D).rearrange("p (b d) -> p b d", d=2 * D)
        w1n = a(NV).rearrange("p (b d) -> p b d", d=D)
        ea64 = [sb(f"ea64_{k}", [128, J, 2, D]) for k in range(2)]
        eaT = Gring[0][:, CH:2 * CH]
        zact = [ea64[k][:, :, :, :].rearrange("p j h d -> p (j h d)") for k in range(2)]

        def chunk(vec, half, i, k, w=1):
            base = (B0 if half else 0) + k * CH
            return vec[bass.ds(i * (2 * CH) + base, CH)].rearrange("(p j) -> p j", j=J) if w == 1 else \
                vec[bass.ds(i * (2 * CH) + base, CH), :].rearrange("(p j) d -> p (j d)", j=J)

        def at(i, k, n=CH):
            return bass.ds(i * (2 * n) + k * n, n)

        def scan_rows(layer, half, i, k):
            return segs[layer][bass.ds(i * (2 * CH) + k * CH + half * HALF, CH), :] \
                .rearrange("(p j) d -> p (j d)", j=J)

        halves = (slice(0, 64), slice(64, 128))
        block = ctx.enter_context(nc.Block())

        @block.sync
        def _(sp):
            for name, unit in ring_unit.items():
                for k in range(2):
                    sp.sem_inc(S(name, k), unit)
            sp.sem_inc(S("hist added"), 1)
            sp.wait_ge(*stage("consts cleared"))
            sp.dma_start(x[:, 0:NB - 1, :], T["x"][0:(NB - 1) * 128, :].rearrange("(b p) d -> p b d", p=128)) \
                .then_inc(S("x loaded"), 16)
            sp.dma_start(x[0:NLAST, NB - 1, :], T["x"][(NB - 1) * 128:N, :]).then_inc(S("x loaded"), 16)
            sp.dma_start(dst_pm[0:HR, :], T["dst"].rearrange("(p t) -> p t", p=HR)).then_inc(S("dst by row loaded"), 16)
            for half in range(2):
                sl = halves[half]
                for slot, m in ((WD2, T["L1_gnn_Wd2"]), (WSELF, T["L0_gnn_W_self"]), (WNEIGH, T["L0_gnn_W_neigh"]),
                                (W1, T["L1_gnn_W1"]), (W2, T["L1_gnn_W2"]), (W3, T["L1_gnn_W3"]),
                                (W1A, T["L2_gnn_W1"][0:D, :]), (W1B, T["L2_gnn_W1"][D:2 * D, :]),
                                (W2A, T["L2_gnn_W2"][0:D, :]), (W2B, T["L2_gnn_W2"][D:2 * D, :])):
                    sp.dma_start(W[sl, slot, sl], m).then_inc(S("weights loaded"), 16)
                for j in range(J):
                    r = half * 3 * J + 3 * j
                    sp.dma_start(Wd1[r:r + 3, 2 * j + half, :], T["L1_gnn_Wd1"]).then_inc(S("weights loaded"), 16)
            for n, b in enumerate((T["L1_gnn_bd1"], T["L1_gnn_bd2"])):
                sp.dma_start(brow[:, n, :, :], b.partition_broadcast(J * 2).unsqueeze(0)) \
                    .then_inc(S("weights loaded"), 16)
            for n, b in enumerate((T["L0_gnn_b_self"], T["L0_gnn_b_neigh"])):
                sp.dma_start(bias0[:, n, :], b.partition_broadcast(128)).then_inc(S("weights loaded"), 16)

            sp.wait_ge(*stage("h0 made"))
            sp.dma_start(tab[0].rearrange("(b p) d -> p b d", p=128), h).then_inc(S("table stored", 0), 16)

            with sp.Fori(0, NIT) as i:
                for k in range(2):
                    sp.wait_ge(S("L0 msg made", k), past(i))
                    for hf in range(2):
                        sp.dma_start(idx[k][:, hf * J:(hf + 1) * J], chunk(T["src"], hf, i, k)) \
                            .then_inc(S("idx loaded", k), 16)
                    for hf in range(2):
                        sp.dma_start(wgt[k][:, hf * J:(hf + 1) * J], chunk(T["edge_weight"], hf, i, k)) \
                            .then_inc(S("L0 weight loaded", k), 16)
                    sp.wait_ge(S("x3 transposed", k), past(i))
                    for hf in range(2):
                        sp.dma_start(ea3[k][:, hf * 3 * J:(hf + 1) * 3 * J], chunk(T["edge_attr_3"], hf, i, k, 3)) \
                            .then_inc(S("x3 loaded", k), 16)
                    sp.wait_ge(S("keep made", 1 - k), past(i + k))
                    for hf in range(2):
                        vec = T["dst"][bass.ds(i * (2 * CH) + k * CH + hf * B0, CH)]
                        sp.dma_start(dstb[k][halves[hf], :], vec.partition_broadcast(64)) \
                            .then_inc(S("dst loaded", k), 16)

            def tail_row(layer, w):
                for k in range(2):
                    sp.wait_ge(S("scan stored", k), n_scan_stored(layer, NIT))
                sp.dma_start(tail[:, 0:w], segs[layer][B0 - 1, :].partition_broadcast(128)) \
                    .then_inc(S("tail loaded", layer), 16)

            def node_table(layer, made, src):
                sp.wait_ge(*stage(made))
                sp.dma_start(tab[layer].rearrange("(b p) d -> p b d", p=128), src).then_inc(S("table stored", layer), 16)

            tail_row(0, D)
            node_table(1, "w3 copied", tabs)
            with sp.Fori(0, NIT) as i:
                for k in range(2):
                    sp.wait_ge(S("in transposed", k), n_in_transposed(1, i))
                    for hf in range(2):
                        sp.dma_start(idx[k][:, hf * J:(hf + 1) * J], chunk(T["src"], hf, i, k)) \
                            .then_inc(S("idx loaded", k), 16)
                    sp.wait_ge(S("u made", k), past(i))
                    sp.dma_start(dch[k], d_dram[:, at(i, k)]).then_inc(S("d loaded", k), 16)
            sp.wait_ge(*stage("L0 merged"))
            tail_row(1, 3 * D)
            node_table(2, "w1a copied", tabs[:, :, 0:D])
            with sp.Fori(0, NIT) as i:
                for k in range(2):
                    sp.wait_ge(S("hidden made", k), past(i))
                    for hf in range(2):
                        sp.dma_start(idx[k][:, hf * J:(hf + 1) * J], chunk(T["src"], hf, i, k)) \
                            .then_inc(S("idx loaded", k), 16)
                    sp.wait_ge(S("ea transposed", k), past(i))
                    for hf in range(2):
                        rows = T["edge_attr_64"][bass.ds(i * (2 * CH) + k * CH + hf * B0, CH), :]
                        sp.dma_start(ea64[k][:, :, hf, :], rows.rearrange("(p j) d -> p j d", j=J)) \
                            .then_inc(S("ea loaded", k), 16)
            sp.wait_ge(*stage("L1 merged"))
            tail_row(2, D)
            node_table(3, "h3 made", h)
            with sp.Fori(0, NIT) as i:
                for k in range(2):
                    sp.wait_ge(S("in transposed", k), n_in_transposed(3, i))
                    for hf in range(2):
                        sp.dma_start(idx[k][:, hf * J:(hf + 1) * J], chunk(T["src"], hf, i, k)) \
                            .then_inc(S("idx loaded", k), 16)
            sp.wait_ge(*stage("L2 merged"))
            tail_row(3, D)
            sp.wait_ge(*stage("x4 made"))
            sp.dma_start(out[0:(NB - 1) * 128, :].rearrange("(b p) d -> p b d", p=128), x[:, 0:NB - 1, :]) \
                .then_inc(S("out stored"), 16)
            sp.dma_start(out[(NB - 1) * 128:N, :], x[0:NLAST, NB - 1, :]).then_inc(S("out stored"), 16)
            sp.wait_ge(S("out stored"), 32)

        @block.gpsimd
        def _(pool):
            pool.memset(ident[:, :], 0.0).then_inc(S("consts begun"), 1)
            pool.memset(upper[:, :], 1.0).then_inc(S("consts begun"), 1)
            pool.iota(iota_i, [[1, 128]], base=0, channel_multiplier=0).then_inc(S("iota made"), 1)
            pool.wait_ge(S("consts begun"), 2)
            pool.affine_select(out=ident[:, :], in_=ident[:, :], compare_op=ALU.not_equal, fill=1.0, base=0,
                               pattern=[[-1, 128]], channel_multiplier=1).then_inc(S("ident made"), 1)
            pool.affine_select(out=upper[:, :], in_=upper[:, :], compare_op=ALU.is_ge, fill=0.0, base=0,
                               pattern=[[1, 128]], channel_multiplier=-1).then_inc(S("ident made"), 1)

            def gathers(layer, width, freed, freed_n=None):
                with pool.Fori(0, NIT) as i:
                    for k in range(2):
                        pool.wait_ge(S("table stored", layer), 16)
                        pool.wait_ge(S("idx loaded", k), n_idx_loaded(layer, i + 1))
                        pool.wait_ge(S(freed, k), (freed_n or past)(i))
                        pool.sem_inc(S("chunk cleared"), 1)
                        for j in range(J):
                            for hf in range(2):
                                q = hf * J + j
                                pool.indirect_dma_start(
                                    out=Gw(k, width)[:, j, hf, :], out_offset=None, in_=tab[layer],
                                    in_offset=bass.IndirectOffsetOnAxis(ap=idx[k][:, q:q + 1].bitcast(U32), axis=0)) \
                                    .then_inc(S("gathered", k), 16)

            def last_rows(layer, width):
                for k in range(2):
                    pool.wait_ge(S("scan stored", k), n_scan_stored(layer, NIT))
                for b in range(NB):
                    pool.indirect_dma_start(
                        out=agg[:, b * width:(b + 1) * width], out_offset=None, in_=segs[layer],
                        in_offset=bass.IndirectOffsetOnAxis(ap=rowidx[:, b:b + 1], axis=0)) \
                        .then_inc(S("last rows", layer), 16)

            gathers(0, D, "L0 msg made")
            pool.wait_ge(*stage("rowidx made"))
            last_rows(0, D)
            gathers(1, 2 * D, "in transposed", lambda n: n_in_transposed(1, n))
            last_rows(1, 3 * D)
            gathers(2, D, "hidden made")
            last_rows(2, D)
            gathers(3, D, "in transposed", lambda n: n_in_transposed(3, n))
            last_rows(3, D)

        @block.tensor
        def _(pe):
            def to_channels(src, made, done, b=0):
                pe.wait_ge(*stage(made))
                for q in range(NPAIR):
                    last = nc.tensor.transpose(PF[:, b * 512 + q * 128:b * 512 + (q + 1) * 128],
                                               src[:, 2 * q:2 * q + 2, :].rearrange("p b d -> p (b d)"), ident[:, :])
                last.then_inc(stage_of(done), 1)

            def linear(rhs, b, done):
                for q in range(NPAIR):
                    last = nc.tensor.matmul(PF[:, b * 512 + q * 128:b * 512 + (q + 1) * 128],
                                            hT[:, q * 128:(q + 1) * 128], rhs, start=True, stop=True)
                last.then_inc(stage_of(done), 1)

            pe.wait_ge(S("ident made"), 2)
            pe.wait_ge(*stage("weights ready"))
            for n in range(2):
                last = nc.tensor.transpose(P[:, 0, n * 128:(n + 1) * 128], W[:, WSELF + n, :], ident[:, :])
            last.then_inc(stage_of("L0 weights transposed"), 1)
            pe.wait_ge(*stage("L0 weights copied"))
            to_channels(h, "h0 made", "h0 transposed")
            pe.wait_ge(*stage("h0T copied"))
            linear(W[:, WSELF_T, :], 4, "self made")
            pe.wait_ge(*stage("x self added"))
            pe.wait_ge(*stage("first onehots made"))
            for t in range(HPRE):
                last = nc.tensor.matmul(P[:, 7, 0:NB], one_p[0:HR, t * 128:(t + 1) * 128],
                                        one_b[0:HR, t * NB:(t + 1) * NB], start=(t == 0), stop=True,
                                        skip_group_check=True)
            last.then_inc(stage_of("first hist added"), 1)

            with pe.Fori(0, NIT) as i:
                for k in range(2):
                    pe.wait_ge(S("x3 loaded", k), past(i + 1, 32))
                    pe.wait_ge(S("x3 copied", 1 - k), past(i + k))
                    nc.tensor.transpose(P[0:24, 0, 0:128], ea3[k], ident[:, :]).then_inc(S("x3 transposed", k), 1)
                    pe.wait_ge(S("x3 copied", k), past(i + 1))
                    pe.wait_ge(S("norm1 made", 1 - k), past(i + k))
                    nc.tensor.matmul(P[:, 1, :], ones[0:1, :], brow[:, 0, :, :].rearrange("p r d -> p (r d)"),
                                     start=True, stop=False)
                    nc.tensor.matmul(P[:, 1, :], x3t[0:24, :], Wd1[:, :, :].rearrange("p r d -> p (r d)"),
                                     start=False, stop=True).then_inc(S("mlp1 made", k), 1)
                    pe.wait_ge(S("L0 msg made", k), past(i + 1))
                    pe.wait_ge(S("scanned", 1 - k), n_scanned(0, i + k))
                    for j in range(J):
                        last = nc.tensor.transpose(P[:, 5, j::J], msg[k][:, j * 128:(j + 1) * 128], ident[:, :])
                    last.then_inc(S("in transposed", k), 1)
                    pe.wait_ge(S("norm1 made", k), past(i + 1))
                    pe.wait_ge(S("y1 made", 1 - k), past(i + k))
                    for j in range(J):
                        last = nc.tensor.transpose(P[:, 2, j::J], norm1[:, j * 128:(j + 1) * 128], ident[:, :])
                    last.then_inc(S("norm1 transposed", k), 1)
                    pe.wait_ge(S("y1 made", k), past(i + 1))
                    pe.wait_ge(S("norm2 made", 1 - k), past(i + k))
                    nc.tensor.matmul(P[:, 3, :], ones[0:1, :], brow[:, 1, :, :].rearrange("p r d -> p (r d)"),
                                     start=True, stop=True)
                    for j in range(J):
                        last = nc.tensor.matmul(P[:, 3, j * 128:(j + 1) * 128], y1[:, j::J], W[:, WD2, :],
                                                start=False, stop=True, skip_group_check=True)
                    last.then_inc(S("mlp2 made", k), 1)
                    pe.wait_ge(S("norm2 made", k), past(i + 1))
                    pe.wait_ge(S("d made", 1 - k), past(i + k))
                    for j in range(J):
                        last = nc.tensor.transpose(P[:, 4, j::J], norm2[:, j * 128:(j + 1) * 128], ident[:, :])
                    last.then_inc(S("norm2 transposed", k), 1)
                    pe.wait_ge(S("scanned", k), n_scanned(0, i + 1))
                    pe.wait_ge(S("evacuated", 1 - k), n_evacuated(0, i + k))
                    for j in range(J):
                        last = nc.tensor.transpose(P[:, 6, j * 128:(j + 1) * 128], scanb[k][:, j::J], ident[:, :])
                    last.then_inc(S("out transposed", k), 1)
                pe.wait_ge(S("onehots made"), i + 1)
                for t in range(HSTEP):
                    last = nc.tensor.matmul(P[:, 7, 0:NB], one_p[0:HR, t * 128:(t + 1) * 128],
                                            one_b[0:HR, t * NB:(t + 1) * NB], start=False, stop=True,
                                            skip_group_check=True)
                last.then_inc(S("hist added"), 1)

            pe.wait_ge(*stage("counts copied"))
            pe.wait_ge(S("evacuated", 1), n_evacuated(0, NIT))
            nc.tensor.matmul(P[:, 6, 0:NB], upper[:, :], small[:, 0, 0:NB], start=True, stop=True)
            nc.tensor.matmul(P[:, 6, 32:32 + NB], ones[:, :], small[:, 0, 0:NB], start=True, stop=True) \
                .then_inc(stage_of("prefix made"), 1)

            to_channels(tmp, "L0 merged", "agg0 transposed")
            pe.wait_ge(*stage("agg0T copied"))
            pe.wait_ge(*stage("rows indexed"))
            linear(W[:, WNEIGH_T, :], 4, "neigh made")
            to_channels(h, "h1 made", "h1 transposed")
            pe.wait_ge(*stage("h1T copied"))
            linear(W[:, W2, :], 4, "w2 made")
            linear(W[:, W3, :], 0, "w3 made")
            pe.wait_ge(*stage("w2 copied"))
            linear(W[:, W1, :], 4, "w1 made")
            pe.wait_ge(*stage("w3 copied"))
            pe.wait_ge(*stage("w1 copied"))

            with pe.Fori(0, NIT) as i:
                for k in range(2):
                    pe.wait_ge(S("gathered", k), n_gathered(1, i + 1))
                    pe.wait_ge(S("logits made", 1 - k), past(i + k))
                    for j in range(J):
                        for hf in range(2):
                            last = nc.tensor.matmul(P[halves[hf], 0, j::J], Gw(k, 2 * D)[:, j, hf, 0:D], ident[:, :],
                                                    start=True, stop=True)
                    last.then_inc(S("L1 w2 transposed", k), 1)
                    pe.wait_ge(S("u made", 1 - k), past(i + k))
                    for j in range(J):
                        for hf in range(2):
                            last = nc.tensor.matmul(P[halves[hf], 1, j::J], Gw(k, 2 * D)[:, j, hf, D:2 * D], ident[:, :],
                                                    start=True, stop=True)
                    last.then_inc(S("in transposed", k), 1)
                    pe.wait_ge(S("scanned", k), n_scanned(1, i + 1))
                    pe.wait_ge(S("evacuated", 1 - k), n_evacuated(1, i + k))
                    for n, run in enumerate((mrun[k][:, 1:CH + 1], srun[k], orun[k])):
                        for j in range(J):
                            last = nc.tensor.transpose(P[:, 2 + n, j * 128:(j + 1) * 128], run[:, j::J], ident[:, :])
                    last.then_inc(S("out transposed", k), 1)

            pe.wait_ge(S("evacuated", 1), n_evacuated(1, NIT))
            to_channels(h, "h2 made", "h2 transposed")
            pe.wait_ge(*stage("h2T copied"))
            linear(W[:, W1A, :], 4, "w1a made")
            pe.wait_ge(*stage("w1a copied"))

            with pe.Fori(0, NIT) as i:
                for k in range(2):
                    pe.wait_ge(S("ea loaded", k), past(i + 1, 32))
                    pe.wait_ge(S("eaT copied", k), past(i))
                    for j in range(J):
                        last = nc.tensor.transpose(P[:, k, j::J], ea64[k][:, j, :, :].rearrange("p h d -> p (h d)"), ident[:, :])
                    last.then_inc(S("ea transposed", k), 1)
                    pe.wait_ge(S("eaT copied", k), past(i + 1))
                    pe.wait_ge(S("hidden made", k), past(i))
                    nc.tensor.matmul(P[:, 2 + k, :], W[:, W1B, :], eaT, start=True, stop=True) \
                        .then_inc(S("ea product made", k), 1)
                    pe.wait_ge(S("gathered", k), n_gathered(2, i + 1))
                    for j in range(J):
                        last = nc.tensor.matmul(P[:, 2 + k, j::J], pair(k, j), ident[:, :],
                                                start=False, stop=True, skip_group_check=True)
                    last.then_inc(S("hidden summed", k), 1)

            def combine(tag):
                for n, name in enumerate(("mean", "var")):
                    pe.wait_ge(*stage(f"{tag} {name} part made"))
                    nc.tensor.matmul(P[:, 7, n:n + 1], both[:, :], bn[:, 2 + n:3 + n], start=True, stop=True) \
                        .then_inc(stage_of(f"{tag} {name} summed"), 1)

            combine("edge bn")
            with pe.Fori(0, NIT) as i:
                for k in range(2):
                    pe.wait_ge(S("scanned", k), n_scanned(2, i + 1))
                    pe.wait_ge(S("evacuated", k), n_evacuated(2, i))
                    for j in range(J):
                        last = nc.tensor.transpose(P[:, k, j * 128:(j + 1) * 128], scanb[k][:, j::J], ident[:, :])
                    last.then_inc(S("out transposed", k), 1)

            pe.wait_ge(S("evacuated", 0), n_evacuated(2, NIT))
            pe.wait_ge(S("evacuated", 1), n_evacuated(2, NIT))
            to_channels(tmp, "L2 merged", "agg2 transposed")
            pe.wait_ge(*stage("agg2T copied"))
            pe.wait_ge(*stage("edge bn ready"))
            for q in range(4):
                w = min(512, NPAIR * 128 - q * 512)
                nc.tensor.matmul(P[:, 4 + q, 0:w], W[:, W2A, :], hT[:, q * 512:q * 512 + w], start=True, stop=False)
                last = nc.tensor.matmul(P[:, 4 + q, 0:w], W[:, W2B, :], agg[:, q * 512:q * 512 + w],
                                        start=False, stop=True)
            last.then_inc(stage_of("z made"), 1)
            pe.wait_ge(*stage("z copied"))
            combine("node bn")
            pe.wait_ge(*stage("z activated"))
            for q in range(NPAIR):
                last = nc.tensor.transpose(PF[:, q * 128:(q + 1) * 128], agg[:, q * 128:(q + 1) * 128], ident[:, :])
            last.then_inc(stage_of("z transposed"), 1)
            pe.wait_ge(*stage("x3 made"))

            with pe.Fori(0, NIT) as i:
                for k in range(2):
                    pe.wait_ge(S("gathered", k), n_gathered(3, i + 1))
                    pe.wait_ge(S("scanned", k), n_scanned(3, i))
                    for j in range(J):
                        last = nc.tensor.transpose(P[:, 4 + k, j::J], pair(k, j), ident[:, :])
                    last.then_inc(S("in transposed", k), 1)
                    pe.wait_ge(S("scanned", k), n_scanned(3, i + 1))
                    pe.wait_ge(S("evacuated", k), n_evacuated(3, i))
                    for j in range(J):
                        last = nc.tensor.transpose(P[:, 6 + k, j * 128:(j + 1) * 128], scanb[k][:, j::J], ident[:, :])
                    last.then_inc(S("out transposed", k), 1)

        @block.scalar
        def _(act):
            act.wait_ge(*stage("consts cleared"))
            for n, name in enumerate(("L1_gnn_bd1", "L1_gnn_g1", "L1_gnn_b1", "L1_gnn_bd2", "L1_gnn_g2", "L1_gnn_b2",
                                      "L2_gnn_b1", "L2_gnn_g1", "L2_gnn_be1", "L2_gnn_b2", "L2_gnn_g2", "L2_gnn_be2")):
                for hf in range(2):
                    act.dma_start(cols[halves[hf], n:n + 1], T[name].rearrange("(p a) -> p a", a=1)) \
                        .then_inc(S("columns loaded"), 16)

            def copy(dst, src, need, done, scale=1.0):
                act.wait_ge(*stage(need))
                nc.scalar.activation(dst, src, ACT.Copy, scale=scale).then_inc(stage_of(done), 1)

            def evacuate(layer, i, k, bank):
                act.wait_ge(S("out transposed", k), n_out_transposed(layer, i + 1))
                act.wait_ge(S("scan stored", k), n_scan_stored(layer, i))
                nc.scalar.activation(ostage[k][:, :, :, :].rearrange("p h j d -> p j h d"),
                                     P[:, bank, :].rearrange("p (j h d) -> p j h d", h=2, d=D), ACT.Copy) \
                    .then_inc(S("evacuated", k), 1)
                act.wait_ge(S("evacuated", k), n_evacuated(layer, i + 1))
                for hf in range(2):
                    act.dma_start(scan_rows(layer, hf, i, k), ostage[k][:, hf, :, :].rearrange("p j d -> p (j d)")) \
                        .then_inc(S("scan stored", k), 16)

            copy(W[:, WSELF_T:WNEIGH_T + 1, :].rearrange("p a d -> p (a d)"), P[:, 0, 0:256],
                 "L0 weights transposed", "L0 weights copied")
            copy(hT[:, :], PF[:, 0:NPAIR * 128], "h0 transposed", "h0T copied")

            with act.Fori(0, NIT) as i:
                for k in range(2):
                    act.wait_ge(S("x3 transposed", k), past(i + 1))
                    act.wait_ge(S("mlp1 made", 1 - k), past(i + k))
                    nc.scalar.activation(x3t[0:24, :], P[0:24, 0, 0:128], ACT.Copy).then_inc(S("x3 copied", k), 1)
                    act.wait_ge(S("mlp1 made", k), past(i + 1))
                    act.wait_ge(S("squares1 summed", 1 - k), past(i + k))
                    nc.scalar.activation(sq1, P[:, 1, :], ACT.Square).then_inc(S("sq1 made", k), 1)
                    act.wait_ge(S("norm1 transposed", k), past(i + 1))
                    act.wait_ge(S("mlp2 made", 1 - k), past(i + k))
                    nc.scalar.activation(y1, P[:, 2, :], ACT.Gelu, bias=cols[:, B1:B1 + 1], scale=cols[:, G1:G1 + 1]) \
                        .then_inc(S("y1 made", k), 1)
                    act.wait_ge(S("mlp2 made", k), past(i + 1))
                    act.wait_ge(S("squares2 summed", 1 - k), past(i + k))
                    nc.scalar.activation(sq2, P[:, 3, :], ACT.Square).then_inc(S("sq2 made", k), 1)
                    act.wait_ge(S("norm2 transposed", k), past(i + 1))
                    act.wait_ge(S("d stored", k), past(i, 16))
                    nc.scalar.activation(dout[k], P[:, 4, :], ACT.Gelu, bias=cols[:, B2:B2 + 1], scale=cols[:, G2:G2 + 1]) \
                        .then_inc(S("d made", k), 1)
                    act.wait_ge(S("d made", k), past(i + 1))
                    act.dma_start(d_dram[:, at(i, k)], dout[k]).then_inc(S("d stored", k), 16)
                    evacuate(0, i, k, 6)

            copy(hT[:, :], PF[:, 0:NPAIR * 128], "agg0 transposed", "agg0T copied")
            copy(hT[:, :], PF[:, 0:NPAIR * 128], "h1 transposed", "h1T copied")
            bank4 = PF[:, 2048:2048 + NW].rearrange("p (b d) -> p b d", d=D)
            bank0 = PF[:, 0:NW].rearrange("p (b d) -> p b d", d=D)
            copy(tabs[:, :, 0:D], bank4, "w2 made", "w2 copied", scale=-1.0)
            copy(tabs[:, :, D:2 * D], bank0, "w3 made", "w3 copied")
            copy(w1n, bank4[:, 0:NB, :], "w1 made", "w1 copied")
            for k in range(2):
                act.wait_ge(S("d stored", k), past(NIT, 16))
                act.wait_ge(S("keep made", k), past(NIT))

            with act.Fori(0, NIT) as i:
                for k in range(2):
                    act.wait_ge(S("m scanned", 1 - k), past(i + k))
                    nc.scalar.activation(neg, keep[:, at(i, k)], ACT.Copy, scale=BIG, bias=-BIG) \
                        .then_inc(S("neg made", k), 1)
                    act.wait_ge(S("diff made", k), past(i + 1))
                    act.wait_ge(S("scanned", 1 - k), n_scanned(1, i + k))
                    nc.scalar.activation(expd, diff, ACT.Exp).then_inc(S("expd made", k), 1)
                    act.wait_ge(S("out transposed", k), n_out_transposed(1, i + 1))
                    act.wait_ge(S("scan stored", k), n_scan_stored(1, i))
                    for n in range(3):
                        last = nc.scalar.activation(
                            ostage1[k][:, :, :, n * D:(n + 1) * D].rearrange("p h j d -> p j h d"),
                            P[:, 2 + n, :].rearrange("p (j h d) -> p j h d", h=2, d=D), ACT.Copy)
                    last.then_inc(S("evacuated", k), 1)
                    act.wait_ge(S("evacuated", k), n_evacuated(1, i + 1))
                    for hf in range(2):
                        act.dma_start(scan_rows(1, hf, i, k), ostage1[k][:, hf, :, :].rearrange("p j d -> p (j d)")) \
                            .then_inc(S("scan stored", k), 16)

            act.wait_ge(*stage("merge diffs made"))
            nc.scalar.activation(tabs[:, 0:NB, :], tabs[:, 0:NB, :], ACT.Exp).then_inc(stage_of("merge factors made"), 1)
            copy(hT[:, :], PF[:, 0:NPAIR * 128], "h2 transposed", "h2T copied")
            copy(tabs[:, :, 0:D], bank4, "w1a made", "w1a copied")

            with act.Fori(0, NIT) as i:
                for k in range(2):
                    act.wait_ge(S("ea transposed", k), past(i + 1))
                    act.wait_ge(S("ea product made", 1 - k), past(i + k))
                    nc.scalar.activation(eaT, P[:, k, :], ACT.Copy).then_inc(S("eaT copied", k), 1)
                    act.wait_ge(S("hidden summed", k), past(i + 1))
                    nc.scalar.activation(arena[:, at(i, k)], P[:, 2 + k, :], ACT.Identity, bias=cols[:, LB1:LB1 + 1]) \
                        .then_inc(S("hidden made", k), 1)

            act.wait_ge(*stage("edge bn ready"))
            with act.Fori(0, NIT) as i:
                for k in range(2):
                    act.wait_ge(S("scanned", k), n_scanned(2, i))
                    nc.scalar.activation(zact[k], arena[:, at(i, k)], ACT.Silu, bias=bn[:, 6:7], scale=bn[:, 5:6]) \
                        .then_inc(S("edges activated", k), 1)
                    evacuate(2, i, k, k)

            copy(agg[:, 0:NPAIR * 128], PF[:, 0:NPAIR * 128], "agg2 transposed", "agg2T copied")
            act.wait_ge(*stage("z made"))
            nc.scalar.activation(tabs[:, 0:NPAIR, :].rearrange("p b d -> p (b d)"), PF[:, 2048:2048 + NPAIR * 128],
                                 ACT.Identity, bias=cols[:, LB2:LB2 + 1]).then_inc(stage_of("z copied"), 1)
            act.wait_ge(*stage("node bn ready"))
            nc.scalar.activation(agg[:, 0:NPAIR * 128], tabs[:, 0:NPAIR, :].rearrange("p b d -> p (b d)"),
                                 ACT.Silu, bias=bn[:, 6:7], scale=bn[:, 5:6]).then_inc(stage_of("z activated"), 1)

            with act.Fori(0, NIT) as i:
                for k in range(2):
                    evacuate(3, i, k, 6 + k)

        @block.vector
        def _(dve):
            v = nc.vector
            steps = [0]

            def step(ins):
                steps[0] += 1
                ins.then_inc(S("dve step"), 1)
                dve.wait_ge(S("dve step"), steps[0])

            def bc(colmat, w=D):
                return colmat.unsqueeze(2).to_broadcast([128, NB, w])

            def rsqrt(n, step):
                arg, res, t = (rs[:, m, 0:n] for m in range(3))
                step(v.tensor_scalar(t.bitcast(I32), arg.bitcast(I32), 1, None, ALU.arith_shift_right))
                step(v.tensor_scalar(res.bitcast(I32), t.bitcast(I32), -1.0, float(0x5f3759df), ALU.mult, ALU.add))
                for _ in range(3):
                    step(v.scalar_tensor_tensor(t, res, -0.5, arg, ALU.mult, ALU.mult))
                    step(v.tensor_tensor(t, t, res, ALU.mult))
                    step(v.scalar_tensor_tensor(res, t, 1.5, res, ALU.add, ALU.mult))

            def layernorm_relu(dst, done):
                xs, xc, hs = x[:, 0:NB, :], tmp[:, 0:NB, :], dst[:, 0:NB, :]
                s1, s2 = small[:, 1, 0:NB], small[:, 2, 0:NB]
                step(v.reduce_sum(s1, xs, axis=AX))
                step(v.tensor_scalar(s1, s1, 1.0 / D, None, ALU.mult))
                step(v.tensor_tensor(xc, xs, bc(s1), ALU.subtract))
                step(v.tensor_tensor(hs, xc, xc, ALU.mult))
                step(v.reduce_sum(s2, hs, axis=AX))
                step(v.tensor_scalar(rs[:, 0, 0:NB], s2, 1.0 / D, EPS, ALU.mult, ALU.add))
                rsqrt(NB, step)
                step(v.scalar_tensor_tensor(hs, xc, 0.0, bc(rs[:, 1, 0:NB]), ALU.max, ALU.mult))
                dve.sem_inc(stage_of(done), 1)

            for t in (x[:, :, :], W[:, :, :], Wd1[:, :, :], h, both[:, :], scanb[1][:, :]):
                step(v.memset(t, 0.0))
            dve.sem_inc(stage_of("consts cleared"), 1)
            step(v.memset(ones[:, :], 1.0))
            for hf, (ne, nn) in zip(halves, ((B0, 64 * 0 + (NPAIR - 1) * 128 + NLAST), (HALF, (NPAIR - 1) * 128))):
                step(v.memset(bnw[hf, 0:1], ne / E))
                step(v.memset(bnw[hf, 1:2], nn / N))
            dve.wait_ge(S("x loaded"), 32)
            layernorm_relu(h, "h0 made")

            dve.wait_ge(S("ident made"), 2)
            for hf in halves:
                for hg in halves:
                    step(v.tensor_copy(both[hf, hg], ident[hf, hf]))
            dve.wait_ge(S("weights loaded"), 16 * 32)
            dve.wait_ge(S("columns loaded"), 16 * 24)
            for m, s in ((Wd1[:, :, :], small[0:24, 3, 0:2 * J]),
                         (brow[:, :, :, :].rearrange("p n r d -> p (n r) d"), small[0:1, 3, 0:4 * J]),
                         (W[:, WD2, :].rearrange("p (a d) -> p a d", d=D), small[:, 4, 0:2])):
                step(v.reduce_sum(s, m, axis=AX))
                step(v.tensor_scalar(s, s, 1.0 / D, None, ALU.mult))
                step(v.tensor_tensor(m, m, s.unsqueeze(2).to_broadcast(list(m.shape)), ALU.subtract))
            dve.sem_inc(stage_of("weights ready"), 1)
            dve.wait_ge(*stage("self made"))
            step(v.tensor_tensor(x[:, 0:NB, :], x[:, 0:NB, :], PF[:, 2048:2048 + NV].rearrange("p (b d) -> p b d", d=D),
                                 ALU.add))
            for n in range(2):
                step(v.tensor_tensor(x[:, 0:NB, :], x[:, 0:NB, :],
                                     bias0[:, n, :].unsqueeze(1).to_broadcast([128, NB, D]), ALU.add))
            dve.sem_inc(stage_of("x self added"), 1)
            dve.wait_ge(S("iota made"), 1)
            dve.wait_ge(S("dst by row loaded"), 16)
            step(v.tensor_copy(iota_f, iota_i))
            step(v.tensor_scalar(dst_b[0:HR, :].bitcast(I32), dst_pm[0:HR, :], 7, None, ALU.arith_shift_right))
            step(v.tensor_scalar(dst_pm[0:HR, :], dst_pm[0:HR, :], 127, None, ALU.bitwise_and))
            step(v.tensor_copy(dst_p[0:HR, :], dst_pm[0:HR, :]))
            step(v.tensor_copy(dst_b[0:HR, :], dst_b[0:HR, :].bitcast(I32)))

            def onehots(first, n):
                for key, dst, w in ((dst_p, one_p, 128), (dst_b, one_b, NB)):
                    last = v.tensor_tensor(dst[0:HR, 0:n * w].rearrange("p (t c) -> p t c", c=w),
                                           key[0:HR, first].unsqueeze(2).to_broadcast([HR, n, w]),
                                           iota_f[0:HR, 0:w].unsqueeze(1).to_broadcast([HR, n, w]), ALU.is_equal)
                return last

            onehots(slice(0, HPRE), HPRE).then_inc(stage_of("first onehots made"), 1)
            step(v.memset(dstb[1], -1))
            dve.wait_ge(*stage("first hist added"))

            with dve.Fori(0, NIT) as i:
                for k in range(2):
                    c0 = i * (2 * CH) + k * CH
                    dve.wait_ge(S("dst loaded", k), past(i + 1, 32))
                    dve.wait_ge(S("dst loaded", 1 - k), past(i + k, 32))
                    v.tensor_tensor(keep[:, bass.ds(c0, 1)], dstb[k][:, 0:1], dstb[1 - k][:, CH - 1:CH], ALU.is_equal)
                    v.tensor_tensor(keep[:, bass.ds(c0 + 1, CH - 1)], dstb[k][:, 1:CH], dstb[k][:, 0:CH - 1],
                                    ALU.is_equal).then_inc(S("keep made", k), 1)
                    for n, bank, sq, norm in ((1, 1, sq1, norm1), (2, 3, sq2, norm2)):
                        made = [0]

                        def norm_step(ins):
                            made[0] += 1
                            ins.then_inc(S("norm step"), 1)
                            dve.wait_ge(S("norm step"), i * 48 + (k * 24 + (n - 1) * 12 + made[0]))

                        dve.wait_ge(S(f"sq{n} made", k), past(i + 1))
                        v.reduce_sum(rs[:, 2, 0:2 * J], sq.rearrange("p (r d) -> p r d", d=D), axis=AX) \
                            .then_inc(S(f"squares{n} summed", k), 1)
                        dve.wait_ge(S(f"squares{n} summed", k), past(i + 1))
                        norm_step(v.tensor_scalar(rs[:, 0, 0:2 * J], rs[:, 2, 0:2 * J], 1.0 / D, EPS, ALU.mult, ALU.add))
                        rsqrt(2 * J, norm_step)
                        dve.wait_ge(S(f"norm{n} transposed", 1 - k), past(i + k))
                        v.tensor_tensor(norm.rearrange("p (r d) -> p r d", d=D),
                                        P[:, bank, :].rearrange("p (r d) -> p r d", d=D),
                                        rs[:, 1, 0:2 * J].unsqueeze(2).to_broadcast([128, 2 * J, D]), ALU.mult) \
                            .then_inc(S(f"norm{n} made", k), 1)
                        if n == 1:
                            dve.wait_ge(S("gathered", k), n_gathered(0, i + 1))
                            dve.wait_ge(S("L0 weight loaded", k), past(i + 1, 32))
                            dve.wait_ge(S("in transposed", k), n_in_transposed(0, i))
                            v.tensor_tensor(msg[k].rearrange("p (j h d) -> p j h d", h=2, d=D), Gw(k, D),
                                            wgt[k].rearrange("p (h j) -> p j h", h=2).unsqueeze(3)
                                            .to_broadcast([128, J, 2, D]), ALU.mult).then_inc(S("L0 msg made", k), 1)
                    dve.wait_ge(S("in transposed", k), n_in_transposed(0, i + 1))
                    dve.wait_ge(S("keep made", k), past(i + 1))
                    dve.wait_ge(S("scanned", 1 - k), n_scanned(0, i + k))
                    dve.wait_ge(S("out transposed", k), n_out_transposed(0, i))
                    v.tensor_tensor_scan(scanb[k][:, :], keep[:, bass.ds(c0, CH)], P[:, 5, :],
                                         scanb[1 - k][:, CH - 1:CH], ALU.mult, ALU.add).then_inc(S("scanned", k), 1)
                dve.wait_ge(S("hist added"), past(i))
                onehots(bass.ds(i * HSTEP + HPRE, HSTEP), HSTEP).then_inc(S("onehots made"), 1)

            cnt, pre, tot, incl, end, ge = (small[:, n, 0:NB] for n in range(6))
            dve.wait_ge(S("hist added"), past(NIT))
            step(v.tensor_copy(cnt, P[:, 7, 0:NB]))
            dve.sem_inc(stage_of("counts copied"), 1)
            dve.wait_ge(*stage("prefix made"))
            step(v.tensor_copy(pre, P[:, 6, 0:NB]))
            step(v.tensor_copy(tot, P[:, 6, 32:32 + NB]))
            step(v.tensor_tensor_scan(incl, ones[:, 0:NB], tot, 0.0, ALU.mult, ALU.add))
            step(v.tensor_tensor(end, incl, tot, ALU.subtract))
            step(v.tensor_tensor(end, end, pre, ALU.add))
            step(v.tensor_scalar(ge, end, float(B0 + 1), None, ALU.is_ge))
            step(v.tensor_tensor(span[:, :], end, cnt, ALU.subtract))
            step(v.tensor_scalar(span[:, :], span[:, :], float(B0), None, ALU.is_lt))
            step(v.tensor_tensor(span[:, :], span[:, :], ge, ALU.mult))
            step(v.tensor_scalar(negspan[:, :], span[:, :], BIG, -BIG, ALU.mult, ALU.add))
            step(v.tensor_scalar(end, end, -1.0, 0.0, ALU.add, ALU.max))
            step(v.scalar_tensor_tensor(end, ge, float(OVER), end, ALU.mult, ALU.add))
            step(v.tensor_copy(rowidx[:, :], end))
            dve.sem_inc(stage_of("rowidx made"), 1)
            step(v.tensor_scalar(degpos[:, :], cnt, 0.0, None, ALU.is_gt))
            step(v.tensor_scalar(end, cnt, 1.0, None, ALU.max))
            step(v.reciprocal(end, end))
            step(v.tensor_tensor(invdeg[:, :], degpos[:, :], end, ALU.mult))
            dve.sem_inc(stage_of("rows indexed"), 1)

            aggs = agg[:, 0:NV].rearrange("p (b d) -> p b d", d=D)

            def merge_sum(layer, factor, dst):
                dve.wait_ge(S("last rows", layer), 16 * NB)
                dve.wait_ge(S("tail loaded", layer), 16)
                step(v.tensor_tensor(dst, tail[:, 0:D].unsqueeze(1).to_broadcast([128, NB, D]), bc(span[:, :]), ALU.mult))
                step(v.tensor_tensor(dst, dst, aggs, ALU.add))
                step(v.tensor_tensor(dst, dst, bc(factor), ALU.mult))

            merge_sum(0, invdeg[:, :], tmp[:, 0:NB, :])
            step(v.memset(tmp[:, NB:NBP, :], 0.0))
            dve.sem_inc(stage_of("L0 merged"), 1)
            dve.wait_ge(*stage("neigh made"))
            step(v.tensor_tensor(x[:, 0:NB, :], x[:, 0:NB, :], PF[:, 2048:2048 + NV].rearrange("p (b d) -> p b d", d=D),
                                 ALU.add))
            layernorm_relu(h, "h1 made")

            step(v.memset(mrun[1][:, CH:CH + 1], -BIG))
            step(v.memset(srun[1][:, CH - 1:CH], 0.0))
            step(v.memset(orun[1][:, CH - 1:CH], 0.0))
            with dve.Fori(0, NIT) as i:
                for k in range(2):
                    dve.wait_ge(S("d loaded", k), past(i + 1, 16))
                    dve.wait_ge(S("L1 w2 transposed", k), past(i + 1))
                    v.tensor_tensor(logit, P[:, 0, :], dch[k], ALU.add).then_inc(S("logits made", k), 1)
                    dve.wait_ge(S("out transposed", k), n_out_transposed(1, i))
                    dve.wait_ge(S("m scanned", 1 - k), past(i + k))
                    v.tensor_copy(mrun[k][:, 0:1], mrun[1 - k][:, CH:CH + 1]).then_inc(S("m carried", k), 1)
                    dve.wait_ge(S("neg made", k), past(i + 1))
                    dve.wait_ge(S("logits made", k), past(i + 1))
                    dve.wait_ge(S("m carried", k), past(i + 1))
                    v.tensor_tensor_scan(mrun[k][:, 1:CH + 1], neg, logit, mrun[k][:, 0:1], ALU.add, ALU.max) \
                        .then_inc(S("m scanned", k), 1)
                    dve.wait_ge(S("m scanned", k), past(i + 1))
                    dve.wait_ge(S("expd made", 1 - k), past(i + k))
                    v.tensor_tensor(diff[:, CH:2 * CH], logit, mrun[k][:, 1:CH + 1], ALU.subtract)
                    v.tensor_tensor(diff[:, 0:CH], mrun[k][:, 0:CH], mrun[k][:, 1:CH + 1], ALU.subtract) \
                        .then_inc(S("diff made", k), 1)
                    dve.wait_ge(S("in transposed", k), n_in_transposed(1, i + 1))
                    v.tensor_tensor(u1, P[:, 1, :], dch[k], ALU.add).then_inc(S("u made", k), 1)
                    dve.wait_ge(S("expd made", k), past(i + 1))
                    v.scalar_tensor_tensor(damp, expd[:, 0:CH], 1.0, keep[:, at(i, k)], ALU.min, ALU.mult) \
                        .then_inc(S("damp made", k), 1)
                    dve.wait_ge(S("u made", k), past(i + 1))
                    v.tensor_tensor(eu, expd[:, CH:2 * CH], u1, ALU.mult).then_inc(S("eu made", k), 1)
                    dve.wait_ge(S("damp made", k), past(i + 1))
                    dve.wait_ge(S("scanned", 1 - k), n_scanned(1, i + k))
                    v.tensor_tensor_scan(srun[k], damp, expd[:, CH:2 * CH], srun[1 - k][:, CH - 1:CH],
                                         ALU.mult, ALU.add).then_inc(S("s scanned", k), 1)
                    dve.wait_ge(S("eu made", k), past(i + 1))
                    dve.wait_ge(S("s scanned", k), past(i + 1))
                    v.tensor_tensor_scan(orun[k], damp, eu, orun[1 - k][:, CH - 1:CH],
                                         ALU.mult, ALU.add).then_inc(S("scanned", k), 1)

            g = agg.rearrange("p (b d) -> p b d", d=3 * D)
            mB, sB, oB = g[:, :, 0:D], g[:, :, D:2 * D], g[:, :, 2 * D:3 * D]
            lA, lB, mx = tabs[:, 0:NB, 0:D], tabs[:, 0:NB, D:2 * D], tmp[:, 0:NB, :]

            def tail_bc(n):
                return tail[:, n * D:(n + 1) * D].unsqueeze(1).to_broadcast([128, NB, D])

            dve.wait_ge(S("last rows", 1), 16 * NB)
            dve.wait_ge(S("tail loaded", 1), 16)
            dve.wait_ge(*stage("w1 copied"))
            step(v.tensor_tensor(lA, tail_bc(0), bc(negspan[:, :]), ALU.add))
            step(v.tensor_tensor(lA, lA, w1n, ALU.add))
            step(v.tensor_tensor(lB, mB, w1n, ALU.add))
            step(v.tensor_tensor(mx, lA, lB, ALU.max))
            step(v.tensor_tensor(lA, lA, mx, ALU.subtract))
            step(v.tensor_tensor(lB, lB, mx, ALU.subtract))
            dve.sem_inc(stage_of("merge diffs made"), 1)
            dve.wait_ge(*stage("merge factors made"))
            for n, part in ((1, sB), (2, oB)):
                step(v.tensor_tensor(part, part, lB, ALU.mult))
                step(v.tensor_tensor(mx, tail_bc(n), lA, ALU.mult))
                step(v.tensor_tensor(part, part, mx, ALU.add))
            dve.sem_inc(stage_of("L1 merged"), 1)
            step(v.reciprocal(sB, sB))
            step(v.tensor_tensor(oB, oB, sB, ALU.mult))
            step(v.tensor_tensor(oB, oB, bc(degpos[:, :]), ALU.mult))
            step(v.tensor_tensor(x[:, 0:NB, :], x[:, 0:NB, :], oB, ALU.add))
            layernorm_relu(h, "h2 made")

            with dve.Fori(0, NIT) as i:
                for k in range(2):
                    dve.wait_ge(S("hidden made", k), past(i + 1))
                    v.bn_stats(stats[:, bass.ds(i * 12 + k * 6, 6)], arena[:, at(i, k)]).then_inc(S("stats made"), 1)
            dve.wait_ge(S("stats made"), NCH)
            step(v.bn_stats(stats[0:64, (NCH - 1) * 6:NCH * 6], arena[0:64, (NCH - 1) * CH:(NCH - 1) * CH + LASTA]))
            step(v.bn_aggr(bn[:, 0:2], stats[:, :]))

            def batchnorm(tag, wcol, gcol, bcol):
                share = bnw[:, wcol:wcol + 1]
                step(v.tensor_tensor(bn[:, 2:3], bn[:, 0:1], share, ALU.mult))
                dve.sem_inc(stage_of(f"{tag} mean part made"), 1)
                dve.wait_ge(*stage(f"{tag} mean summed"))
                step(v.tensor_copy(bn[:, 4:5], P[:, 7, 0:1]))
                step(v.tensor_tensor(bn[:, 7:8], bn[:, 0:1], bn[:, 4:5], ALU.subtract))
                step(v.tensor_tensor(bn[:, 7:8], bn[:, 7:8], bn[:, 7:8], ALU.mult))
                step(v.tensor_tensor(bn[:, 7:8], bn[:, 7:8], bn[:, 1:2], ALU.add))
                step(v.tensor_tensor(bn[:, 3:4], bn[:, 7:8], share, ALU.mult))
                dve.sem_inc(stage_of(f"{tag} var part made"), 1)
                dve.wait_ge(*stage(f"{tag} var summed"))
                step(v.tensor_scalar(rs[:, 0, 0:1], P[:, 7, 1:2], EPS, None, ALU.add))
                rsqrt(1, step)
                step(v.tensor_tensor(bn[:, 5:6], rs[:, 1, 0:1], cols[:, gcol:gcol + 1], ALU.mult))
                step(v.tensor_tensor(bn[:, 7:8], bn[:, 5:6], bn[:, 4:5], ALU.mult))
                step(v.tensor_tensor(bn[:, 6:7], cols[:, bcol:bcol + 1], bn[:, 7:8], ALU.subtract))
                dve.sem_inc(stage_of(f"{tag} ready"), 1)

            batchnorm("edge bn", 0, LG1, LBE1)

            step(v.memset(scanb[1][:, CH - 1:CH], 0.0))
            with dve.Fori(0, NIT) as i:
                for k in range(2):
                    dve.wait_ge(S("edges activated", k), past(i + 1))
                    dve.wait_ge(S("scanned", 1 - k), n_scanned(2, i + k))
                    dve.wait_ge(S("out transposed", k), n_out_transposed(2, i))
                    v.tensor_tensor_scan(scanb[k][:, :], keep[:, at(i, k)], zact[k],
                                         scanb[1 - k][:, CH - 1:CH], ALU.mult, ALU.add).then_inc(S("scanned", k), 1)

            merge_sum(2, invdeg[:, :], tmp[:, 0:NB, :])
            step(v.memset(tmp[:, NB:NBP, :], 0.0))
            dve.sem_inc(stage_of("L2 merged"), 1)
            dve.wait_ge(*stage("z copied"))
            z = tabs[:, 0:NPAIR, :].rearrange("p b d -> p (b d)")
            for n in range(3):
                step(v.bn_stats(stats[:, n * 6:(n + 1) * 6], z[:, n * 512:(n + 1) * 512]))
            step(v.bn_stats(stats[0:64, 18:24], z[0:64, 1536:1536 + NLAST]))
            step(v.bn_aggr(bn[0:64, 0:2], stats[0:64, 0:24]))
            step(v.bn_aggr(bn[64:128, 0:2], stats[64:128, 0:18]))
            batchnorm("node bn", 1, LG2, LBE2)
            dve.wait_ge(*stage("z transposed"))
            step(v.tensor_tensor(x[:, 0:NB, :], x[:, 0:NB, :], PF[:, 0:NV].rearrange("p (b d) -> p b d", d=D), ALU.add))
            dve.sem_inc(stage_of("x3 made"), 1)
            step(v.memset(h[:, NB:NBP, :], 0.0))
            layernorm_relu(h, "h3 made")

            step(v.memset(scanb[1][:, CH - 1:CH], 0.0))
            with dve.Fori(0, NIT) as i:
                for k in range(2):
                    dve.wait_ge(S("in transposed", k), n_in_transposed(3, i + 1))
                    dve.wait_ge(S("scanned", 1 - k), n_scanned(3, i + k))
                    dve.wait_ge(S("out transposed", k), n_out_transposed(3, i))
                    v.tensor_tensor_scan(scanb[k][:, :], keep[:, at(i, k)], P[:, 4 + k, :],
                                         scanb[1 - k][:, CH - 1:CH], ALU.mult, ALU.add).then_inc(S("scanned", k), 1)
            merge_sum(3, degpos[:, :], tmp[:, 0:NB, :])
            step(v.tensor_tensor(x[:, 0:NB, :], x[:, 0:NB, :], tmp[:, 0:NB, :], ALU.add))
            dve.sem_inc(stage_of("x4 made"), 1)

        for names in stages.values():
            assert [n for n in counted if n in names] == list(names)


def kernel(**inputs):
    import concourse.bacc as bacc
    from concourse.bass_utils import run_bass_kernel_spmd as run

    nc = bacc.Bacc("TRN2", target_bir_lowering=False, num_devices=1)
    arrays, args = {}, {}
    for name, value in inputs.items():
        value = np.ascontiguousarray(value)
        arrays[f"in_{name}"] = value
        args[name] = nc.dram_tensor(f"in_{name}", value.shape, mybir.dt.from_np(value.dtype),
                                    kind="ExternalInput").ap()
    out = nc.dram_tensor("out_x", (N, D), F32, kind="ExternalOutput").ap()
    build(nc, args, out)
    return run(nc, [arrays], core_ids=[0]).results[0]["out_x"]
```

```python
import numpy as np
import concourse.bass as bass
from concourse import mybir
from contextlib import ExitStack

F32 = mybir.dt.float32
BF16 = mybir.dt.bfloat16
I32 = mybir.dt.int32
U32 = mybir.dt.uint32
ALU = mybir.AluOpType
ACT = mybir.ActivationFunctionType
AX = mybir.AxisListType.X

N, D, E = 3125, 64, 53125
CH = 512
J = CH // 128
HALF = -(-E // (2 * CH)) * CH
NCH = HALF // CH
NIT = NCH // 2
B0 = E - HALF
OVER = HALF - B0
LASTA = CH - OVER
NB = -(-N // 128)
NBP = NB + 1
NPAIR = NBP // 2
NLAST = N - (NB - 1) * 128
NW = NBP * D
NV = NB * D
HR, HC = 125, E // 125
HSTEP = 2 * 8
HPRE = HC - NIT * HSTEP
BIG = 1e30
EPS = 1e-5


def build(nc, T, out):
    ctx = ExitStack()
    with ctx:
        def sb(name, shape, dt=F32):
            return ctx.enter_context(nc.sbuf_tensor(name, shape, dt))

        sems = {}

        def S(name, slot=None):
            key = name if slot is None else f"{name} [{slot}]"
            if key not in sems:
                sems[key] = ctx.enter_context(nc.semaphore(key.replace(" ", "_").strip("]").replace("[", "")))
            return sems[key]

        ring_unit = {
            "L0 msg made": 1, "L0 weight loaded": 16, "L1 w2 transposed": 1, "L1 split": 1, "d loaded": 16, 
            "damp made": 1, "diff made": 1,  "ea loaded": 32,
            "ea product made": 1, "ea transposed": 1, "eaT copied": 1, "edges activated": 1, "eu made": 1,
            "evacuated": 1, "expd made": 1, "hidden made": 1, "hidden summed": 1,
            "idx loaded": 16, "in transposed": 1,  "logits made": 1, "m carried": 1,
            "m scanned": 1,   "neg made": 1, 
               "out transposed": 1,
            "s scanned": 1, "scan stored": 16, "scanned": 1,  
              "u made": 1,  
             
        }

        def past(n, each=1):
            return (n + 1) * each

        def n_chunks(before, n, each=1):
            return past(n + before * NIT, each)

        def n_idx_loaded(layer, n):
            return n_chunks(layer, n, 16)

        def n_gathered(layer, n):
            return (n + layer * NIT) * 128

        def n_scan_stored(layer, n):
            return n_chunks(layer, n, 16)

        def n_scanned(layer, n):
            return n_chunks(layer, n)

        def n_out_transposed(layer, n):
            return n_chunks(layer, n)

        def n_evacuated(layer, n):
            return n_chunks(layer, n)

        def n_in_transposed(layer, n):
            return n_chunks((0, 1, None, 2)[layer], n)

        stages = {
            "PE": ("L0 weights transposed", "h0 transposed", "self made", "first hist added",
                "prefix made", "agg0 transposed", "neigh made", "h1 transposed", "w2 made", "w3 made",
                "w1 made", "h2 transposed", "w1a made", "edge bn mean summed", "edge bn var summed",
                "agg2 transposed", "z made", "node bn mean summed", "node bn var summed", "z transposed"),
            "ACT": ("L0 weights copied", "h0T copied", "agg0T copied", "h1T copied", "w2 copied", "w3 copied",
                "w1 copied", "merge factors made", "h2T copied", "w1a copied", "agg2T copied", "z copied",
                "z activated"),
            "DVE": ("consts cleared", "h0 made", "weights ready", "x self added",
                "first onehots made", "counts copied", "rowidx made", "rows indexed", "L0 merged", "h1 made",
                "merge diffs made", "L1 merged", "h2 made", "edge bn mean part made", "edge bn var part made",
                "edge bn ready", "L2 merged", "node bn mean part made", "node bn var part made",
                "node bn ready", "x3 made", "h3 made", "x4 made"),
        }

        def stage(name):
            engine = next(e for e in stages if name in stages[e])
            return S(f"{engine} stages"), stages[engine].index(name) + 1

        def stage_of(name):
            counted.append(name)
            return stage(name)[0]

        counted = []

        def dram(name, shape):
            return nc.dram_tensor(name, shape, F32, kind="Internal").ap()

        tab = [dram("table0", (NBP * 128, D)), dram("table1", (NBP * 128, 2 * D)),
               dram("table2", (NBP * 128, D)), dram("table3", (NBP * 128, D))]
        segs = [dram("scan0", (2 * HALF, D)), dram("scan1", (2 * HALF, 3 * D)),
                dram("scan2", (2 * HALF, D)), dram("scan3", (2 * HALF, D))]
        d_dram = dram("d_mlp", (128, HALF))

        keep = sb("keep", [128, HALF], BF16)
        arena = sb("arena", [128, HALF])
        x = sb("x", [128, NBP, D])
        hT = sb("hT", [128, NPAIR * 128])
        W = sb("W", [128, 12, 128])
        WSELF, WNEIGH, WD2, W1, W2, W3, W1A, W1B, W2A, W2B, WSELF_T, WNEIGH_T = range(12)
        cols = sb("cols", [128, 12])
        BD1, G1, B1, BD2, G2, B2, LB1, LG1, LBE1, LB2, LG2, LBE2 = range(12)
        X3 = 3 * 2 * J
        Wd1 = sb("Wd1", [X3 + 1, J * 2, D])
        bias0 = sb("bias0", [128, 2, D])
        ident = sb("ident", [128, 128])
        ones = sb("ones", [128, 128])
        upper = sb("upper", [128, 128])
        both = sb("both", [128, 128])
        small = sb("small", [128, 8, 32])
        rowidx = sb("rowidx", [128, NB], U32)
        degpos = sb("degpos", [128, NB])
        invdeg = sb("invdeg", [128, NB])
        span = sb("span", [128, NB])
        negspan = sb("negspan", [128, NB])
        tail = sb("tail", [128, 3 * D])
        stats = sb("stats", [128, NCH * 6])
        bnw = sb("bnw", [128, 2])
        bn = sb("bn", [128, 8])
        BROWS = 2 * 32 + 1
        brow = sb("brow", [BROWS, J * 2, D])
        rs = sb("rs", [128, 3, 32])
        idx = [sb(f"idx{k}", [128, 2 * J], I32) for k in range(2)]
        Gring = [sb(f"gathered{k}", [128, J * 2 * 2 * D]) for k in range(2)]

        def Gw(k, width):
            return Gring[k][:, 0:J * 2 * width].rearrange("p (j h d) -> p j h d", h=2, d=width)

        def pair(k, j):
            return Gring[k][:, j * 2 * D:(j + 1) * 2 * D]
        scanb = [sb(f"scan_ring{k}", [128, CH]) for k in range(2)]
        ostage = [sb(f"ostage{k}", [128, 2, J, D]) for k in range(2)]

        P = ctx.enter_context(nc.psum_tensor("psum", [128, 8, 512], F32))
        PF = P[:, :, :].rearrange("p b n -> p (b n)")

        def take(start):
            at = [start]

            def f(n):
                at[0] += n
                assert at[0] <= HALF
                return arena[:, at[0] - n:at[0]]
            return f

        a = take(0)
        wgt = [a(2 * J) for _ in range(2)]
        ea3 = a(2 * 2 * J * 3)
        dstb = a(2 * CH + 2)[:, 0:2 * CH + 1].bitcast(I32)
        msg = [a(CH) for _ in range(2)]
        x3t = a(2 * 128)
        mlp = [a(2 * CH) for _ in range(2)]
        y1 = [a(CH) for _ in range(2)]
        dout = a(2 * CH)
        brow3 = a(CH // 2).bitcast(BF16)
        bpart = a(CH // 2).bitcast(BF16)
        bones = a(64).bitcast(BF16)
        bres = a(CH)
        dst_pm, dst_p, dst_b, iota_i = (a(HC).bitcast(I32), a(HC), a(HC), a(128).bitcast(I32))
        iota_f = a(128)
        one_p = a(HSTEP * 128 // 2).bitcast(BF16)
        one_b = a(HSTEP * NB // 2).bitcast(BF16)
        a = take(0)
        dch = [a(CH) for _ in range(2)]
        neg = [a(CH) for _ in range(2)]
        soft = [a(2 * CH) for _ in range(2)]
        val = [a(CH) for _ in range(2)]
        part = [a(2 * CH) for _ in range(2)]
        mrun = [a(CH + 1) for _ in range(2)]
        srun = [a(CH) for _ in range(2)]
        orun = [a(CH) for _ in range(2)]
        ostage1 = [a(2 * J * 3 * D).rearrange("p (h j d) -> p h j d", h=2, j=J) for _ in range(2)]
        a = take(11800)
        h = a(NW).rearrange("p (b d) -> p b d", d=D)
        tmp = a(NW).rearrange("p (b d) -> p b d", d=D)
        agg = a(NB * 3 * D)
        tabs = a(NBP * 2 * D).rearrange("p (b d) -> p b d", d=2 * D)
        w1n = a(NV).rearrange("p (b d) -> p b d", d=D)
        ea64 = [sb(f"ea64_{k}", [128, J, 2, D]) for k in range(2)]
        eaT = Gring[0][:, CH:2 * CH]
        zact = [ea64[k][:, :, :, :].rearrange("p j h d -> p (j h d)") for k in range(2)]

        def halves_of(arr, w=1):
            return bass.AP(tensor=arr.tensor, offset=0, ap=[[B0 * w, 2], [1, HALF * w]])

        def chunk(arr, i, k, w=1):
            return halves_of(arr, w)[:, bass.ds(i * (2 * CH * w) + k * CH * w, CH * w)] \
                .rearrange("h (p x) -> p h x", x=J * w)

        def at(i, k, n=CH):
            return bass.ds(i * (2 * n) + k * n, n)

        def scan_rows(layer, i, k):
            return segs[layer].rearrange("(h e) d -> h e d", h=2)[:, bass.ds(i * (2 * CH) + k * CH, CH), :] \
                .rearrange("h (p j) d -> p h (j d)", j=J)

        def events(i, first=False):
            return 0 if first else i * 4 - 2

        halves = (slice(0, 64), slice(64, 128))
        block = ctx.enter_context(nc.Block())

        @block.sync
        def _(sp):
            for name, unit in ring_unit.items():
                for k in range(2):
                    sp.sem_inc(S(name, k), unit)
            for name in ("hist added", "keep made", "gelu made", "norms2 made"):
                sp.sem_inc(S(name), 1)
            sp.sem_inc(S("d stored"), 16)
            sp.wait_ge(*stage("consts cleared"))
            sp.dma_start(x[:, 0:NB - 1, :], T["x"][0:(NB - 1) * 128, :].rearrange("(b p) d -> p b d", p=128)) \
                .then_inc(S("x loaded"), 16)
            sp.dma_start(x[0:NLAST, NB - 1, :], T["x"][(NB - 1) * 128:N, :]).then_inc(S("x loaded"), 16)
            sp.dma_start(dst_pm[0:HR, :], T["dst"].rearrange("(p t) -> p t", p=HR)).then_inc(S("dst by row loaded"), 16)
            for half in range(2):
                sl = halves[half]
                for slot, m in ((WD2, T["L1_gnn_Wd2"]), (WSELF, T["L0_gnn_W_self"]), (WNEIGH, T["L0_gnn_W_neigh"]),
                                (W1, T["L1_gnn_W1"]), (W2, T["L1_gnn_W2"]), (W3, T["L1_gnn_W3"]),
                                (W1A, T["L2_gnn_W1"][0:D, :]), (W1B, T["L2_gnn_W1"][D:2 * D, :]),
                                (W2A, T["L2_gnn_W2"][0:D, :]), (W2B, T["L2_gnn_W2"][D:2 * D, :])):
                    sp.dma_start(W[sl, slot, sl], m).then_inc(S("weights loaded"), 16)
                for j in range(J):
                    r = half * 3 * J + 3 * j
                    sp.dma_start(Wd1[r:r + 3, 2 * j + half, :], T["L1_gnn_Wd1"]).then_inc(S("weights loaded"), 16)
            sp.dma_start(Wd1[X3:X3 + 1, :, :], T["L1_gnn_bd1"].partition_broadcast(J * 2).unsqueeze(0)) \
                .then_inc(S("weights loaded"), 16)
            for n in range(0, BROWS, 32):
                sp.dma_start(brow[n:n + 1, :, :], T["L1_gnn_bd2"].partition_broadcast(J * 2).unsqueeze(0)) \
                    .then_inc(S("weights loaded"), 16)
            for n, b in enumerate((T["L0_gnn_b_self"], T["L0_gnn_b_neigh"])):
                sp.dma_start(bias0[:, n, :], b.partition_broadcast(128)).then_inc(S("weights loaded"), 16)

            sp.wait_ge(*stage("h0 made"))
            sp.dma_start(tab[0].rearrange("(b p) d -> p b d", p=128), h).then_inc(S("table stored", 0), 16)

            def load_idx(i, k):
                sp.dma_start(idx[k][:, :].rearrange("p (h j) -> p h j", h=2), chunk(T["src"], i, k)) \
                    .then_inc(S("idx loaded", k), 16)

            def load_x3(m):
                for k in range(2):
                    sp.dma_start(ea3[:, k * X3:(k + 1) * X3].rearrange("p (h x) -> p h x", h=2),
                                 chunk(T["edge_attr_3"], m, k, 3)).then_inc(S("x3 loaded"), 16)

            def l0_loads(i, more=True):
                if more:
                    sp.wait_ge(S("x3 transposed"), i + 1)
                    load_x3(i + 1)
                for k in range(2):
                    sp.wait_ge(S("L0 msg made", k), past(i))
                    load_idx(i, k)
                    sp.dma_start(wgt[k].rearrange("p (h j) -> p h j", h=2), chunk(T["edge_weight"], i, k)) \
                        .then_inc(S("L0 weight loaded", k), 16)
                    if k == 0:
                        sp.wait_ge(S("keep made"), past(i))
                        for hf in range(2):
                            vec = T["dst"][bass.ds(i * (2 * CH) + hf * B0, 2 * CH)]
                            sp.dma_start(dstb[halves[hf], 1:], vec.partition_broadcast(64)) \
                                .then_inc(S("dst loaded"), 16)

            load_x3(0)
            with sp.Fori(0, NIT - 1) as i:
                l0_loads(i)
            l0_loads(NIT - 1, more=False)

            def tail_row(layer, w):
                for k in range(2):
                    sp.wait_ge(S("scan stored", k), n_scan_stored(layer, NIT))
                sp.dma_start(tail[:, 0:w], segs[layer][B0 - 1, :].partition_broadcast(128)) \
                    .then_inc(S("tail loaded", layer), 16)

            def node_table(layer, made, src):
                sp.wait_ge(*stage(made))
                sp.dma_start(tab[layer].rearrange("(b p) d -> p b d", p=128), src).then_inc(S("table stored", layer), 16)

            tail_row(0, D)
            node_table(1, "w3 copied", tabs)
            with sp.Fori(0, NIT) as i:
                for k in range(2):
                    sp.wait_ge(S("L1 split", k), past(i))
                    load_idx(i, k)
                    sp.wait_ge(S("u made", k), past(i))
                    sp.dma_start(dch[k], d_dram[:, at(i, k)]).then_inc(S("d loaded", k), 16)
            sp.wait_ge(*stage("L0 merged"))
            tail_row(1, 3 * D)
            node_table(2, "w1a copied", tabs[:, :, 0:D])
            with sp.Fori(0, NIT) as i:
                for k in range(2):
                    sp.wait_ge(S("hidden made", k), past(i))
                    load_idx(i, k)
                    sp.wait_ge(S("ea transposed", k), past(i))
                    for hf in range(2):
                        sp.dma_start(ea64[k][:, :, hf, :],
                                     T["edge_attr_64"][bass.ds(i * (2 * CH) + k * CH + hf * B0, CH), :]
                                     .rearrange("(p j) d -> p j d", j=J)).then_inc(S("ea loaded", k), 16)
            with sp.Fori(0, NIT) as i:
                for k in range(2):
                    sp.wait_ge(S("evacuated", k), n_evacuated(2, i + 1))
                    sp.dma_start(scan_rows(2, i, k), ostage[k][:, :, :, :].rearrange("p h j d -> p h (j d)")) \
                        .then_inc(S("scan stored", k), 16)
            sp.wait_ge(*stage("L1 merged"))
            tail_row(2, D)
            node_table(3, "h3 made", h)
            with sp.Fori(0, NIT) as i:
                for k in range(2):
                    sp.wait_ge(S("in transposed", k), n_in_transposed(3, i))
                    load_idx(i, k)
            sp.wait_ge(*stage("L2 merged"))
            tail_row(3, D)
            sp.wait_ge(*stage("x4 made"))
            sp.dma_start(out[0:(NB - 1) * 128, :].rearrange("(b p) d -> p b d", p=128), x[:, 0:NB - 1, :]) \
                .then_inc(S("out stored"), 16)
            sp.dma_start(out[(NB - 1) * 128:N, :], x[0:NLAST, NB - 1, :]).then_inc(S("out stored"), 16)
            sp.wait_ge(S("out stored"), 32)

        @block.gpsimd
        def _(pool):
            pool.memset(ident[:, :], 0.0).then_inc(S("consts begun"), 1)
            pool.memset(upper[:, :], 1.0).then_inc(S("consts begun"), 1)
            pool.iota(iota_i, [[1, 128]], base=0, channel_multiplier=0).then_inc(S("iota made"), 1)
            pool.wait_ge(S("consts begun"), 2)
            pool.affine_select(out=ident[:, :], in_=ident[:, :], compare_op=ALU.not_equal, fill=1.0, base=0,
                               pattern=[[-1, 128]], channel_multiplier=1).then_inc(S("ident made"), 1)
            pool.affine_select(out=upper[:, :], in_=upper[:, :], compare_op=ALU.is_ge, fill=0.0, base=0,
                               pattern=[[1, 128]], channel_multiplier=-1).then_inc(S("ident made"), 1)

            def gathers(layer, width, freed, freed_n=None):
                with pool.Fori(0, NIT) as i:
                    for k in range(2):
                        pool.wait_ge(S("table stored", layer), 16)
                        pool.wait_ge(S("idx loaded", k), n_idx_loaded(layer, i + 1))
                        pool.wait_ge(S(freed, k), (freed_n or past)(i))
                        pool.sem_inc(S("chunk cleared"), 1)
                        for j in range(J):
                            for hf in range(2):
                                q = hf * J + j
                                pool.indirect_dma_start(
                                    out=Gw(k, width)[:, j, hf, :], out_offset=None, in_=tab[layer],
                                    in_offset=bass.IndirectOffsetOnAxis(ap=idx[k][:, q:q + 1].bitcast(U32), axis=0)) \
                                    .then_inc(S("gathered", k), 16)

            def last_rows(layer, width):
                for k in range(2):
                    pool.wait_ge(S("scan stored", k), n_scan_stored(layer, NIT))
                for b in range(NB):
                    pool.indirect_dma_start(
                        out=agg[:, b * width:(b + 1) * width], out_offset=None, in_=segs[layer],
                        in_offset=bass.IndirectOffsetOnAxis(ap=rowidx[:, b:b + 1], axis=0)) \
                        .then_inc(S("last rows", layer), 16)

            gathers(0, D, "L0 msg made")
            pool.wait_ge(*stage("rowidx made"))
            last_rows(0, D)
            gathers(1, 2 * D, "L1 split")
            last_rows(1, 3 * D)
            gathers(2, D, "hidden made")
            last_rows(2, D)
            gathers(3, D, "in transposed", lambda n: n_in_transposed(3, n))
            last_rows(3, D)

        @block.tensor
        def _(pe):
            def to_channels(src, made, done, b=0):
                pe.wait_ge(*stage(made))
                for q in range(NPAIR):
                    last = nc.tensor.transpose(PF[:, b * 512 + q * 128:b * 512 + (q + 1) * 128],
                                               src[:, 2 * q:2 * q + 2, :].rearrange("p b d -> p (b d)"), ident[:, :])
                last.then_inc(stage_of(done), 1)

            def linear(rhs, b, done):
                for q in range(NPAIR):
                    last = nc.tensor.matmul(PF[:, b * 512 + q * 128:b * 512 + (q + 1) * 128],
                                            hT[:, q * 128:(q + 1) * 128], rhs, start=True, stop=True)
                last.then_inc(stage_of(done), 1)

            pe.wait_ge(S("ident made"), 2)
            pe.wait_ge(*stage("weights ready"))
            for n in range(2):
                last = nc.tensor.transpose(P[:, 0, n * 128:(n + 1) * 128], W[:, WSELF + n, :], ident[:, :])
            last.then_inc(stage_of("L0 weights transposed"), 1)
            pe.wait_ge(*stage("L0 weights copied"))
            to_channels(h, "h0 made", "h0 transposed")
            pe.wait_ge(*stage("h0T copied"))
            linear(W[:, WSELF_T, :], 4, "self made")
            pe.wait_ge(*stage("x self added"))
            pe.wait_ge(*stage("first onehots made"))
            for t in range(HPRE):
                last = nc.tensor.matmul(P[:, 7, 0:NB], one_p[0:HR, t * 128:(t + 1) * 128],
                                        one_b[0:HR, t * NB:(t + 1) * NB], start=(t == 0), stop=True,
                                        skip_group_check=True)
            last.then_inc(stage_of("first hist added"), 1)

            def x3_transposes(m, event=None):
                pe.wait_ge(S("x3 loaded"), (m + 1) * 32)
                if event is not None:
                    pe.wait_ge(S("gelu made"), past(event))
                for k in range(2):
                    last = nc.tensor.transpose(P[0:X3, 4, k * 128:(k + 1) * 128], ea3[:, k * X3:(k + 1) * X3],
                                               ident[:, :])
                last.then_inc(S("x3 transposed"), 1)

            def mlp1_products(m, first=False):
                pe.wait_ge(S("x3 copied"), m + 1)
                if not first:
                    pe.wait_ge(S("norms1 made"), m)
                for k in range(2):
                    last = nc.tensor.matmul(P[:, k, :], x3t[0:X3 + 1, k * 128:(k + 1) * 128],
                                            Wd1[:, :, :].rearrange("p r d -> p (r d)"), start=True, stop=True)
                last.then_inc(S("mlp1 made"), 1)

            def mlp2_products():
                for k in range(2):
                    nc.tensor.matmul(P[:, 2 + k, :], bones[0:BROWS, :], brow3[0:BROWS, :], start=True, stop=True)
                    for j in range(J):
                        last = nc.tensor.matmul(P[:, 2 + k, j * 128:(j + 1) * 128], y1[k][:, j::J], W[:, WD2, :],
                                                start=False, stop=True, skip_group_check=True)
                last.then_inc(S("mlp2 made"), 1)

            def norm_transpose(layer, k):
                for j in range(J):
                    last = nc.tensor.transpose(P[:, 4, j::J],
                                               mlp[layer][:, k * CH + j * 128:k * CH + (j + 1) * 128], ident[:, :])
                last.then_inc(S("norm transposed"), 1)

            def l0_in(i, k):
                pe.wait_ge(S("L0 msg made", k), past(i + 1))
                pe.wait_ge(S("scanned", 1 - k), n_scanned(0, i + k))
                for j in range(J):
                    last = nc.tensor.transpose(P[:, 5, j::J], msg[k][:, j * 128:(j + 1) * 128], ident[:, :])
                last.then_inc(S("in transposed", k), 1)

            def l0_out(i, k):
                pe.wait_ge(S("scanned", k), n_scanned(0, i + 1))
                pe.wait_ge(S("evacuated", 1 - k), n_evacuated(0, i + k))
                for j in range(J):
                    last = nc.tensor.transpose(P[:, 6, j * 128:(j + 1) * 128], scanb[k][:, j::J], ident[:, :])
                last.then_inc(S("out transposed", k), 1)

            def l0_hist(i):
                pe.wait_ge(S("onehots made"), i + 1)
                for t in range(HSTEP):
                    last = nc.tensor.matmul(P[:, 7, 0:NB], one_p[0:HR, t * 128:(t + 1) * 128],
                                            one_b[0:HR, t * NB:(t + 1) * NB], start=False, stop=True,
                                            skip_group_check=True)
                last.then_inc(S("hist added"), 1)

            def l0_body(i, first=False, more=True):
                g = events(i, first)
                if more:
                    x3_transposes(i + 1, g)
                    pe.wait_ge(S("x3 copied"), i + 2)
                else:
                    pe.wait_ge(S("gelu made"), past(g))
                pe.wait_ge(S("norms1 made"), i + 1)
                norm_transpose(0, 0)
                l0_in(i, 0)
                pe.wait_ge(S("gelu made"), past(g + 1))
                norm_transpose(0, 1)
                if not first:
                    l0_out(i - 1, 1)
                if more:
                    mlp1_products(i + 1)
                pe.wait_ge(S("gelu made"), past(g + 2))
                if not first:
                    pe.wait_ge(S("norms2 made"), past(i))
                    norm_transpose(1, 0)
                l0_in(i, 1)
                if not first:
                    pe.wait_ge(S("gelu made"), past(g + 3))
                    norm_transpose(1, 1)
                mlp2_products()
                l0_hist(i)
                l0_out(i, 0)

            x3_transposes(0)
            mlp1_products(0, first=True)
            l0_body(0, first=True)
            with pe.Fori(1, NIT - 1) as i:
                l0_body(i)
            l0_body(NIT - 1, more=False)
            l0_out(NIT - 1, 1)
            pe.wait_ge(S("norms2 made"), past(NIT))
            for k in range(2):
                pe.wait_ge(S("gelu made"), past(events(NIT) + k))
                norm_transpose(1, k)

            pe.wait_ge(*stage("counts copied"))
            pe.wait_ge(S("evacuated", 1), n_evacuated(0, NIT))
            nc.tensor.matmul(P[:, 6, 0:NB], upper[:, :], small[:, 0, 0:NB], start=True, stop=True)
            nc.tensor.matmul(P[:, 6, 32:32 + NB], ones[:, :], small[:, 0, 0:NB], start=True, stop=True) \
                .then_inc(stage_of("prefix made"), 1)

            to_channels(tmp, "L0 merged", "agg0 transposed")
            pe.wait_ge(*stage("agg0T copied"))
            pe.wait_ge(*stage("rows indexed"))
            linear(W[:, WNEIGH_T, :], 4, "neigh made")
            to_channels(h, "h1 made", "h1 transposed")
            pe.wait_ge(*stage("h1T copied"))
            linear(W[:, W2, :], 4, "w2 made")
            linear(W[:, W3, :], 0, "w3 made")
            pe.wait_ge(*stage("w2 copied"))
            linear(W[:, W1, :], 4, "w1 made")
            pe.wait_ge(*stage("w3 copied"))
            pe.wait_ge(*stage("w1 copied"))

            def l1_out(i, k):
                pe.wait_ge(S("scanned", k), n_scanned(1, i + 1))
                pe.wait_ge(S("evacuated", 1 - k), n_evacuated(1, i + k))
                for n, run in enumerate((mrun[k][:, 1:CH + 1], srun[k], orun[k])):
                    for j in range(J):
                        last = nc.tensor.transpose(P[:, 2 + n, j * 128:(j + 1) * 128], run[:, j::J], ident[:, :])
                last.then_inc(S("out transposed", k), 1)

            def l1_body(i, first=False):
                for k in range(2):
                    pe.wait_ge(S("L1 split", k), past(i + 1))
                    pe.wait_ge(S("logits made", 1 - k), past(i + k))
                    for j in range(J):
                        last = nc.tensor.transpose(P[:, 0, j::J], part[k][:, j * 128:(j + 1) * 128], ident[:, :])
                    last.then_inc(S("L1 w2 transposed", k), 1)
                    pe.wait_ge(S("u made", 1 - k), past(i + k))
                    for j in range(J):
                        last = nc.tensor.transpose(P[:, 1, j::J], part[k][:, CH + j * 128:CH + (j + 1) * 128],
                                                   ident[:, :])
                    last.then_inc(S("in transposed", k), 1)
                    if k == 1:
                        l1_out(i, 0)
                    elif not first:
                        l1_out(i - 1, 1)

            l1_body(0, first=True)
            with pe.Fori(1, NIT) as i:
                l1_body(i)
            l1_out(NIT - 1, 1)

            pe.wait_ge(S("evacuated", 1), n_evacuated(1, NIT))
            to_channels(h, "h2 made", "h2 transposed")
            pe.wait_ge(*stage("h2T copied"))
            linear(W[:, W1A, :], 4, "w1a made")
            pe.wait_ge(*stage("w1a copied"))

            with pe.Fori(0, NIT) as i:
                for k in range(2):
                    pe.wait_ge(S("ea loaded", k), past(i + 1, 32))
                    pe.wait_ge(S("eaT copied", k), past(i))
                    for j in range(J):
                        last = nc.tensor.transpose(P[:, k, j::J], ea64[k][:, j, :, :].rearrange("p h d -> p (h d)"), ident[:, :])
                    last.then_inc(S("ea transposed", k), 1)
                    pe.wait_ge(S("eaT copied", k), past(i + 1))
                    pe.wait_ge(S("hidden made", k), past(i))
                    nc.tensor.matmul(P[:, 2 + k, :], W[:, W1B, :], eaT, start=True, stop=True) \
                        .then_inc(S("ea product made", k), 1)
                    pe.wait_ge(S("gathered", k), n_gathered(2, i + 1))
                    for j in range(J):
                        last = nc.tensor.matmul(P[:, 2 + k, j::J], pair(k, j), ident[:, :],
                                                start=False, stop=True, skip_group_check=True)
                    last.then_inc(S("hidden summed", k), 1)

            def combine(tag):
                for n, name in enumerate(("mean", "var")):
                    pe.wait_ge(*stage(f"{tag} {name} part made"))
                    nc.tensor.matmul(P[:, 7, n:n + 1], both[:, :], bn[:, 2 + n:3 + n], start=True, stop=True) \
                        .then_inc(stage_of(f"{tag} {name} summed"), 1)

            combine("edge bn")
            with pe.Fori(0, NIT) as i:
                for k in range(2):
                    pe.wait_ge(S("scanned", k), n_scanned(2, i + 1))
                    pe.wait_ge(S("evacuated", k), n_evacuated(2, i))
                    for j in range(J):
                        last = nc.tensor.transpose(P[:, k, j * 128:(j + 1) * 128], scanb[k][:, j::J], ident[:, :])
                    last.then_inc(S("out transposed", k), 1)

            pe.wait_ge(S("evacuated", 0), n_evacuated(2, NIT))
            pe.wait_ge(S("evacuated", 1), n_evacuated(2, NIT))
            to_channels(tmp, "L2 merged", "agg2 transposed")
            pe.wait_ge(*stage("agg2T copied"))
            pe.wait_ge(*stage("edge bn ready"))
            for q in range(4):
                w = min(512, NPAIR * 128 - q * 512)
                nc.tensor.matmul(P[:, 4 + q, 0:w], W[:, W2A, :], hT[:, q * 512:q * 512 + w], start=True, stop=False)
                last = nc.tensor.matmul(P[:, 4 + q, 0:w], W[:, W2B, :], agg[:, q * 512:q * 512 + w],
                                        start=False, stop=True)
            last.then_inc(stage_of("z made"), 1)
            pe.wait_ge(*stage("z copied"))
            combine("node bn")
            pe.wait_ge(*stage("z activated"))
            for q in range(NPAIR):
                last = nc.tensor.transpose(PF[:, q * 128:(q + 1) * 128], agg[:, q * 128:(q + 1) * 128], ident[:, :])
            last.then_inc(stage_of("z transposed"), 1)
            pe.wait_ge(*stage("x3 made"))

            with pe.Fori(0, NIT) as i:
                for k in range(2):
                    pe.wait_ge(S("gathered", k), n_gathered(3, i + 1))
                    pe.wait_ge(S("scanned", k), n_scanned(3, i))
                    for j in range(J):
                        last = nc.tensor.transpose(P[:, 4 + k, j::J], pair(k, j), ident[:, :])
                    last.then_inc(S("in transposed", k), 1)
                    pe.wait_ge(S("scanned", k), n_scanned(3, i + 1))
                    pe.wait_ge(S("evacuated", k), n_evacuated(3, i))
                    for j in range(J):
                        last = nc.tensor.transpose(P[:, 6 + k, j * 128:(j + 1) * 128], scanb[k][:, j::J], ident[:, :])
                    last.then_inc(S("out transposed", k), 1)

        @block.scalar
        def _(act):
            act.wait_ge(*stage("consts cleared"))
            for n, name in enumerate(("L1_gnn_bd1", "L1_gnn_g1", "L1_gnn_b1", "L1_gnn_bd2", "L1_gnn_g2", "L1_gnn_b2",
                                      "L2_gnn_b1", "L2_gnn_g1", "L2_gnn_be1", "L2_gnn_b2", "L2_gnn_g2", "L2_gnn_be2")):
                for hf in range(2):
                    act.dma_start(cols[halves[hf], n:n + 1], T[name].rearrange("(p a) -> p a", a=1)) \
                        .then_inc(S("columns loaded"), 16)

            def copy(dst, src, need, done, scale=1.0):
                act.wait_ge(*stage(need))
                nc.scalar.activation(dst, src, ACT.Copy, scale=scale).then_inc(stage_of(done), 1)

            def evacuate(layer, i, k, bank, store=True):
                act.wait_ge(S("out transposed", k), n_out_transposed(layer, i + 1))
                act.wait_ge(S("scan stored", k), n_scan_stored(layer, i))
                nc.scalar.activation(ostage[k][:, :, :, :].rearrange("p h j d -> p j h d"),
                                     P[:, bank, :].rearrange("p (j h d) -> p j h d", h=2, d=D), ACT.Copy) \
                    .then_inc(S("evacuated", k), 1)
                if store:
                    act.wait_ge(S("evacuated", k), n_evacuated(layer, i + 1))
                    act.dma_start(scan_rows(layer, i, k), ostage[k][:, :, :, :].rearrange("p h j d -> p h (j d)")) \
                        .then_inc(S("scan stored", k), 16)

            copy(W[:, WSELF_T:WNEIGH_T + 1, :].rearrange("p a d -> p (a d)"), P[:, 0, 0:256],
                 "L0 weights transposed", "L0 weights copied")
            copy(hT[:, :], PF[:, 0:NPAIR * 128], "h0 transposed", "h0T copied")

            def x3_copy(m):
                act.wait_ge(S("x3 transposed"), m + 1)
                nc.scalar.activation(x3t[0:X3, :], P[0:X3, 4, 0:256], ACT.Copy).then_inc(S("x3 copied"), 1)

            def squares(layer, n):
                act.wait_ge(S(f"mlp{layer + 1} made"), n + 1)
                nc.scalar.activation(mlp[layer], PF[:, layer * 2 * CH:(layer + 1) * 2 * CH], ACT.Square) \
                    .then_inc(S(f"squares{layer + 1} made"), 1)

            def gelu1(k, event):
                act.wait_ge(S("norm transposed"), event)
                nc.scalar.activation(y1[k], P[:, 4, :], ACT.Gelu, bias=cols[:, B1:B1 + 1],
                                     scale=cols[:, G1:G1 + 1]).then_inc(S("gelu made"), 1)

            def gelu2(k, event):
                act.wait_ge(S("norm transposed"), event)
                nc.scalar.activation(dout[:, k * CH:(k + 1) * CH], P[:, 4, :], ACT.Gelu, bias=cols[:, B2:B2 + 1],
                                     scale=cols[:, G2:G2 + 1]).then_inc(S("gelu made"), 1)

            def store_d(m, event):
                act.wait_ge(S("gelu made"), past(event))
                act.dma_start(d_dram[:, bass.ds(m * (2 * CH), 2 * CH)], dout).then_inc(S("d stored"), 16)

            def l0_body(i, first=False, more=True):
                g = events(i, first)
                if more:
                    x3_copy(i + 1)
                gelu1(0, g + 1)
                gelu1(1, g + 2)
                if not first:
                    evacuate(0, i - 1, 1, 6)
                if more:
                    squares(0, i + 1)
                if not first:
                    act.wait_ge(S("d stored"), past(i - 1, 16))
                    gelu2(0, g + 3)
                    gelu2(1, g + 4)
                    store_d(i - 1, g + 4)
                squares(1, i)
                evacuate(0, i, 0, 6)

            x3_copy(0)
            squares(0, 0)
            l0_body(0, first=True)
            with act.Fori(1, NIT - 1) as i:
                l0_body(i)
            l0_body(NIT - 1, more=False)
            evacuate(0, NIT - 1, 1, 6)
            act.wait_ge(S("d stored"), past(NIT - 1, 16))
            gelu2(0, events(NIT) + 1)
            gelu2(1, events(NIT) + 2)
            store_d(NIT - 1, events(NIT) + 2)

            copy(hT[:, :], PF[:, 0:NPAIR * 128], "agg0 transposed", "agg0T copied")
            copy(hT[:, :], PF[:, 0:NPAIR * 128], "h1 transposed", "h1T copied")
            bank4 = PF[:, 2048:2048 + NW].rearrange("p (b d) -> p b d", d=D)
            bank0 = PF[:, 0:NW].rearrange("p (b d) -> p b d", d=D)
            copy(tabs[:, :, 0:D], bank4, "w2 made", "w2 copied", scale=-1.0)
            copy(tabs[:, :, D:2 * D], bank0, "w3 made", "w3 copied")
            copy(w1n, bank4[:, 0:NB, :], "w1 made", "w1 copied")
            act.wait_ge(S("d stored"), past(NIT, 16))
            act.wait_ge(S("keep made"), past(NIT))

            def l1_evacuate(i, k):
                act.wait_ge(S("out transposed", k), n_out_transposed(1, i + 1))
                act.wait_ge(S("scan stored", k), n_scan_stored(1, i))
                for n in range(3):
                    last = nc.scalar.activation(
                        ostage1[k][:, :, :, n * D:(n + 1) * D].rearrange("p h j d -> p j h d"),
                        P[:, 2 + n, :].rearrange("p (j h d) -> p j h d", h=2, d=D), ACT.Copy)
                last.then_inc(S("evacuated", k), 1)
                act.wait_ge(S("evacuated", k), n_evacuated(1, i + 1))
                act.dma_start(scan_rows(1, i, k), ostage1[k].rearrange("p h j d -> p h (j d)")) \
                    .then_inc(S("scan stored", k), 16)

            def l1_body(i, first=False):
                for k in range(2):
                    act.wait_ge(S("m scanned", k), past(i))
                    nc.scalar.activation(neg[k], keep[:, at(i, k)], ACT.Copy, scale=BIG, bias=-BIG) \
                        .then_inc(S("neg made", k), 1)
                    act.wait_ge(S("gathered", k), n_gathered(1, i + 1))
                    act.wait_ge(S("in transposed", k), n_in_transposed(1, i))
                    nc.scalar.activation(part[k].rearrange("p (n r d) -> p r n d", n=2, d=D),
                                         Gring[k][:, :].rearrange("p (r n d) -> p r n d", n=2, d=D), ACT.Copy) \
                        .then_inc(S("L1 split", k), 1)
                    if k == 1:
                        l1_evacuate(i, 0)
                    elif not first:
                        l1_evacuate(i - 1, 1)
                    act.wait_ge(S("diff made", k), past(i + 1))
                    nc.scalar.activation(soft[k], soft[k], ACT.Exp).then_inc(S("expd made", k), 1)

            l1_body(0, first=True)
            with act.Fori(1, NIT) as i:
                l1_body(i)
            l1_evacuate(NIT - 1, 1)

            act.wait_ge(*stage("merge diffs made"))
            nc.scalar.activation(tabs[:, 0:NB, :], tabs[:, 0:NB, :], ACT.Exp).then_inc(stage_of("merge factors made"), 1)
            copy(hT[:, :], PF[:, 0:NPAIR * 128], "h2 transposed", "h2T copied")
            copy(tabs[:, :, 0:D], bank4, "w1a made", "w1a copied")

            with act.Fori(0, NIT) as i:
                for k in range(2):
                    act.wait_ge(S("ea transposed", k), past(i + 1))
                    act.wait_ge(S("ea product made", 1 - k), past(i + k))
                    nc.scalar.activation(eaT, P[:, k, :], ACT.Copy).then_inc(S("eaT copied", k), 1)
                    act.wait_ge(S("hidden summed", k), past(i + 1))
                    nc.scalar.activation(arena[:, at(i, k)], P[:, 2 + k, :], ACT.Identity, bias=cols[:, LB1:LB1 + 1]) \
                        .then_inc(S("hidden made", k), 1)

            act.wait_ge(*stage("edge bn ready"))
            with act.Fori(0, NIT) as i:
                for k in range(2):
                    act.wait_ge(S("scanned", k), n_scanned(2, i))
                    nc.scalar.activation(zact[k], arena[:, at(i, k)], ACT.Silu, bias=bn[:, 6:7], scale=bn[:, 5:6]) \
                        .then_inc(S("edges activated", k), 1)
                for k in range(2):
                    evacuate(2, i, k, k, store=False)

            copy(agg[:, 0:NPAIR * 128], PF[:, 0:NPAIR * 128], "agg2 transposed", "agg2T copied")
            act.wait_ge(*stage("z made"))
            nc.scalar.activation(tabs[:, 0:NPAIR, :].rearrange("p b d -> p (b d)"), PF[:, 2048:2048 + NPAIR * 128],
                                 ACT.Identity, bias=cols[:, LB2:LB2 + 1]).then_inc(stage_of("z copied"), 1)
            act.wait_ge(*stage("node bn ready"))
            nc.scalar.activation(agg[:, 0:NPAIR * 128], tabs[:, 0:NPAIR, :].rearrange("p b d -> p (b d)"),
                                 ACT.Silu, bias=bn[:, 6:7], scale=bn[:, 5:6]).then_inc(stage_of("z activated"), 1)

            with act.Fori(0, NIT) as i:
                for k in range(2):
                    evacuate(3, i, k, 6 + k)

        @block.vector
        def _(dve):
            v = nc.vector
            steps = [0]

            def step(ins):
                steps[0] += 1
                ins.then_inc(S("dve step"), 1)
                dve.wait_ge(S("dve step"), steps[0])

            def bc(colmat, w=D):
                return colmat.unsqueeze(2).to_broadcast([128, NB, w])

            def rsqrt(n, step, tuned=False):
                arg, res, t = (rs[:, m, n] for m in range(3))
                magic, first = (0x5f1ffff9, (0.703952253, 2.38924456)) if tuned else (0x5f3759df, (0.5, 3.0))
                step(v.tensor_scalar(t.bitcast(I32), arg.bitcast(I32), 1, None, ALU.arith_shift_right))
                step(v.tensor_scalar(res.bitcast(I32), t.bitcast(I32), -1.0, float(magic), ALU.mult, ALU.add))
                for c, m in (first, *[(0.5, 3.0)] * (1 if tuned else 2)):
                    step(v.scalar_tensor_tensor(t, res, -c, arg, ALU.mult, ALU.mult))
                    step(v.tensor_tensor(t, t, res, ALU.mult))
                    step(v.scalar_tensor_tensor(res, t, c * m, res, ALU.add, ALU.mult))

            def layernorm_relu(dst, done):
                xs, xc, hs = x[:, 0:NB, :], tmp[:, 0:NB, :], dst[:, 0:NB, :]
                s1, s2 = small[:, 1, 0:NB], small[:, 2, 0:NB]
                step(v.reduce_sum(s1, xs, axis=AX))
                step(v.tensor_scalar(s1, s1, 1.0 / D, None, ALU.mult))
                step(v.tensor_tensor(xc, xs, bc(s1), ALU.subtract))
                step(v.tensor_tensor(hs, xc, xc, ALU.mult))
                step(v.reduce_sum(s2, hs, axis=AX))
                step(v.tensor_scalar(rs[:, 0, 0:NB], s2, 1.0 / D, EPS, ALU.mult, ALU.add))
                rsqrt(slice(0, NB), step)
                step(v.scalar_tensor_tensor(hs, xc, 0.0, bc(rs[:, 1, 0:NB]), ALU.max, ALU.mult))
                dve.sem_inc(stage_of(done), 1)

            for t in (x[:, :, :], W[:, :, :], Wd1[:, :, :], brow[:, :, :], h, both[:, :], scanb[1][:, :]):
                step(v.memset(t, 0.0))
            dve.sem_inc(stage_of("consts cleared"), 1)
            step(v.memset(ones[:, :], 1.0))
            for hf, (ne, nn) in zip(halves, ((B0, 64 * 0 + (NPAIR - 1) * 128 + NLAST), (HALF, (NPAIR - 1) * 128))):
                step(v.memset(bnw[hf, 0:1], ne / E))
                step(v.memset(bnw[hf, 1:2], nn / N))
            dve.wait_ge(S("x loaded"), 32)
            layernorm_relu(h, "h0 made")

            dve.wait_ge(S("ident made"), 2)
            for hf in halves:
                for hg in halves:
                    step(v.tensor_copy(both[hf, hg], ident[hf, hf]))
            dve.wait_ge(S("weights loaded"), 16 * 34)
            dve.wait_ge(S("columns loaded"), 16 * 24)
            for m, s in ((Wd1[:, :, :], small[0:X3 + 1, 3, 0:2 * J]),
                         (brow[:, :, :], small[0:BROWS, 5, 0:2 * J]),
                         (W[:, WD2, :].rearrange("p (a d) -> p a d", d=D), small[:, 4, 0:2])):
                step(v.reduce_sum(s, m, axis=AX))
                step(v.tensor_scalar(s, s, 1.0 / D, None, ALU.mult))
                step(v.tensor_tensor(m, m, s.unsqueeze(2).to_broadcast(list(m.shape)), ALU.subtract))
            row = brow[:, :, :].rearrange("p r d -> p (r d)")
            step(v.memset(brow3[0:BROWS, :], 0.0))
            for n in range(3):
                step(v.tensor_copy(bpart[0:BROWS, :], row))
                step(v.tensor_copy(brow3[32 * n:32 * n + 1, :], bpart[32 * n:32 * n + 1, :]))
                step(v.tensor_copy(bres[0:BROWS, :], bpart[0:BROWS, :]))
                step(v.tensor_tensor(row, row, bres[0:BROWS, :], ALU.subtract))
            step(v.memset(bones[0:BROWS, :], 1.0))
            step(v.memset(x3t[0:32, :], 1.0))
            dve.sem_inc(stage_of("weights ready"), 1)
            dve.wait_ge(*stage("self made"))
            step(v.tensor_tensor(x[:, 0:NB, :], x[:, 0:NB, :], PF[:, 2048:2048 + NV].rearrange("p (b d) -> p b d", d=D),
                                 ALU.add))
            for n in range(2):
                step(v.tensor_tensor(x[:, 0:NB, :], x[:, 0:NB, :],
                                     bias0[:, n, :].unsqueeze(1).to_broadcast([128, NB, D]), ALU.add))
            dve.sem_inc(stage_of("x self added"), 1)
            dve.wait_ge(S("iota made"), 1)
            dve.wait_ge(S("dst by row loaded"), 16)
            step(v.tensor_copy(iota_f, iota_i))
            step(v.tensor_scalar(dst_b[0:HR, :].bitcast(I32), dst_pm[0:HR, :], 7, None, ALU.arith_shift_right))
            step(v.tensor_scalar(dst_pm[0:HR, :], dst_pm[0:HR, :], 127, None, ALU.bitwise_and))
            step(v.tensor_copy(dst_p[0:HR, :], dst_pm[0:HR, :]))
            step(v.tensor_copy(dst_b[0:HR, :], dst_b[0:HR, :].bitcast(I32)))

            def onehots(first, n):
                for key, dst, w in ((dst_p, one_p, 128), (dst_b, one_b, NB)):
                    last = v.tensor_tensor(dst[0:HR, 0:n * w].rearrange("p (t c) -> p t c", c=w),
                                           key[0:HR, first].unsqueeze(2).to_broadcast([HR, n, w]),
                                           iota_f[0:HR, 0:w].unsqueeze(1).to_broadcast([HR, n, w]), ALU.is_equal)
                return last

            onehots(slice(0, HPRE), HPRE).then_inc(stage_of("first onehots made"), 1)
            step(v.memset(dstb[:, 0:1], -1))
            dve.wait_ge(*stage("first hist added"))

            def norms(layer, n):
                made = [0]
                name = f"norm{layer + 1} step"

                def norm_step(ins):
                    made[0] += 1
                    ins.then_inc(S(name), 1)
                    dve.wait_ge(S(name), n * 9 + made[0])

                r = slice(layer * 4 * J, (layer + 1) * 4 * J)
                dve.wait_ge(S(f"squares{layer + 1} made"), n + 1)
                v.reduce_sum(rs[:, 2, r], mlp[layer].rearrange("p (r d) -> p r d", d=D), axis=AX) \
                    .then_inc(S(f"squares{layer + 1} summed"), 1)
                dve.wait_ge(S(f"squares{layer + 1} summed"), n + 1)
                norm_step(v.tensor_scalar(rs[:, 0, r], rs[:, 2, r], 1.0 / D, EPS, ALU.mult, ALU.add))
                rsqrt(r, norm_step, tuned=True)
                assert made[0] == 9
                v.tensor_tensor(mlp[layer].rearrange("p (r d) -> p r d", d=D),
                                PF[:, layer * 2 * CH:(layer + 1) * 2 * CH].rearrange("p (r d) -> p r d", d=D),
                                rs[:, 1, r].unsqueeze(2).to_broadcast([128, 4 * J, D]), ALU.mult) \
                    .then_inc(S(f"norms{layer + 1} made"), 1)

            def l0_message(i, k):
                dve.wait_ge(S("gathered", k), n_gathered(0, i + 1))
                dve.wait_ge(S("L0 weight loaded", k), past(i + 1, 16))
                dve.wait_ge(S("in transposed", k), n_in_transposed(0, i))
                v.tensor_tensor(msg[k].rearrange("p (j h d) -> p j h d", h=2, d=D), Gw(k, D),
                                wgt[k].rearrange("p (h j) -> p j h", h=2).unsqueeze(3)
                                .to_broadcast([128, J, 2, D]), ALU.mult).then_inc(S("L0 msg made", k), 1)

            def l0_scan(i, k):
                dve.wait_ge(S("in transposed", k), n_in_transposed(0, i + 1))
                dve.wait_ge(S("scanned", 1 - k), n_scanned(0, i + k))
                dve.wait_ge(S("out transposed", k), n_out_transposed(0, i))
                v.tensor_tensor_scan(scanb[k][:, :], keep[:, at(i, k)], P[:, 5, :],
                                     scanb[1 - k][:, CH - 1:CH], ALU.mult, ALU.add).then_inc(S("scanned", k), 1)

            def l0_body(i, first=False, more=True):
                dve.wait_ge(S("dst loaded"), (i + 1) * 32)
                v.tensor_tensor(keep[:, bass.ds(i * (2 * CH), 2 * CH)], dstb[:, 1:2 * CH + 1], dstb[:, 0:2 * CH],
                                ALU.is_equal).then_inc(S("pair compared"), 1)
                dve.wait_ge(S("pair compared"), i + 1)
                v.tensor_copy(dstb[:, 0:1], dstb[:, 2 * CH:2 * CH + 1]).then_inc(S("keep made"), 1)
                l0_message(i, 0)
                if not first:
                    norms(1, i - 1)
                dve.wait_ge(S("keep made"), past(i + 1))
                l0_scan(i, 0)
                l0_message(i, 1)
                if more:
                    norms(0, i + 1)
                dve.wait_ge(S("hist added"), past(i))
                onehots(bass.ds(i * HSTEP + HPRE, HSTEP), HSTEP).then_inc(S("onehots made"), 1)
                l0_scan(i, 1)

            norms(0, 0)
            l0_body(0, first=True)
            with dve.Fori(1, NIT - 1) as i:
                l0_body(i)
            l0_body(NIT - 1, more=False)
            norms(1, NIT - 1)

            cnt, pre, tot, incl, end, ge = (small[:, n, 0:NB] for n in range(6))
            dve.wait_ge(S("hist added"), past(NIT))
            step(v.tensor_copy(cnt, P[:, 7, 0:NB]))
            dve.sem_inc(stage_of("counts copied"), 1)
            dve.wait_ge(*stage("prefix made"))
            step(v.tensor_copy(pre, P[:, 6, 0:NB]))
            step(v.tensor_copy(tot, P[:, 6, 32:32 + NB]))
            step(v.tensor_tensor_scan(incl, ones[:, 0:NB], tot, 0.0, ALU.mult, ALU.add))
            step(v.tensor_tensor(end, incl, tot, ALU.subtract))
            step(v.tensor_tensor(end, end, pre, ALU.add))
            step(v.tensor_scalar(ge, end, float(B0 + 1), None, ALU.is_ge))
            step(v.tensor_tensor(span[:, :], end, cnt, ALU.subtract))
            step(v.tensor_scalar(span[:, :], span[:, :], float(B0), None, ALU.is_lt))
            step(v.tensor_tensor(span[:, :], span[:, :], ge, ALU.mult))
            step(v.tensor_scalar(negspan[:, :], span[:, :], BIG, -BIG, ALU.mult, ALU.add))
            step(v.tensor_scalar(end, end, -1.0, 0.0, ALU.add, ALU.max))
            step(v.scalar_tensor_tensor(end, ge, float(OVER), end, ALU.mult, ALU.add))
            step(v.tensor_copy(rowidx[:, :], end))
            dve.sem_inc(stage_of("rowidx made"), 1)
            step(v.tensor_scalar(degpos[:, :], cnt, 0.0, None, ALU.is_gt))
            step(v.tensor_scalar(end, cnt, 1.0, None, ALU.max))
            step(v.reciprocal(end, end))
            step(v.tensor_tensor(invdeg[:, :], degpos[:, :], end, ALU.mult))
            dve.sem_inc(stage_of("rows indexed"), 1)

            aggs = agg[:, 0:NV].rearrange("p (b d) -> p b d", d=D)

            def merge_sum(layer, factor, dst):
                dve.wait_ge(S("last rows", layer), 16 * NB)
                dve.wait_ge(S("tail loaded", layer), 16)
                step(v.tensor_tensor(dst, tail[:, 0:D].unsqueeze(1).to_broadcast([128, NB, D]), bc(span[:, :]), ALU.mult))
                step(v.tensor_tensor(dst, dst, aggs, ALU.add))
                step(v.tensor_tensor(dst, dst, bc(factor), ALU.mult))

            merge_sum(0, invdeg[:, :], tmp[:, 0:NB, :])
            step(v.memset(tmp[:, NB:NBP, :], 0.0))
            dve.sem_inc(stage_of("L0 merged"), 1)
            dve.wait_ge(*stage("neigh made"))
            step(v.tensor_tensor(x[:, 0:NB, :], x[:, 0:NB, :], PF[:, 2048:2048 + NV].rearrange("p (b d) -> p b d", d=D),
                                 ALU.add))
            layernorm_relu(h, "h1 made")

            step(v.memset(mrun[1][:, CH:CH + 1], -BIG))
            step(v.memset(srun[1][:, CH - 1:CH], 0.0))
            step(v.memset(orun[1][:, CH - 1:CH], 0.0))
            with dve.Fori(0, NIT) as i:
                for k in range(2):
                    dve.wait_ge(S("d loaded", k), past(i + 1, 16))
                    dve.wait_ge(S("L1 w2 transposed", k), past(i + 1))
                    v.tensor_tensor(soft[k][:, CH:2 * CH], P[:, 0, :], dch[k], ALU.add).then_inc(S("logits made", k), 1)
                    dve.wait_ge(S("out transposed", k), n_out_transposed(1, i))
                    dve.wait_ge(S("m scanned", 1 - k), past(i + k))
                    v.tensor_copy(mrun[k][:, 0:1], mrun[1 - k][:, CH:CH + 1]).then_inc(S("m carried", k), 1)
                    dve.wait_ge(S("in transposed", k), n_in_transposed(1, i + 1))
                    v.tensor_tensor(val[k], P[:, 1, :], dch[k], ALU.add).then_inc(S("u made", k), 1)
                    dve.wait_ge(S("neg made", k), past(i + 1))
                    dve.wait_ge(S("logits made", k), past(i + 1))
                    dve.wait_ge(S("m carried", k), past(i + 1))
                    v.tensor_tensor_scan(mrun[k][:, 1:CH + 1], neg[k], soft[k][:, CH:2 * CH], mrun[k][:, 0:1],
                                         ALU.add, ALU.max).then_inc(S("m scanned", k), 1)
                    dve.wait_ge(S("m scanned", k), past(i + 1))
                    v.tensor_tensor(soft[k][:, 0:CH], mrun[k][:, 0:CH], mrun[k][:, 1:CH + 1], ALU.subtract)
                    v.tensor_tensor(soft[k][:, CH:2 * CH], soft[k][:, CH:2 * CH], mrun[k][:, 1:CH + 1], ALU.subtract) \
                        .then_inc(S("diff made", k), 1)
                    damp, num = soft[k][:, 0:CH], soft[k][:, CH:2 * CH]
                    dve.wait_ge(S("expd made", k), past(i + 1))
                    dve.wait_ge(S("u made", k), past(i + 1))
                    v.scalar_tensor_tensor(damp, damp, 1.0, keep[:, at(i, k)], ALU.min, ALU.mult) \
                        .then_inc(S("damp made", k), 1)
                    v.tensor_tensor(val[k], num, val[k], ALU.mult).then_inc(S("eu made", k), 1)
                    dve.wait_ge(S("damp made", k), past(i + 1))
                    dve.wait_ge(S("scanned", 1 - k), n_scanned(1, i + k))
                    v.tensor_tensor_scan(srun[k], damp, num, srun[1 - k][:, CH - 1:CH],
                                         ALU.mult, ALU.add).then_inc(S("s scanned", k), 1)
                    dve.wait_ge(S("eu made", k), past(i + 1))
                    dve.wait_ge(S("s scanned", k), past(i + 1))
                    v.tensor_tensor_scan(orun[k], damp, val[k], orun[1 - k][:, CH - 1:CH],
                                         ALU.mult, ALU.add).then_inc(S("scanned", k), 1)

            g = agg.rearrange("p (b d) -> p b d", d=3 * D)
            mB, sB, oB = g[:, :, 0:D], g[:, :, D:2 * D], g[:, :, 2 * D:3 * D]
            lA, lB, mx = tabs[:, 0:NB, 0:D], tabs[:, 0:NB, D:2 * D], tmp[:, 0:NB, :]

            def tail_bc(n):
                return tail[:, n * D:(n + 1) * D].unsqueeze(1).to_broadcast([128, NB, D])

            dve.wait_ge(S("last rows", 1), 16 * NB)
            dve.wait_ge(S("tail loaded", 1), 16)
            dve.wait_ge(*stage("w1 copied"))
            step(v.tensor_tensor(lA, tail_bc(0), bc(negspan[:, :]), ALU.add))
            step(v.tensor_tensor(lA, lA, w1n, ALU.add))
            step(v.tensor_tensor(lB, mB, w1n, ALU.add))
            step(v.tensor_tensor(mx, lA, lB, ALU.max))
            step(v.tensor_tensor(lA, lA, mx, ALU.subtract))
            step(v.tensor_tensor(lB, lB, mx, ALU.subtract))
            dve.sem_inc(stage_of("merge diffs made"), 1)
            dve.wait_ge(*stage("merge factors made"))
            for n, part in ((1, sB), (2, oB)):
                step(v.tensor_tensor(part, part, lB, ALU.mult))
                step(v.tensor_tensor(mx, tail_bc(n), lA, ALU.mult))
                step(v.tensor_tensor(part, part, mx, ALU.add))
            dve.sem_inc(stage_of("L1 merged"), 1)
            step(v.reciprocal(sB, sB))
            step(v.tensor_tensor(oB, oB, sB, ALU.mult))
            step(v.tensor_tensor(oB, oB, bc(degpos[:, :]), ALU.mult))
            step(v.tensor_tensor(x[:, 0:NB, :], x[:, 0:NB, :], oB, ALU.add))
            layernorm_relu(h, "h2 made")

            with dve.Fori(0, NIT) as i:
                for k in range(2):
                    dve.wait_ge(S("hidden made", k), past(i + 1))
                    v.bn_stats(stats[:, bass.ds(i * 12 + k * 6, 6)], arena[:, at(i, k)]).then_inc(S("stats made"), 1)
            dve.wait_ge(S("stats made"), NCH)
            step(v.bn_stats(stats[0:64, (NCH - 1) * 6:NCH * 6], arena[0:64, (NCH - 1) * CH:(NCH - 1) * CH + LASTA]))
            step(v.bn_aggr(bn[:, 0:2], stats[:, :]))

            def batchnorm(tag, wcol, gcol, bcol):
                share = bnw[:, wcol:wcol + 1]
                step(v.tensor_tensor(bn[:, 2:3], bn[:, 0:1], share, ALU.mult))
                dve.sem_inc(stage_of(f"{tag} mean part made"), 1)
                dve.wait_ge(*stage(f"{tag} mean summed"))
                step(v.tensor_copy(bn[:, 4:5], P[:, 7, 0:1]))
                step(v.tensor_tensor(bn[:, 7:8], bn[:, 0:1], bn[:, 4:5], ALU.subtract))
                step(v.tensor_tensor(bn[:, 7:8], bn[:, 7:8], bn[:, 7:8], ALU.mult))
                step(v.tensor_tensor(bn[:, 7:8], bn[:, 7:8], bn[:, 1:2], ALU.add))
                step(v.tensor_tensor(bn[:, 3:4], bn[:, 7:8], share, ALU.mult))
                dve.sem_inc(stage_of(f"{tag} var part made"), 1)
                dve.wait_ge(*stage(f"{tag} var summed"))
                step(v.tensor_scalar(rs[:, 0, 0:1], P[:, 7, 1:2], EPS, None, ALU.add))
                rsqrt(slice(0, 1), step)
                step(v.tensor_tensor(bn[:, 5:6], rs[:, 1, 0:1], cols[:, gcol:gcol + 1], ALU.mult))
                step(v.tensor_tensor(bn[:, 7:8], bn[:, 5:6], bn[:, 4:5], ALU.mult))
                step(v.tensor_tensor(bn[:, 6:7], cols[:, bcol:bcol + 1], bn[:, 7:8], ALU.subtract))
                dve.sem_inc(stage_of(f"{tag} ready"), 1)

            batchnorm("edge bn", 0, LG1, LBE1)

            step(v.memset(scanb[1][:, CH - 1:CH], 0.0))
            with dve.Fori(0, NIT) as i:
                for k in range(2):
                    dve.wait_ge(S("edges activated", k), past(i + 1))
                    dve.wait_ge(S("scanned", 1 - k), n_scanned(2, i + k))
                    dve.wait_ge(S("out transposed", k), n_out_transposed(2, i))
                    v.tensor_tensor_scan(scanb[k][:, :], keep[:, at(i, k)], zact[k],
                                         scanb[1 - k][:, CH - 1:CH], ALU.mult, ALU.add).then_inc(S("scanned", k), 1)

            merge_sum(2, invdeg[:, :], tmp[:, 0:NB, :])
            step(v.memset(tmp[:, NB:NBP, :], 0.0))
            dve.sem_inc(stage_of("L2 merged"), 1)
            dve.wait_ge(*stage("z copied"))
            z = tabs[:, 0:NPAIR, :].rearrange("p b d -> p (b d)")
            for n in range(3):
                step(v.bn_stats(stats[:, n * 6:(n + 1) * 6], z[:, n * 512:(n + 1) * 512]))
            step(v.bn_stats(stats[0:64, 18:24], z[0:64, 1536:1536 + NLAST]))
            step(v.bn_aggr(bn[0:64, 0:2], stats[0:64, 0:24]))
            step(v.bn_aggr(bn[64:128, 0:2], stats[64:128, 0:18]))
            batchnorm("node bn", 1, LG2, LBE2)
            dve.wait_ge(*stage("z transposed"))
            step(v.tensor_tensor(x[:, 0:NB, :], x[:, 0:NB, :], PF[:, 0:NV].rearrange("p (b d) -> p b d", d=D), ALU.add))
            dve.sem_inc(stage_of("x3 made"), 1)
            step(v.memset(h[:, NB:NBP, :], 0.0))
            layernorm_relu(h, "h3 made")

            step(v.memset(scanb[1][:, CH - 1:CH], 0.0))
            with dve.Fori(0, NIT) as i:
                for k in range(2):
                    dve.wait_ge(S("in transposed", k), n_in_transposed(3, i + 1))
                    dve.wait_ge(S("scanned", 1 - k), n_scanned(3, i + k))
                    dve.wait_ge(S("out transposed", k), n_out_transposed(3, i))
                    v.tensor_tensor_scan(scanb[k][:, :], keep[:, at(i, k)], P[:, 4 + k, :],
                                         scanb[1 - k][:, CH - 1:CH], ALU.mult, ALU.add).then_inc(S("scanned", k), 1)
            merge_sum(3, degpos[:, :], tmp[:, 0:NB, :])
            step(v.tensor_tensor(x[:, 0:NB, :], x[:, 0:NB, :], tmp[:, 0:NB, :], ALU.add))
            dve.sem_inc(stage_of("x4 made"), 1)

        for names in stages.values():
            assert [n for n in counted if n in names] == list(names)


def kernel(**inputs):
    import concourse.bacc as bacc
    from concourse.bass_utils import run_bass_kernel_spmd as run

    nc = bacc.Bacc("TRN2", target_bir_lowering=False, num_devices=1)
    arrays, args = {}, {}
    for name, value in inputs.items():
        value = np.ascontiguousarray(value)
        arrays[f"in_{name}"] = value
        args[name] = nc.dram_tensor(f"in_{name}", value.shape, mybir.dt.from_np(value.dtype),
                                    kind="ExternalInput").ap()
    out = nc.dram_tensor("out_x", (N, D), F32, kind="ExternalOutput").ap()
    build(nc, args, out)
    return run(nc, [arrays], core_ids=[0]).results[0]["out_x"]
```

```python
import numpy as np
import concourse.bass as bass
from concourse import mybir
from contextlib import ExitStack

F32 = mybir.dt.float32
BF16 = mybir.dt.bfloat16
I32 = mybir.dt.int32
U32 = mybir.dt.uint32
ALU = mybir.AluOpType
ACT = mybir.ActivationFunctionType
AX = mybir.AxisListType.X

N, D, E = 3125, 64, 53125
CH = 512
J = CH // 128
HALF = -(-E // (2 * CH)) * CH
NCH = HALF // CH
NIT = NCH // 2
B0 = E - HALF
OVER = HALF - B0
LASTA = CH - OVER
NB = -(-N // 128)
NBP = NB + 1
NPAIR = NBP // 2
NLAST = N - (NB - 1) * 128
PARTS = {"a": slice(0, 16), "b": slice(16, NB)}
PAIRS = {"a": range(0, 8), "b": range(8, NPAIR)}
NPICK = 17
NW = NBP * D
NV = NB * D
HR, HC = 125, E // 125
HSTEP = 2 * 8
HPRE = HC - NIT * HSTEP
BIG = 1e30
EPS = 1e-5


def build(nc, T, out):
    ctx = ExitStack()
    with ctx:
        def sb(name, shape, dt=F32):
            return ctx.enter_context(nc.sbuf_tensor(name, shape, dt))

        sems = {}

        def S(name, slot=None):
            key = name if slot is None else f"{name} [{slot}]"
            if key not in sems:
                sems[key] = ctx.enter_context(nc.semaphore(key.replace(" ", "_").strip("]").replace("[", "")))
            return sems[key]

        ring_unit = {
            "L0 msg made": 1, "L0 weight loaded": 16, "L1 w2 transposed": 1, "L1 split": 1, "d loaded": 16,
            "damp made": 1, "diff made": 1, "ea loaded": 32,
            "ea product made": 1, "ea transposed": 1, "eaT copied": 1, "eu made": 1,
            "src spread": 16, "pick onehots made": 1, "rows multiplied": 1, "rows picked": 1,
            "evacuated": 1, "expd made": 1, "hidden made": 1, "hidden summed": 1,
            "idx loaded": 16, "L2 scan stored": 16, "in transposed": 1, "logits made": 1, "m carried": 1,
            "m evacuated": 1, "m scanned": 1, "m transposed": 1, "neg made": 1,
            "out transposed": 1,
            "s scanned": 1, "scan stored": 16, "scanned": 1,  
              "u made": 1,  
             
        }

        def past(n, each=1):
            return (n + 1) * each

        def n_chunks(before, n, each=1):
            return past(n + before * NIT, each)

        def n_idx_loaded(layer, n):
            return n_chunks(layer, n, 16)

        def n_gathered(layer, n, picking=False):
            if layer < 2 or picking:
                return layer * NIT * 128 + n * (112 if picking else 128)
            if layer == 2:
                return layer * NIT * 128 + n * 128 - NPICK * 16
            return layer * NIT * 128 - NPICK * 16 + n * 112

        def n_picked(layer, n, each=1):
            return past(n + (NPICK if layer == 3 else 0), each)

        def n_last_rows(layer, part):
            return 16 * (layer + 1) * (PARTS[part].stop - PARTS[part].start)

        def n_scan_stored(layer, n):
            return n_chunks((0, 1, None, 2)[layer], n, 16)

        def n_scanned(layer, n):
            return n_chunks(layer, n)

        def n_out_transposed(layer, n):
            return n_chunks(layer, n)

        def n_evacuated(layer, n):
            return n_chunks(layer, n)

        def n_in_transposed(layer, n):
            return n_chunks((0, 1, None, 2)[layer], n)

        stages = {
            "PE": ("L0 weights transposed", "h0 transposed", "first hist added", "prefix made", "span parts summed", "self made",
                "agg0 transposed a", "neigh made a", "agg0 transposed b", "neigh made b", "h1 transposed a",
                "w2 made a", "w3 made a", "h1 transposed b", "w2 made b", "w3 made b", "w1 made a", "w1 made b",
                "h2 transposed a", "w1a made a", "h2 transposed b", "w1a made b", "edge bn mean summed",
                "edge bn var summed", "agg2 transposed a", "z made a", "agg2 transposed b", "z made b", "node bn mean summed",
                "node bn var summed", "z transposed a", "z transposed b"),
            "ACT": ("L0 weights copied", "h0T copied", "agg0T copied a", "agg0T copied b", "h1T copied a",
                "w2 copied a", "w3 copied a", "h1T copied b", "w2 copied b", "w3 copied b", "w1 copied a",
                "w1 copied b", "merge factors made", "h2T copied a", "w1a copied a",
                "h2T copied b", "w1a copied b", "agg2T copied a", "agg2T copied b", "z copied",
                "z activated a", "z activated b"),
            "DVE": ("x cleared", "consts cleared", "h0 made", "weights ready", "first onehots made",
                "counts copied", "rowidx made", "span parts made", "rows indexed", "x self added", "L0 merged a", "L0 merged b",
                "h1 made a", "h1 made b", "merge diffs made", "L1 tail merged", "h2 made a",
                "h2 made b", "w1a split", "edge bn mean part made", "edge bn var part made", "edge bn ready",
                "L2 merged a", "L2 merged b", "node bn mean part made", "node bn var part made",
                "node bn ready", "h3 made a", "h3 made b", "h3 split", "x4 made a", "x4 made b"),
        }

        def stage(name):
            engine = next(e for e in stages if name in stages[e])
            return S(f"{engine} stages"), stages[engine].index(name) + 1

        def stage_of(name):
            counted.append(name)
            return stage(name)[0]

        counted = []

        def dram(name, shape):
            return nc.dram_tensor(name, shape, F32, kind="Internal").ap()

        tab = [dram("table0", (NB * 128, D)), dram("table1", (NB * 128, 2 * D)),
               dram("table2", (NB * 128, D)), dram("table3", (NB * 128, D))]
        w1tab = dram("w1", (NB * 128, D))
        segs = [dram("scan0", (2 * HALF, D)), dram("scan1", (2 * HALF, 3 * D)),
                dram("scan2", (2 * HALF, D)), dram("scan3", (2 * HALF, D))]
        d_dram = dram("d_mlp", (128, HALF))

        keep = sb("keep", [128, HALF], BF16)
        arena = sb("arena", [128, HALF])
        x = sb("x", [128, NBP, D])
        hT = sb("hT", [128, NPAIR * 128])
        W = sb("W", [128, 12, 128])
        WSELF, WNEIGH, WD2, W1, W2, W3, W1A, W1B, W2A, W2B, WSELF_T, WNEIGH_T = range(12)
        cols = sb("cols", [128, 12])
        BD1, G1, B1, BD2, G2, B2, LB1, LG1, LBE1, LB2, LG2, LBE2 = range(12)
        X3 = 3 * 2 * J
        Wd1 = sb("Wd1", [X3 + 1, J * 2, D])
        bias0 = sb("bias0", [128, 2, D])
        ident = sb("ident", [128, 128])
        ones = sb("ones", [128, 128])
        upper = sb("upper", [128, 128])
        both = sb("both", [128, 128])
        small = sb("small", [128, 8, 32])
        rowidx = sb("rowidx", [128, NB], U32)
        node_i = sb("node_i", [128, NB], I32)
        degpos = sb("degpos", [128, NB])
        invdeg = sb("invdeg", [128, NB])
        span = sb("span", [128, NB])
        solo = sb("solo", [128, NB])
        spanidx = sb("spanidx", [128, 2], U32)
        tail = sb("tail", [128, 3 * D])
        stats = sb("stats", [128, NCH * 6])
        bnw = sb("bnw", [128, 2])
        bn = sb("bn", [128, 8])
        BROWS = 2 * 32 + 1
        brow = sb("brow", [BROWS, J * 2, D])
        rs = sb("rs", [128, 3, 32])
        idx = [sb(f"idx{k}", [128, 2 * J], I32) for k in range(2)]
        Gring = [sb(f"gathered{k}", [128, J * 2 * 2 * D]) for k in range(2)]

        def Gw(k, width):
            return Gring[k][:, 0:J * 2 * width].rearrange("p (j h d) -> p j h d", h=2, d=width)

        def pair(k, j):
            return Gring[k][:, j * 2 * D:(j + 1) * 2 * D]
        scanb = [sb(f"scan_ring{k}", [128, CH]) for k in range(2)]
        ostage = [sb(f"ostage{k}", [128, 2, J, D]) for k in range(2)]

        P = ctx.enter_context(nc.psum_tensor("psum", [128, 8, 512], F32))
        PF = P[:, :, :].rearrange("p b n -> p (b n)")

        def take(start):
            at = [start]

            def f(n):
                at[0] += n
                assert at[0] <= HALF
                return arena[:, at[0] - n:at[0]]
            return f

        a = take(0)
        wgt = [a(2 * J) for _ in range(2)]
        ea3 = a(2 * 2 * J * 3)
        dstb = a(2 * CH + 2)[:, 0:2 * CH + 1].bitcast(I32)
        msg = [a(CH) for _ in range(2)]
        x3t = a(2 * 128)
        mlp = [a(2 * CH) for _ in range(2)]
        square = [a(2 * CH), mlp[1]]
        y1 = [a(CH) for _ in range(2)]
        dout = a(2 * CH)
        brow3 = a(CH // 2).bitcast(BF16)
        bpart = a(CH // 2).bitcast(BF16)
        bones = a(64).bitcast(BF16)
        bres = a(CH)
        dst_pm, dst_p, dst_b, iota_i = (a(HC).bitcast(I32), a(HC), a(HC), a(128).bitcast(I32))
        iota_f = a(128)
        one_p = a(HSTEP * 128 // 2).bitcast(BF16)
        one_b = a(HSTEP * NB // 2).bitcast(BF16)
        a = take(0)
        dch = [a(CH) for _ in range(2)]
        neg = [a(CH) for _ in range(2)]
        soft = [a(2 * CH) for _ in range(2)]
        val = [a(CH) for _ in range(2)]
        wsplit = [a(2 * CH) for _ in range(2)]
        mrun = [a(CH + 1) for _ in range(2)]
        srun = [a(CH) for _ in range(2)]
        orun = [a(CH) for _ in range(2)]
        ostage1 = [a(2 * J * 3 * D).rearrange("p (h j d) -> p h j d", h=2, j=J) for _ in range(2)]
        a = take(11800)
        h = a(NW).rearrange("p (b d) -> p b d", d=D)
        tmp = a(NW).rearrange("p (b d) -> p b d", d=D)
        agg = a(NB * 3 * D)
        tabs = a(NBP * 2 * D).rearrange("p (b d) -> p b d", d=2 * D)
        w1n = a(NV).rearrange("p (b d) -> p b d", d=D)
        vec = tabs.rearrange("p b d -> p (b d)")
        span_row, span_w1, factors, tail_so = (vec[:, 0:3 * D], vec[:, 3 * D:4 * D], vec[:, 4 * D:6 * D],
                                               vec[:, 6 * D:8 * D])
        span_max = vec[:, 8 * D:9 * D]
        srcb, pick, split = {}, {}, {}
        for layer, start, split_start in ((2, NPICK * 2 * CH, 23256), (3, 0, 4224)):
            a = take(start)
            srcb[layer] = [a(CH).bitcast(I32) for _ in range(2)]
            pick[layer] = [a(NB * 128 // 2).bitcast(BF16).rearrange("p (b e) -> p b e", e=128) for _ in range(2)]
            a = take(split_start)
            split[layer] = a(NB * 3 * D // 2).bitcast(BF16).rearrange("p (b n d) -> p b n d", n=3, d=D)
        ea64 = [sb(f"ea64_{k}", [128, J, 2, D]) for k in range(2)]
        eaT = Gring[0][:, CH:2 * CH]
        ostage2 = [t[:, :, :, :].rearrange("p a b d -> p (a b d)").rearrange("p (h j d) -> p h j d", h=2, d=D)
                   for t in (*ostage, *ea64)]

        def halves_of(arr, w=1):
            return bass.AP(tensor=arr.tensor, offset=0, ap=[[B0 * w, 2], [1, HALF * w]])

        def chunk(arr, i, k, w=1):
            return halves_of(arr, w)[:, bass.ds(i * (2 * CH * w) + k * CH * w, CH * w)] \
                .rearrange("h (p x) -> p h x", x=J * w)

        def at(i, k, n=CH):
            return bass.ds(i * (2 * n) + k * n, n)

        def scan_rows(layer, i, k):
            return segs[layer].rearrange("(h e) d -> h e d", h=2)[:, bass.ds(i * (2 * CH) + k * CH, CH), :] \
                .rearrange("h (p j) d -> p h (j d)", j=J)

        def events(i, first=False):
            return 0 if first else i * 4 - 2

        def scans_stored(engine, layer):
            for k in range(4 if layer == 2 else 2):
                if layer == 2:
                    engine.wait_ge(S("L2 scan stored", k), past(NIT // 2, 16))
                else:
                    engine.wait_ge(S("scan stored", k), n_scan_stored(layer, NIT))

        halves = (slice(0, 64), slice(64, 128))
        block = ctx.enter_context(nc.Block())

        @block.sync
        def _(sp):
            def load_idx(i, k):
                sp.dma_start(idx[k][:, :].rearrange("p (h j) -> p h j", h=2), chunk(T["src"], i, k)) \
                    .then_inc(S("idx loaded", k), 16)

            def first_idx():
                for k in range(2):
                    load_idx(0, k)

            def next_idx(layer, i, k, picking=False):
                sp.wait_ge(S("gathered", k), n_gathered(layer, i + 1, picking))
                load_idx(i + 1, k)

            for name, unit in ring_unit.items():
                for k in range(4 if name == "L2 scan stored" else 2):
                    sp.sem_inc(S(name, k), unit)
            for name in ("hist added", "keep made", "gelu made", "norms2 made"):
                sp.sem_inc(S(name), 1)
            sp.sem_inc(S("d stored"), 16)
            sp.wait_ge(*stage("x cleared"))
            sp.dma_start(x[:, 0:NB - 1, :], T["x"][0:(NB - 1) * 128, :].rearrange("(b p) d -> p b d", p=128)) \
                .then_inc(S("x loaded"), 16)
            sp.dma_start(x[0:NLAST, NB - 1, :], T["x"][(NB - 1) * 128:N, :]).then_inc(S("x loaded"), 16)
            first_idx()
            sp.dma_start(dst_pm[0:HR, :], T["dst"].rearrange("(p t) -> p t", p=HR)).then_inc(S("dst by row loaded"), 16)
            sp.wait_ge(*stage("consts cleared"))

            def load_blocks(done, matrices):
                for sl in halves:
                    for slot, m in matrices:
                        sp.dma_start(W[sl, slot, sl], m).then_inc(S(done), 16)

            load_blocks("weights loaded", ((WD2, T["L1_gnn_Wd2"]), (WSELF, T["L0_gnn_W_self"]),
                                           (WNEIGH, T["L0_gnn_W_neigh"])))
            for half in range(2):
                for j in range(J):
                    r = half * 3 * J + 3 * j
                    sp.dma_start(Wd1[r:r + 3, 2 * j + half, :], T["L1_gnn_Wd1"]).then_inc(S("weights loaded"), 16)
            sp.dma_start(Wd1[X3:X3 + 1, :, :], T["L1_gnn_bd1"].partition_broadcast(J * 2).unsqueeze(0)) \
                .then_inc(S("weights loaded"), 16)
            for n in range(0, BROWS, 32):
                sp.dma_start(brow[n:n + 1, :, :], T["L1_gnn_bd2"].partition_broadcast(J * 2).unsqueeze(0)) \
                    .then_inc(S("weights loaded"), 16)

            sp.wait_ge(*stage("h0 made"))
            sp.dma_start(tab[0].rearrange("(b p) d -> p b d", p=128), h[:, 0:NB, :]).then_inc(S("table stored", 0), 16)

            def load_x3(m):
                for k in range(2):
                    sp.dma_start(ea3[:, k * X3:(k + 1) * X3].rearrange("p (h x) -> p h x", h=2),
                                 chunk(T["edge_attr_3"], m, k, 3)).then_inc(S("x3 loaded"), 16)

            def load_weight(i, k):
                sp.dma_start(wgt[k].rearrange("p (h j) -> p h j", h=2), chunk(T["edge_weight"], i, k)) \
                    .then_inc(S("L0 weight loaded", k), 16)

            def load_dst(i):
                for hf in range(2):
                    vec = T["dst"][bass.ds(i * (2 * CH) + hf * B0, 2 * CH)]
                    sp.dma_start(dstb[halves[hf], 1:], vec.partition_broadcast(64)).then_inc(S("dst loaded"), 16)

            load_x3(0)
            for k in range(2):
                load_weight(0, k)
            load_dst(0)
            for n, b in enumerate((T["L0_gnn_b_self"], T["L0_gnn_b_neigh"])):
                sp.dma_start(bias0[:, n, :], b.partition_broadcast(128)).then_inc(S("later weights loaded"), 16)
            load_blocks("later weights loaded", ((W1, T["L1_gnn_W1"]), (W2, T["L1_gnn_W2"]), (W3, T["L1_gnn_W3"]),
                                                 (W1A, T["L2_gnn_W1"][0:D, :]), (W1B, T["L2_gnn_W1"][D:2 * D, :]),
                                                 (W2A, T["L2_gnn_W2"][0:D, :]), (W2B, T["L2_gnn_W2"][D:2 * D, :])))
            sp.wait_ge(S("x3 transposed"), 1)
            load_x3(1)
            sp.wait_ge(S("keep made"), past(1))
            load_dst(1)

            def store_scan(layer, i, k):
                sp.wait_ge(S("evacuated", k), n_evacuated(layer, i + 1))
                sp.dma_start(scan_rows(layer, i, k), ostage[k][:, :, :, :].rearrange("p h j d -> p h (j d)")) \
                    .then_inc(S("scan stored", k), 16)

            def l0_body(i, first=False, later=2):
                for k in range(2):
                    if later:
                        next_idx(0, i, k)
                        sp.wait_ge(S("L0 msg made", k), past(i + 1))
                        load_weight(i + 1, k)
                    if k == 0 and not first:
                        store_scan(0, i - 1, 1)
                if later == 2:
                    sp.wait_ge(S("x3 transposed"), i + 2)
                    load_x3(i + 2)
                    sp.wait_ge(S("keep made"), past(i + 2))
                    load_dst(i + 2)
                store_scan(0, i, 0)

            l0_body(0, first=True)
            with sp.Fori(1, NIT - 2) as i:
                l0_body(i)
            l0_body(NIT - 2, later=1)
            l0_body(NIT - 1, later=0)
            store_scan(0, NIT - 1, 1)

            def end_layer(layer):
                for k in range(2):
                    sp.wait_ge(S("gathered", k), n_gathered(layer, NIT))
                first_idx()

            end_layer(0)

            def tail_row(layer, w):
                scans_stored(sp, layer)
                sp.dma_start(tail[:, 0:w], segs[layer][B0 - 1, :].partition_broadcast(128)) \
                    .then_inc(S("tail loaded", layer), 16)

            def node_table(layer, made, src):
                for part, r in PARTS.items():
                    sp.wait_ge(*stage(f"{made} {part}"))
                    sp.dma_start(tab[layer].rearrange("(b p) d -> p b d", p=128)[:, r, :], src[:, r, :]) \
                        .then_inc(S("table stored", layer), 16)

            tail_row(0, D)
            node_table(1, "w3 copied", tabs)
            def load_d(i, k):
                sp.dma_start(dch[k], d_dram[:, at(i, k)]).then_inc(S("d loaded", k), 16)

            sp.wait_ge(S("d stored"), past(NIT, 16))
            for k in range(2):
                load_d(0, k)
            sp.wait_ge(*stage("w1 copied b"))
            sp.dma_start(w1tab.rearrange("(b p) d -> p b d", p=128), w1n).then_inc(S("w1 stored"), 16)

            def l1_store(i, k):
                sp.wait_ge(S("evacuated", k), n_evacuated(1, i + 1))
                sp.dma_start(scan_rows(1, i, k), ostage1[k].rearrange("p h j d -> p h (j d)")) \
                    .then_inc(S("scan stored", k), 16)

            def l1_body(i, first=False, more=True):
                for k in range(2):
                    if more:
                        next_idx(1, i, k)
                        sp.wait_ge(S("u made", k), past(i + 1))
                        load_d(i + 1, k)
                    if k == 1:
                        l1_store(i, 0)
                    elif not first:
                        l1_store(i - 1, 1)

            l1_body(0, first=True)
            with sp.Fori(1, NIT - 1) as i:
                l1_body(i)
            l1_body(NIT - 1, more=False)
            l1_store(NIT - 1, 1)
            end_layer(1)
            sp.wait_ge(*stage("L0 merged b"))
            tail_row(1, 3 * D)
            node_table(2, "w1a copied", tabs[:, :, 0:D])
            def load_ea(i, k):
                sp.wait_ge(S("ea transposed", k), past(i))
                for hf in range(2):
                    sp.dma_start(ea64[k][:, :, hf, :],
                                 T["edge_attr_64"][bass.ds(i * (2 * CH) + k * CH + hf * B0, CH), :]
                                 .rearrange("(p j) d -> p j d", j=J)).then_inc(S("ea loaded", k), 16)

            def load_src(layer, i, k):
                sp.wait_ge(S("pick onehots made", k), n_picked(layer, i))
                sp.dma_start(srcb[layer][k],
                             T["src"][bass.ds(i * (2 * CH) + (k * CH + B0), CH)].partition_broadcast(128)) \
                    .then_inc(S("src spread", k), 16)

            def l2_body(i, picking, src):
                for k in range(2):
                    load_ea(i, k)
                    next_idx(2, i, k, picking)
                    if src:
                        load_src(2, i + 1, k)

            for k in range(2):
                load_src(2, 0, k)
            with sp.Fori(0, NPICK - 1) as i:
                l2_body(i, True, True)
            l2_body(NPICK - 1, True, False)
            with sp.Fori(NPICK, NIT - 1) as i:
                l2_body(i, False, False)
            for k in range(2):
                load_ea(NIT - 1, k)
            end_layer(2)
            with sp.Fori(0, NIT // 2) as n:
                for slot in range(4):
                    i, k = n * 2 + slot // 2, slot % 2
                    sp.wait_ge(S("evacuated", k), n_evacuated(2, i + 1))
                    sp.dma_start(scan_rows(2, i, k), ostage2[slot].rearrange("p h j d -> p h (j d)")) \
                        .then_inc(S("L2 scan stored", slot), 16)
            sp.wait_ge(*stage("L1 tail merged"))
            tail_row(2, D)
            node_table(3, "h3 made", h)
            for k in range(2):
                load_src(3, 0, k)
            with sp.Fori(0, NIT - 1) as i:
                for k in range(2):
                    next_idx(3, i, k)
                    load_src(3, i + 1, k)
                    store_scan(3, i, k)
            for k in range(2):
                store_scan(3, NIT - 1, k)
            sp.wait_ge(*stage("L2 merged b"))
            tail_row(3, D)
            r = PARTS["a"]
            sp.wait_ge(*stage("x4 made a"))
            sp.dma_start(out[0:r.stop * 128, :].rearrange("(b p) d -> p b d", p=128), x[:, r, :]) \
                .then_inc(S("out stored"), 16)
            sp.wait_ge(*stage("x4 made b"))
            sp.dma_start(out[r.stop * 128:(NB - 1) * 128, :].rearrange("(b p) d -> p b d", p=128),
                         x[:, r.stop:NB - 1, :]).then_inc(S("out stored"), 16)
            sp.dma_start(out[(NB - 1) * 128:N, :], x[0:NLAST, NB - 1, :]).then_inc(S("out stored"), 16)
            sp.wait_ge(S("out stored"), 48)

        @block.gpsimd
        def _(pool):
            pool.memset(ident[:, :], 0.0).then_inc(S("consts begun"), 1)
            pool.memset(upper[:, :], 1.0).then_inc(S("consts begun"), 1)
            pool.iota(iota_i, [[1, 128]], base=0, channel_multiplier=0).then_inc(S("iota made"), 1)
            pool.iota(node_i[:, :], [[128, NB]], base=0, channel_multiplier=1).then_inc(S("iota made"), 1)
            pool.wait_ge(S("consts begun"), 2)
            pool.affine_select(out=ident[:, :], in_=ident[:, :], compare_op=ALU.not_equal, fill=1.0, base=0,
                               pattern=[[-1, 128]], channel_multiplier=1).then_inc(S("ident made"), 1)
            pool.affine_select(out=upper[:, :], in_=upper[:, :], compare_op=ALU.is_ge, fill=0.0, base=0,
                               pattern=[[1, 128]], channel_multiplier=-1).then_inc(S("ident made"), 1)

            for n, name in enumerate(("L1_gnn_bd1", "L1_gnn_g1", "L1_gnn_b1", "L1_gnn_bd2", "L1_gnn_g2", "L1_gnn_b2",
                                      "L2_gnn_b1", "L2_gnn_g1", "L2_gnn_be1", "L2_gnn_b2", "L2_gnn_g2", "L2_gnn_be2")):
                if n in (BD1, BD2):
                    continue
                for hf in range(2):
                    pool.dma_start(cols[halves[hf], n:n + 1], T[name].rearrange("(p a) -> p a", a=1)) \
                        .then_inc(S("columns loaded"), 16)

            def gathers(layer, width, freed, freed_n=past, first=0, end=NIT, picking=False):
                with pool.Fori(first, end) as i:
                    for k in range(2):
                        pool.wait_ge(S("table stored", layer), 16 if layer == 0 else 32)
                        pool.wait_ge(S("idx loaded", k), n_idx_loaded(layer, i + 1))
                        pool.wait_ge(S(freed, k), freed_n(i))
                        pool.sem_inc(S("chunk cleared"), 1)
                        for j in range(J):
                            for hf in range(2):
                                q = hf * J + j
                                if picking and q == 2 * J - 1:
                                    continue
                                pool.indirect_dma_start(
                                    out=Gw(k, width)[:, j, hf, :], out_offset=None, in_=tab[layer],
                                    in_offset=bass.IndirectOffsetOnAxis(ap=idx[k][:, q:q + 1].bitcast(U32), axis=0)) \
                                    .then_inc(S("gathered", k), 16)

            def last_rows(layer, width):
                scans_stored(pool, layer)
                if layer == 1:
                    pool.wait_ge(S("w1 stored"), 16)
                    for row, table, n in ((span_row, segs[1], 0), (span_w1, w1tab, 1)):
                        pool.indirect_dma_start(
                            out=row, out_offset=None, in_=table,
                            in_offset=bass.IndirectOffsetOnAxis(ap=spanidx[:, n:n + 1], axis=0)) \
                            .then_inc(S("span rows"), 16)
                for part, r in PARTS.items():
                    for b in range(r.start, r.stop):
                        pool.indirect_dma_start(
                            out=agg[:, b * width:(b + 1) * width], out_offset=None, in_=segs[layer],
                            in_offset=bass.IndirectOffsetOnAxis(ap=rowidx[:, b:b + 1], axis=0)) \
                            .then_inc(S(f"last rows {part}"), 16)

            gathers(0, D, "L0 msg made")
            pool.wait_ge(*stage("rowidx made"))
            last_rows(0, D)
            gathers(1, 2 * D, "L1 split")
            last_rows(1, 3 * D)
            gathers(2, D, "hidden made", end=NPICK, picking=True)
            gathers(2, D, "hidden made", first=NPICK)
            last_rows(2, D)
            gathers(3, D, "in transposed", lambda n: n_in_transposed(3, n), picking=True)
            last_rows(3, D)

        @block.tensor
        def _(pe):
            def to_channels(src, made, done, part=None, b=0):
                pe.wait_ge(*stage(made))
                for q in PAIRS[part] if part else range(NPAIR):
                    last = nc.tensor.transpose(PF[:, b * 512 + q * 128:b * 512 + (q + 1) * 128],
                                               src[:, 2 * q:2 * q + 2, :].rearrange("p b d -> p (b d)"), ident[:, :])
                last.then_inc(stage_of(done), 1)

            def linear(rhs, b, done, part=None):
                for q in PAIRS[part] if part else range(NPAIR):
                    last = nc.tensor.matmul(PF[:, b * 512 + q * 128:b * 512 + (q + 1) * 128],
                                            hT[:, q * 128:(q + 1) * 128], rhs, start=True, stop=True)
                last.then_inc(stage_of(done), 1)

            pe.wait_ge(S("ident made"), 2)
            pe.wait_ge(*stage("weights ready"))
            for n in range(2):
                last = nc.tensor.transpose(P[:, 0, n * 128:(n + 1) * 128], W[:, WSELF + n, :], ident[:, :])
            last.then_inc(stage_of("L0 weights transposed"), 1)
            pe.wait_ge(*stage("L0 weights copied"))
            to_channels(h, "h0 made", "h0 transposed")
            pe.wait_ge(*stage("first onehots made"))
            for t in range(HPRE):
                last = nc.tensor.matmul(P[:, 7, 0:NB], one_p[0:HR, t * 128:(t + 1) * 128],
                                        one_b[0:HR, t * NB:(t + 1) * NB], start=(t == 0), stop=True,
                                        skip_group_check=True)
            last.then_inc(stage_of("first hist added"), 1)

            def x3_transposes(m, event=None):
                pe.wait_ge(S("x3 loaded"), (m + 1) * 32)
                if event is not None:
                    pe.wait_ge(S("gelu made"), past(event))
                for k in range(2):
                    last = nc.tensor.transpose(P[0:X3, 4, k * 128:(k + 1) * 128], ea3[:, k * X3:(k + 1) * X3],
                                               ident[:, :])
                last.then_inc(S("x3 transposed"), 1)

            def mlp1_products(m, first=False):
                pe.wait_ge(S("x3 copied"), m + 1)
                if not first:
                    pe.wait_ge(S("norms1 made"), m)
                for k in range(2):
                    last = nc.tensor.matmul(P[:, k, :], x3t[0:X3 + 1, k * 128:(k + 1) * 128],
                                            Wd1[:, :, :].rearrange("p r d -> p (r d)"), start=True, stop=True)
                last.then_inc(S("mlp1 made"), 1)

            def mlp2_products():
                for k in range(2):
                    nc.tensor.matmul(P[:, 2 + k, :], bones[0:BROWS, :], brow3[0:BROWS, :], start=True, stop=True)
                    for j in range(J):
                        last = nc.tensor.matmul(P[:, 2 + k, j * 128:(j + 1) * 128], y1[k][:, j::J], W[:, WD2, :],
                                                start=False, stop=True, skip_group_check=True)
                last.then_inc(S("mlp2 made"), 1)

            def norm_transpose(layer, k):
                for j in range(J):
                    last = nc.tensor.transpose(P[:, 4, j::J],
                                               mlp[layer][:, k * CH + j * 128:k * CH + (j + 1) * 128], ident[:, :])
                last.then_inc(S("norm transposed"), 1)

            def l0_in(i, k):
                pe.wait_ge(S("L0 msg made", k), past(i + 1))
                pe.wait_ge(S("scanned", 1 - k), n_scanned(0, i + k))
                for j in range(J):
                    last = nc.tensor.transpose(P[:, 5, j::J], msg[k][:, j * 128:(j + 1) * 128], ident[:, :])
                last.then_inc(S("in transposed", k), 1)

            def l0_out(i, k):
                pe.wait_ge(S("scanned", k), n_scanned(0, i + 1))
                pe.wait_ge(S("evacuated", 1 - k), n_evacuated(0, i + k))
                for j in range(J):
                    last = nc.tensor.transpose(P[:, 6, j * 128:(j + 1) * 128], scanb[k][:, j::J], ident[:, :])
                last.then_inc(S("out transposed", k), 1)

            def l0_hist(i):
                pe.wait_ge(S("onehots made"), i + 1)
                for t in range(HSTEP):
                    last = nc.tensor.matmul(P[:, 7, 0:NB], one_p[0:HR, t * 128:(t + 1) * 128],
                                            one_b[0:HR, t * NB:(t + 1) * NB], start=False, stop=True,
                                            skip_group_check=True)
                last.then_inc(S("hist added"), 1)

            def l0_body(i, first=False, more=True):
                g = events(i, first)
                if more:
                    x3_transposes(i + 1, g)
                    pe.wait_ge(S("x3 copied"), i + 2)
                else:
                    pe.wait_ge(S("gelu made"), past(g))
                pe.wait_ge(S("norms1 made"), i + 1)
                norm_transpose(0, 0)
                l0_in(i, 0)
                if more:
                    mlp1_products(i + 1)
                pe.wait_ge(S("gelu made"), past(g + 1))
                norm_transpose(0, 1)
                if not first:
                    l0_out(i - 1, 1)
                pe.wait_ge(S("gelu made"), past(g + 2))
                if not first:
                    pe.wait_ge(S("norms2 made"), past(i))
                    norm_transpose(1, 0)
                l0_in(i, 1)
                if not first:
                    pe.wait_ge(S("gelu made"), past(g + 3))
                    norm_transpose(1, 1)
                if more:
                    mlp2_products()
                l0_hist(i)
                l0_out(i, 0)

            x3_transposes(0)
            mlp1_products(0, first=True)
            l0_body(0, first=True)
            with pe.Fori(1, NIT - 1) as i:
                l0_body(i)
            l0_body(NIT - 1, more=False)
            l0_out(NIT - 1, 1)

            pe.wait_ge(*stage("counts copied"))
            nc.tensor.matmul(P[:, 7, 64:64 + NB], upper[:, :], small[:, 0, 0:NB], start=True, stop=True)
            nc.tensor.matmul(P[:, 7, 96:96 + NB], ones[:, :], small[:, 0, 0:NB], start=True, stop=True) \
                .then_inc(stage_of("prefix made"), 1)
            mlp2_products()
            pe.wait_ge(S("norms2 made"), past(NIT))
            for k in range(2):
                pe.wait_ge(S("gelu made"), past(events(NIT) + k))
                norm_transpose(1, k)

            pe.wait_ge(*stage("span parts made"))
            nc.tensor.matmul(P[:, 7, 128:130], ones[:, :], small[:, 7, 0:2], start=True, stop=True) \
                .then_inc(stage_of("span parts summed"), 1)

            pe.wait_ge(*stage("rows indexed"))
            pe.wait_ge(S("gelu made"), past(events(NIT) + 2))
            pe.wait_ge(S("later weights loaded"), 16 * 16)
            linear(W[:, WSELF_T, :], 4, "self made")
            for part in PARTS:
                to_channels(tmp, f"L0 merged {part}", f"agg0 transposed {part}", part)
                pe.wait_ge(*stage(f"agg0T copied {part}"))
                pe.wait_ge(*stage("x self added"))
                linear(W[:, WNEIGH_T, :], 4, f"neigh made {part}", part)
            for part in PARTS:
                to_channels(h, f"h1 made {part}", f"h1 transposed {part}", part)
                pe.wait_ge(*stage(f"h1T copied {part}"))
                linear(W[:, W2, :], 4, f"w2 made {part}", part)
                linear(W[:, W3, :], 0, f"w3 made {part}", part)
            for part in PARTS:
                pe.wait_ge(*stage(f"w2 copied {part}"))
                linear(W[:, W1, :], 4, f"w1 made {part}", part)
            pe.wait_ge(*stage("w3 copied b"))
            pe.wait_ge(*stage("w1 copied b"))

            def l1_out_m(i, k):
                pe.wait_ge(S("m scanned", k), past(i + 1))
                pe.wait_ge(S("m evacuated", 1 - k), past(i + k))
                for j in range(J):
                    last = nc.tensor.transpose(P[:, 2, j * 128:(j + 1) * 128], mrun[k][:, 1 + j:CH + 1:J], ident[:, :])
                last.then_inc(S("m transposed", k), 1)

            def l1_out(i, k):
                pe.wait_ge(S("scanned", k), n_scanned(1, i + 1))
                pe.wait_ge(S("evacuated", 1 - k), n_evacuated(1, i + k))
                for n, run in enumerate((srun[k], orun[k])):
                    for j in range(J):
                        last = nc.tensor.transpose(P[:, 3 + n, j * 128:(j + 1) * 128], run[:, j::J], ident[:, :])
                last.then_inc(S("out transposed", k), 1)

            def l1_body(i, first=False):
                for k in range(2):
                    pe.wait_ge(S("L1 split", k), past(i + 1))
                    pe.wait_ge(S("logits made", 1 - k), past(i + k))
                    for j in range(J):
                        last = nc.tensor.transpose(P[:, 0, j::J], wsplit[k][:, j * 128:(j + 1) * 128], ident[:, :])
                    last.then_inc(S("L1 w2 transposed", k), 1)
                    pe.wait_ge(S("u made", 1 - k), past(i + k))
                    for j in range(J):
                        last = nc.tensor.transpose(P[:, 1, j::J], wsplit[k][:, CH + j * 128:CH + (j + 1) * 128],
                                                   ident[:, :])
                    last.then_inc(S("in transposed", k), 1)
                    if k == 1:
                        l1_out(i, 0)
                    elif not first:
                        l1_out(i - 1, 1)
                    l1_out_m(i, k)

            l1_body(0, first=True)
            with pe.Fori(1, NIT) as i:
                l1_body(i)
            l1_out(NIT - 1, 1)

            pe.wait_ge(S("evacuated", 1), n_evacuated(1, NIT))
            for part in PARTS:
                to_channels(h, f"h2 made {part}", f"h2 transposed {part}", part)
                pe.wait_ge(*stage(f"h2T copied {part}"))
                linear(W[:, W1A, :], 4, f"w1a made {part}", part)
            pe.wait_ge(*stage("w1a copied b"))

            def pick_rows(layer, i, k, bank):
                pe.wait_ge(S("pick onehots made", k), n_picked(layer, i + 1))
                pe.wait_ge(S("rows picked", k), n_picked(layer, i))
                for b in range(NB):
                    last = nc.tensor.matmul(P[:, bank, 0:3 * D], pick[layer][k][:, b, :],
                                            split[layer][:, b, :, :].rearrange("p n d -> p (n d)"),
                                            start=(b == 0), stop=(b == NB - 1))
                last.then_inc(S("rows multiplied", k), 1)

            def l2_body(i, picking):
                for k in range(2):
                    pe.wait_ge(S("ea loaded", k), past(i + 1, 32))
                    pe.wait_ge(S("eaT copied", k), past(i))
                    for j in range(J):
                        last = nc.tensor.transpose(P[:, k, j::J], ea64[k][:, j, :, :].rearrange("p h d -> p (h d)"),
                                                   ident[:, :])
                    last.then_inc(S("ea transposed", k), 1)
                    if picking:
                        pick_rows(2, i, k, 4 + k)
                    pe.wait_ge(S("eaT copied", k), past(i + 1))
                    pe.wait_ge(S("hidden made", k), past(i))
                    nc.tensor.matmul(P[:, 2 + k, :], W[:, W1B, :], eaT, start=True, stop=True) \
                        .then_inc(S("ea product made", k), 1)
                    pe.wait_ge(S("gathered", k), n_gathered(2, i + 1, picking))
                    if picking:
                        pe.wait_ge(S("rows picked", k), n_picked(2, i + 1))
                    for j in range(J):
                        last = nc.tensor.matmul(P[:, 2 + k, j::J], pair(k, j), ident[:, :],
                                                start=False, stop=True, skip_group_check=True)
                    last.then_inc(S("hidden summed", k), 1)

            pe.wait_ge(*stage("w1a split"))
            with pe.Fori(0, NPICK) as i:
                l2_body(i, True)
            with pe.Fori(NPICK, NIT) as i:
                l2_body(i, False)

            def combine(tag):
                for n, name in enumerate(("mean", "var")):
                    pe.wait_ge(*stage(f"{tag} {name} part made"))
                    nc.tensor.matmul(P[:, 7, n:n + 1], both[:, :], bn[:, 2 + n:3 + n], start=True, stop=True) \
                        .then_inc(stage_of(f"{tag} {name} summed"), 1)

            combine("edge bn")
            with pe.Fori(0, NIT) as i:
                for k in range(2):
                    pe.wait_ge(S("scanned", k), n_scanned(2, i + 1))
                    pe.wait_ge(S("evacuated", k), n_evacuated(2, i))
                    for j in range(J):
                        last = nc.tensor.transpose(P[:, k, j * 128:(j + 1) * 128], scanb[k][:, j::J], ident[:, :])
                    last.then_inc(S("out transposed", k), 1)

            pe.wait_ge(S("evacuated", 0), n_evacuated(2, NIT))
            pe.wait_ge(S("evacuated", 1), n_evacuated(2, NIT))
            pe.wait_ge(*stage("edge bn ready"))
            for q in range(4):
                w = min(512, NPAIR * 128 - q * 512)
                nc.tensor.matmul(P[:, 4 + q, 0:w], W[:, W2A, :], hT[:, q * 512:q * 512 + w], start=True, stop=True)
            for part, banks in (("a", (0, 1)), ("b", (2, 3))):
                to_channels(tmp, f"L2 merged {part}", f"agg2 transposed {part}", part)
                pe.wait_ge(*stage(f"agg2T copied {part}"))
                for q in banks:
                    w = min(512, NPAIR * 128 - q * 512)
                    last = nc.tensor.matmul(P[:, 4 + q, 0:w], W[:, W2B, :], agg[:, q * 512:q * 512 + w],
                                            start=False, stop=True, skip_group_check=True)
                last.then_inc(stage_of(f"z made {part}"), 1)
            pe.wait_ge(*stage("z copied"))
            combine("node bn")
            for part in PARTS:
                pe.wait_ge(*stage(f"z activated {part}"))
                for q in PAIRS[part]:
                    last = nc.tensor.transpose(PF[:, q * 128:(q + 1) * 128], agg[:, q * 128:(q + 1) * 128],
                                               ident[:, :])
                last.then_inc(stage_of(f"z transposed {part}"), 1)

            def l3_out(i, k):
                pe.wait_ge(S("scanned", k), n_scanned(3, i + 1))
                pe.wait_ge(S("evacuated", k), n_evacuated(3, i))
                for j in range(J):
                    last = nc.tensor.transpose(P[:, 6 + k, j * 128:(j + 1) * 128], scanb[k][:, j::J], ident[:, :])
                last.then_inc(S("out transposed", k), 1)

            def l3_body(i, first=False):
                for k in range(2):
                    pick_rows(3, i, k, k)
                    if k == 1:
                        l3_out(i, 0)
                    elif not first:
                        l3_out(i - 1, 1)
                    pe.wait_ge(S("gathered", k), n_gathered(3, i + 1))
                    pe.wait_ge(S("rows picked", k), n_picked(3, i + 1))
                    pe.wait_ge(S("scanned", k), n_scanned(3, i))
                    for j in range(J):
                        last = nc.tensor.transpose(P[:, 4 + k, j::J], pair(k, j), ident[:, :])
                    last.then_inc(S("in transposed", k), 1)

            pe.wait_ge(*stage("h3 split"))
            l3_body(0, first=True)
            with pe.Fori(1, NIT) as i:
                l3_body(i)
            l3_out(NIT - 1, 1)

        @block.scalar
        def _(act):
            def copy(dst, src, need, done, scale=1.0):
                act.wait_ge(*stage(need))
                nc.scalar.activation(dst, src, ACT.Copy, scale=scale).then_inc(stage_of(done), 1)

            def evacuate(layer, i, k, bank):
                act.wait_ge(S("out transposed", k), n_out_transposed(layer, i + 1))
                act.wait_ge(S("scan stored", k), n_scan_stored(layer, i))
                nc.scalar.activation(ostage[k][:, :, :, :].rearrange("p h j d -> p j h d"),
                                     P[:, bank, :].rearrange("p (j h d) -> p j h d", h=2, d=D), ACT.Copy) \
                    .then_inc(S("evacuated", k), 1)

            copy(W[:, WSELF_T:WNEIGH_T + 1, :].rearrange("p a d -> p (a d)"), P[:, 0, 0:256],
                 "L0 weights transposed", "L0 weights copied")
            copy(hT[:, :], PF[:, 0:NPAIR * 128], "h0 transposed", "h0T copied")

            def x3_copy(m):
                act.wait_ge(S("x3 transposed"), m + 1)
                nc.scalar.activation(x3t[0:X3, :], P[0:X3, 4, 0:256], ACT.Copy).then_inc(S("x3 copied"), 1)

            def squares(layer, n):
                act.wait_ge(S(f"mlp{layer + 1} made"), n + 1)
                nc.scalar.activation(square[layer], PF[:, layer * 2 * CH:(layer + 1) * 2 * CH], ACT.Square) \
                    .then_inc(S(f"squares{layer + 1} made"), 1)

            def gelu1(k, event):
                act.wait_ge(S("norm transposed"), event)
                nc.scalar.activation(y1[k], P[:, 4, :], ACT.Gelu, bias=cols[:, B1:B1 + 1],
                                     scale=cols[:, G1:G1 + 1]).then_inc(S("gelu made"), 1)

            def gelu2(k, event):
                act.wait_ge(S("norm transposed"), event)
                nc.scalar.activation(dout[:, k * CH:(k + 1) * CH], P[:, 4, :], ACT.Gelu, bias=cols[:, B2:B2 + 1],
                                     scale=cols[:, G2:G2 + 1]).then_inc(S("gelu made"), 1)

            def store_d(m, event):
                act.wait_ge(S("gelu made"), past(event))
                act.dma_start(d_dram[:, bass.ds(m * (2 * CH), 2 * CH)], dout).then_inc(S("d stored"), 16)

            def l0_body(i, first=False, more=True):
                g = events(i, first)
                if more:
                    x3_copy(i + 1)
                gelu1(0, g + 1)
                if more:
                    squares(0, i + 1)
                gelu1(1, g + 2)
                if not first:
                    evacuate(0, i - 1, 1, 6)
                if not first:
                    act.wait_ge(S("d stored"), past(i - 1, 16))
                    gelu2(0, g + 3)
                    gelu2(1, g + 4)
                    store_d(i - 1, g + 4)
                if more:
                    squares(1, i)
                evacuate(0, i, 0, 6)

            x3_copy(0)
            squares(0, 0)
            act.wait_ge(S("columns loaded"), 16 * 20)
            l0_body(0, first=True)
            with act.Fori(1, NIT - 1) as i:
                l0_body(i)
            l0_body(NIT - 1, more=False)
            evacuate(0, NIT - 1, 1, 6)
            squares(1, NIT - 1)
            act.wait_ge(S("d stored"), past(NIT - 1, 16))
            gelu2(0, events(NIT) + 1)
            gelu2(1, events(NIT) + 2)
            store_d(NIT - 1, events(NIT) + 2)

            def copy_channels(dst, need, done, part):
                c = slice(PAIRS[part].start * 128, PAIRS[part].stop * 128)
                copy(dst[:, c], PF[:, c], f"{need} {part}", f"{done} {part}")

            def copy_nodes(dst, bank, need, done, part, scale=1.0):
                r = PARTS[part]
                copy(dst[:, r, :], PF[:, bank * 512:bank * 512 + NV].rearrange("p (b d) -> p b d", d=D)[:, r, :],
                     f"{need} {part}", f"{done} {part}", scale=scale)

            for part in PARTS:
                copy_channels(hT, "agg0 transposed", "agg0T copied", part)
            for part in PARTS:
                copy_channels(hT, "h1 transposed", "h1T copied", part)
                copy_nodes(tabs[:, :, 0:D], 4, "w2 made", "w2 copied", part, scale=-1.0)
                copy_nodes(tabs[:, :, D:2 * D], 0, "w3 made", "w3 copied", part)
            for part in PARTS:
                copy_nodes(w1n, 4, "w1 made", "w1 copied", part)
            act.wait_ge(S("d stored"), past(NIT, 16))
            act.wait_ge(S("keep made"), past(NIT))

            def l1_evacuate_run(i, k, n):
                return nc.scalar.activation(
                    ostage1[k][:, :, :, n * D:(n + 1) * D].rearrange("p h j d -> p j h d"),
                    P[:, 2 + n, :].rearrange("p (j h d) -> p j h d", h=2, d=D), ACT.Copy)

            def l1_evacuate_m(i, k):
                act.wait_ge(S("m transposed", k), past(i + 1))
                act.wait_ge(S("scan stored", k), n_scan_stored(1, i))
                l1_evacuate_run(i, k, 0).then_inc(S("m evacuated", k), 1)

            def l1_evacuate(i, k):
                act.wait_ge(S("out transposed", k), n_out_transposed(1, i + 1))
                for n in (1, 2):
                    last = l1_evacuate_run(i, k, n)
                last.then_inc(S("evacuated", k), 1)

            def l1_negate(i, k):
                act.wait_ge(S("m scanned", k), past(i))
                nc.scalar.activation(neg[k], keep[:, at(i, k)], ACT.Copy, scale=BIG, bias=-BIG) \
                    .then_inc(S("neg made", k), 1)

            def l1_body(i, first=False, more=True):
                for k in range(2):
                    act.wait_ge(S("gathered", k), n_gathered(1, i + 1))
                    act.wait_ge(S("in transposed", k), n_in_transposed(1, i))
                    nc.scalar.activation(wsplit[k].rearrange("p (n r d) -> p r n d", n=2, d=D),
                                         Gring[k][:, :].rearrange("p (r n d) -> p r n d", n=2, d=D), ACT.Copy) \
                        .then_inc(S("L1 split", k), 1)
                    before = (i, 0) if k == 1 else (i - 1, 1)
                    if k == 1 or not first:
                        l1_evacuate_m(*before)
                    if k == 0:
                        l1_negate(i, 1)
                    elif more:
                        l1_negate(i + 1, 0)
                    act.wait_ge(S("diff made", k), past(i + 1))
                    nc.scalar.activation(soft[k], soft[k], ACT.Exp).then_inc(S("expd made", k), 1)
                    if k == 1 or not first:
                        l1_evacuate(*before)

            l1_negate(0, 0)
            l1_body(0, first=True)
            with act.Fori(1, NIT - 1) as i:
                l1_body(i)
            l1_body(NIT - 1, more=False)
            l1_evacuate_m(NIT - 1, 1)
            l1_evacuate(NIT - 1, 1)

            act.wait_ge(*stage("merge diffs made"))
            nc.scalar.activation(factors, factors, ACT.Exp).then_inc(stage_of("merge factors made"), 1)
            for part in PARTS:
                copy_channels(hT, "h2 transposed", "h2T copied", part)
                copy_nodes(tabs[:, :, 0:D], 4, "w1a made", "w1a copied", part)

            with act.Fori(0, NIT) as i:
                for k in range(2):
                    act.wait_ge(S("ea transposed", k), past(i + 1))
                    act.wait_ge(S("ea product made", 1 - k), past(i + k))
                    nc.scalar.activation(eaT, P[:, k, :], ACT.Copy).then_inc(S("eaT copied", k), 1)
                    act.wait_ge(S("hidden summed", k), past(i + 1))
                    nc.scalar.activation(arena[:, at(i, k)], P[:, 2 + k, :], ACT.Identity, bias=cols[:, LB1:LB1 + 1]) \
                        .then_inc(S("hidden made", k), 1)

            def activate(m):
                pair_m = arena[:, bass.ds(m * (2 * CH), 2 * CH)]
                nc.scalar.activation(pair_m, pair_m, ACT.Silu, bias=bn[:, 6:7], scale=bn[:, 5:6]) \
                    .then_inc(S("edges activated"), 1)

            def l2_evacuate(n, slot):
                i, k = n * 2 + slot // 2, slot % 2
                act.wait_ge(S("out transposed", k), n_out_transposed(2, i + 1))
                act.wait_ge(S("L2 scan stored", slot), past(n, 16))
                nc.scalar.activation(ostage2[slot].rearrange("p h j d -> p j h d"),
                                     P[:, k, :].rearrange("p (j h d) -> p j h d", h=2, d=D), ACT.Copy) \
                    .then_inc(S("evacuated", k), 1)

            def l2_body(n, more=True):
                for slot in range(4):
                    if more and slot % 2 == 0:
                        activate(n * 2 + 2 + slot // 2)
                    l2_evacuate(n, slot)

            act.wait_ge(*stage("edge bn ready"))
            activate(0)
            activate(1)
            with act.Fori(0, NIT // 2 - 1) as n:
                l2_body(n)
            l2_body(NIT // 2 - 1, more=False)

            for part in PARTS:
                copy_channels(agg, "agg2 transposed", "agg2T copied", part)
            act.wait_ge(*stage("z made b"))
            nc.scalar.activation(tabs[:, 0:NPAIR, :].rearrange("p b d -> p (b d)"), PF[:, 2048:2048 + NPAIR * 128],
                                 ACT.Identity, bias=cols[:, LB2:LB2 + 1]).then_inc(stage_of("z copied"), 1)
            act.wait_ge(*stage("node bn ready"))
            for part in PARTS:
                c = slice(PAIRS[part].start * 128, PAIRS[part].stop * 128)
                nc.scalar.activation(agg[:, c], tabs[:, 0:NPAIR, :].rearrange("p b d -> p (b d)")[:, c],
                                     ACT.Silu, bias=bn[:, 6:7], scale=bn[:, 5:6]) \
                    .then_inc(stage_of(f"z activated {part}"), 1)

            with act.Fori(0, NIT) as i:
                for k in range(2):
                    evacuate(3, i, k, 6 + k)

        @block.vector
        def _(dve):
            v = nc.vector
            steps = [0]

            def step(ins):
                steps[0] += 1
                ins.then_inc(S("dve step"), 1)
                dve.wait_ge(S("dve step"), steps[0])

            def bc(colmat, r=slice(0, NB)):
                return colmat[:, r].unsqueeze(2).to_broadcast([128, r.stop - r.start, D])

            def rsqrt(n, step, tuned=False):
                arg, res, t = (rs[:, m, n] for m in range(3))
                magic, first = (0x5f1ffff9, (0.703952253, 2.38924456)) if tuned else (0x5f3759df, (0.5, 3.0))
                step(v.tensor_scalar(t.bitcast(I32), arg.bitcast(I32), 1, None, ALU.arith_shift_right))
                step(v.tensor_scalar(res.bitcast(I32), t.bitcast(I32), -1.0, float(magic), ALU.mult, ALU.add))
                for c, m in (first, *[(0.5, 3.0)] * (1 if tuned else 2)):
                    step(v.scalar_tensor_tensor(t, res, -c, arg, ALU.mult, ALU.mult))
                    step(v.tensor_tensor(t, t, res, ALU.mult))
                    step(v.scalar_tensor_tensor(res, t, c * m, res, ALU.add, ALU.mult))

            def layernorm_relu(dst, done, r=slice(0, NB)):
                xs, xc, hs = x[:, r, :], tmp[:, r, :], dst[:, r, :]
                s1, s2 = small[:, 1, r], small[:, 2, r]
                step(v.reduce_sum(s1, xs, axis=AX))
                step(v.tensor_scalar(s1, s1, 1.0 / D, None, ALU.mult))
                step(v.tensor_tensor(xc, xs, bc(small[:, 1, :], r), ALU.subtract))
                step(v.tensor_tensor(hs, xc, xc, ALU.mult))
                step(v.reduce_sum(s2, hs, axis=AX))
                step(v.tensor_scalar(rs[:, 0, r], s2, 1.0 / D, EPS, ALU.mult, ALU.add))
                rsqrt(r, step)
                step(v.scalar_tensor_tensor(hs, xc, 0.0, bc(rs[:, 1, :], r), ALU.max, ALU.mult))
                dve.sem_inc(stage_of(done), 1)

            def add_to_x(bank, r=slice(0, NB)):
                step(v.tensor_tensor(x[:, r, :], x[:, r, :],
                                     PF[:, bank * 512:bank * 512 + NV].rearrange("p (b d) -> p b d", d=D)[:, r, :],
                                     ALU.add))

            step(v.memset(x[:, NB - 1:NBP, :], 0.0))
            dve.sem_inc(stage_of("x cleared"), 1)
            for t in (W[:, :, :], Wd1[:, :, :], brow[:, :, :], h[:, NB:NBP, :]):
                step(v.memset(t, 0.0))
            dve.sem_inc(stage_of("consts cleared"), 1)
            dve.wait_ge(S("x loaded"), 32)
            layernorm_relu(h, "h0 made")

            step(v.memset(ones[:, :], 1.0))
            dve.wait_ge(S("ident made"), 2)
            dve.wait_ge(S("weights loaded"), 16 * 18)
            for m, s in ((Wd1[:, :, :], small[0:X3 + 1, 3, 0:2 * J]),
                         (brow[:, :, :], small[0:BROWS, 5, 0:2 * J]),
                         (W[:, WD2, :].rearrange("p (a d) -> p a d", d=D), small[:, 4, 0:2])):
                step(v.reduce_sum(s, m, axis=AX))
                step(v.tensor_scalar(s, s, 1.0 / D, None, ALU.mult))
                step(v.tensor_tensor(m, m, s.unsqueeze(2).to_broadcast(list(m.shape)), ALU.subtract))
            row = brow[:, :, :].rearrange("p r d -> p (r d)")
            step(v.memset(brow3[0:BROWS, :], 0.0))
            for n in range(3):
                step(v.tensor_copy(bpart[0:BROWS, :], row))
                step(v.tensor_copy(brow3[32 * n:32 * n + 1, :], bpart[32 * n:32 * n + 1, :]))
                step(v.tensor_copy(bres[0:BROWS, :], bpart[0:BROWS, :]))
                step(v.tensor_tensor(row, row, bres[0:BROWS, :], ALU.subtract))
            step(v.memset(bones[0:BROWS, :], 1.0))
            step(v.memset(x3t[0:32, :], 1.0))
            dve.sem_inc(stage_of("weights ready"), 1)
            dve.wait_ge(S("iota made"), 2)
            dve.wait_ge(S("dst by row loaded"), 16)
            step(v.tensor_copy(iota_f, iota_i))
            step(v.tensor_scalar(dst_b[0:HR, :].bitcast(I32), dst_pm[0:HR, :], 7, None, ALU.arith_shift_right))
            step(v.tensor_scalar(dst_pm[0:HR, :], dst_pm[0:HR, :], 127, None, ALU.bitwise_and))
            step(v.tensor_copy(dst_p[0:HR, :], dst_pm[0:HR, :]))
            step(v.tensor_copy(dst_b[0:HR, :], dst_b[0:HR, :].bitcast(I32)))

            def onehots(first, n):
                for key, dst, w in ((dst_p, one_p, 128), (dst_b, one_b, NB)):
                    last = v.tensor_tensor(dst[0:HR, 0:n * w].rearrange("p (t c) -> p t c", c=w),
                                           key[0:HR, first].unsqueeze(2).to_broadcast([HR, n, w]),
                                           iota_f[0:HR, 0:w].unsqueeze(1).to_broadcast([HR, n, w]), ALU.is_equal)
                return last

            onehots(slice(0, HPRE), HPRE).then_inc(stage_of("first onehots made"), 1)
            step(v.memset(dstb[:, 0:1], -1))
            step(v.memset(scanb[1][:, CH - 1:CH], 0.0))

            def norms(layer, n, transposed=None):
                made = [0]
                name = f"norm{layer + 1} step"

                def norm_step(ins):
                    made[0] += 1
                    ins.then_inc(S(name), 1)
                    dve.wait_ge(S(name), n * 9 + made[0])

                r = slice(layer * 4 * J, (layer + 1) * 4 * J)
                dve.wait_ge(S(f"squares{layer + 1} made"), n + 1)
                v.reduce_sum(rs[:, 2, r], square[layer].rearrange("p (r d) -> p r d", d=D), axis=AX) \
                    .then_inc(S(f"squares{layer + 1} summed"), 1)
                dve.wait_ge(S(f"squares{layer + 1} summed"), n + 1)
                norm_step(v.tensor_scalar(rs[:, 0, r], rs[:, 2, r], 1.0 / D, EPS, ALU.mult, ALU.add))
                rsqrt(r, norm_step, tuned=True)
                assert made[0] == 9
                if transposed is not None:
                    dve.wait_ge(S("norm transposed"), transposed)
                v.tensor_tensor(mlp[layer].rearrange("p (r d) -> p r d", d=D),
                                PF[:, layer * 2 * CH:(layer + 1) * 2 * CH].rearrange("p (r d) -> p r d", d=D),
                                rs[:, 1, r].unsqueeze(2).to_broadcast([128, 4 * J, D]), ALU.mult) \
                    .then_inc(S(f"norms{layer + 1} made"), 1)

            def l0_message(i, k):
                dve.wait_ge(S("gathered", k), n_gathered(0, i + 1))
                dve.wait_ge(S("L0 weight loaded", k), past(i + 1, 16))
                dve.wait_ge(S("in transposed", k), n_in_transposed(0, i))
                v.tensor_tensor(msg[k].rearrange("p (j h d) -> p j h d", h=2, d=D), Gw(k, D),
                                wgt[k].rearrange("p (h j) -> p j h", h=2).unsqueeze(3)
                                .to_broadcast([128, J, 2, D]), ALU.mult).then_inc(S("L0 msg made", k), 1)

            def l0_scan(i, k):
                dve.wait_ge(S("in transposed", k), n_in_transposed(0, i + 1))
                dve.wait_ge(S("scanned", 1 - k), n_scanned(0, i + k))
                dve.wait_ge(S("out transposed", k), n_out_transposed(0, i))
                v.tensor_tensor_scan(scanb[k][:, :], keep[:, at(i, k)], P[:, 5, :],
                                     scanb[1 - k][:, CH - 1:CH], ALU.mult, ALU.add).then_inc(S("scanned", k), 1)

            def compare(i):
                dve.wait_ge(S("dst loaded"), (i + 1) * 32)
                v.tensor_tensor(keep[:, bass.ds(i * (2 * CH), 2 * CH)], dstb[:, 1:2 * CH + 1], dstb[:, 0:2 * CH],
                                ALU.is_equal).then_inc(S("pair compared"), 1)
                dve.wait_ge(S("pair compared"), i + 1)
                v.tensor_copy(dstb[:, 0:1], dstb[:, 2 * CH:2 * CH + 1]).then_inc(S("keep made"), 1)

            def count(i):
                dve.wait_ge(S("hist added"), past(i))
                onehots(bass.ds(i * HSTEP + HPRE, HSTEP), HSTEP).then_inc(S("onehots made"), 1)

            def l0_body(i, first=False, more=True):
                if not more:
                    count(i)
                if not first:
                    norms(1, i - 1)
                dve.wait_ge(S("keep made"), past(i + 1))
                l0_scan(i, 0)
                l0_message(i, 1)
                if more:
                    count(i)
                    norms(0, i + 1, events(i, first) + 2)
                    compare(i + 1)
                    l0_message(i + 1, 0)
                l0_scan(i, 1)

            compare(0)
            l0_message(0, 0)
            norms(0, 0)
            dve.wait_ge(*stage("first hist added"))
            l0_body(0, first=True)
            with dve.Fori(1, NIT - 1) as i:
                l0_body(i)
            l0_body(NIT - 1, more=False)

            cnt, pre, tot, incl, end, ge = (small[:, n, 0:NB] for n in range(6))
            dve.wait_ge(S("hist added"), past(NIT))
            step(v.tensor_copy(cnt, P[:, 7, 0:NB]))
            dve.sem_inc(stage_of("counts copied"), 1)
            dve.wait_ge(*stage("prefix made"))
            step(v.tensor_copy(pre, P[:, 7, 64:64 + NB]))
            step(v.tensor_copy(tot, P[:, 7, 96:96 + NB]))
            step(v.tensor_tensor_scan(incl, ones[:, 0:NB], tot, 0.0, ALU.mult, ALU.add))
            step(v.tensor_tensor(end, incl, tot, ALU.subtract))
            step(v.tensor_tensor(end, end, pre, ALU.add))
            step(v.tensor_scalar(ge, end, float(B0 + 1), None, ALU.is_ge))
            step(v.tensor_tensor(span[:, :], end, cnt, ALU.subtract))
            step(v.tensor_scalar(span[:, :], span[:, :], float(B0), None, ALU.is_lt))
            step(v.tensor_tensor(span[:, :], span[:, :], ge, ALU.mult))
            step(v.tensor_scalar(end, end, -1.0, 0.0, ALU.add, ALU.max))
            step(v.scalar_tensor_tensor(end, ge, float(OVER), end, ALU.mult, ALU.add))
            step(v.tensor_copy(rowidx[:, :], end))
            dve.sem_inc(stage_of("rowidx made"), 1)
            norms(1, NIT - 1)
            for n, key in ((0, end), (1, pre)):
                if n == 1:
                    step(v.tensor_copy(pre, node_i[:, :]))
                step(v.tensor_tensor(incl, span[:, :], key, ALU.mult))
                step(v.reduce_sum(small[:, 7, n:n + 1], incl, axis=AX))
            dve.sem_inc(stage_of("span parts made"), 1)
            step(v.tensor_scalar(degpos[:, :], cnt, 0.0, None, ALU.is_gt))
            step(v.tensor_tensor(solo[:, :], degpos[:, :], span[:, :], ALU.subtract))
            step(v.tensor_scalar(end, cnt, 1.0, None, ALU.max))
            step(v.reciprocal(end, end))
            step(v.tensor_tensor(invdeg[:, :], degpos[:, :], end, ALU.mult))
            dve.wait_ge(*stage("span parts summed"))
            step(v.tensor_copy(spanidx[:, :], P[:, 7, 128:130]))
            dve.sem_inc(stage_of("rows indexed"), 1)
            for hf, (ne, nn) in zip(halves, ((B0, (NPAIR - 1) * 128 + NLAST), (HALF, (NPAIR - 1) * 128))):
                step(v.memset(bnw[hf, 0:1], ne / E))
                step(v.memset(bnw[hf, 1:2], nn / N))
            for hf in halves:
                for hg in halves:
                    step(v.tensor_copy(both[hf, hg], ident[hf, hf]))
            dve.wait_ge(S("later weights loaded"), 16 * 16)
            for n in range(2):
                step(v.tensor_tensor(x[:, 0:NB, :], x[:, 0:NB, :],
                                     bias0[:, n, :].unsqueeze(1).to_broadcast([128, NB, D]), ALU.add))
            dve.wait_ge(*stage("self made"))
            add_to_x(4)
            dve.sem_inc(stage_of("x self added"), 1)

            aggs = agg[:, 0:NV].rearrange("p (b d) -> p b d", d=D)

            def merge_sum(layer, factor, done=None, then=None):
                spanf = small[:, 6, 0:NB]
                dve.wait_ge(S("tail loaded", layer), 16)
                step(v.tensor_tensor(spanf, span[:, :], factor, ALU.mult))
                step(v.tensor_tensor(tmp[:, 0:NB, :], tail[:, 0:D].unsqueeze(1).to_broadcast([128, NB, D]), bc(spanf),
                                     ALU.mult))
                step(v.memset(tmp[:, NB:NBP, :], 0.0))
                for part, r in PARTS.items():
                    dve.wait_ge(S(f"last rows {part}"), n_last_rows(layer, part))
                    step(v.tensor_tensor(aggs[:, r, :], aggs[:, r, :], bc(factor, r), ALU.mult))
                    step(v.tensor_tensor(tmp[:, r, :], tmp[:, r, :], aggs[:, r, :], ALU.add))
                    if done:
                        dve.sem_inc(stage_of(f"{done} {part}"), 1)
                    else:
                        then(part, r)

            merge_sum(0, invdeg[:, :], "L0 merged")
            for part, r in PARTS.items():
                dve.wait_ge(*stage(f"neigh made {part}"))
                add_to_x(4, r)
                layernorm_relu(h, f"h1 made {part}", r)

            step(v.memset(mrun[1][:, CH:CH + 1], -BIG))
            step(v.memset(srun[1][:, CH - 1:CH], 0.0))
            step(v.memset(orun[1][:, CH - 1:CH], 0.0))
            with dve.Fori(0, NIT) as i:
                for k in range(2):
                    dve.wait_ge(S("d loaded", k), past(i + 1, 16))
                    dve.wait_ge(S("L1 w2 transposed", k), past(i + 1))
                    v.tensor_tensor(soft[k][:, CH:2 * CH], P[:, 0, :], dch[k], ALU.add).then_inc(S("logits made", k), 1)
                    dve.wait_ge(S("out transposed", k), n_out_transposed(1, i))
                    dve.wait_ge(S("m scanned", 1 - k), past(i + k))
                    v.tensor_copy(mrun[k][:, 0:1], mrun[1 - k][:, CH:CH + 1]).then_inc(S("m carried", k), 1)
                    dve.wait_ge(S("in transposed", k), n_in_transposed(1, i + 1))
                    v.tensor_tensor(val[k], P[:, 1, :], dch[k], ALU.add).then_inc(S("u made", k), 1)
                    dve.wait_ge(S("neg made", k), past(i + 1))
                    dve.wait_ge(S("logits made", k), past(i + 1))
                    dve.wait_ge(S("m carried", k), past(i + 1))
                    v.tensor_tensor_scan(mrun[k][:, 1:CH + 1], neg[k], soft[k][:, CH:2 * CH], mrun[k][:, 0:1],
                                         ALU.add, ALU.max).then_inc(S("m scanned", k), 1)
                    dve.wait_ge(S("m scanned", k), past(i + 1))
                    v.tensor_tensor(soft[k][:, 0:CH], mrun[k][:, 0:CH], mrun[k][:, 1:CH + 1], ALU.subtract)
                    v.tensor_tensor(soft[k][:, CH:2 * CH], soft[k][:, CH:2 * CH], mrun[k][:, 1:CH + 1], ALU.subtract) \
                        .then_inc(S("diff made", k), 1)
                    damp, num = soft[k][:, 0:CH], soft[k][:, CH:2 * CH]
                    dve.wait_ge(S("expd made", k), past(i + 1))
                    dve.wait_ge(S("u made", k), past(i + 1))
                    v.scalar_tensor_tensor(damp, damp, 1.0, keep[:, at(i, k)], ALU.min, ALU.mult) \
                        .then_inc(S("damp made", k), 1)
                    v.tensor_tensor(val[k], num, val[k], ALU.mult).then_inc(S("eu made", k), 1)
                    dve.wait_ge(S("damp made", k), past(i + 1))
                    dve.wait_ge(S("scanned", 1 - k), n_scanned(1, i + k))
                    v.tensor_tensor_scan(srun[k], damp, num, srun[1 - k][:, CH - 1:CH],
                                         ALU.mult, ALU.add).then_inc(S("s scanned", k), 1)
                    dve.wait_ge(S("eu made", k), past(i + 1))
                    dve.wait_ge(S("s scanned", k), past(i + 1))
                    v.tensor_tensor_scan(orun[k], damp, val[k], orun[1 - k][:, CH - 1:CH],
                                         ALU.mult, ALU.add).then_inc(S("scanned", k), 1)

            def twice(vector):
                return vector.unsqueeze(1).to_broadcast([128, 2, D])

            fA, fB = factors[:, 0:D], factors[:, D:2 * D]
            so = span_row[:, D:3 * D].rearrange("p (n d) -> p n d", d=D)
            tso = tail_so.rearrange("p (n d) -> p n d", d=D)
            dve.wait_ge(S("tail loaded", 1), 16)
            dve.wait_ge(S("span rows"), 32)
            step(v.tensor_tensor(fA, tail[:, 0:D], span_w1, ALU.add))
            step(v.tensor_tensor(fB, span_row[:, 0:D], span_w1, ALU.add))
            step(v.tensor_tensor(span_max, fA, fB, ALU.max))
            step(v.tensor_tensor(factors.rearrange("p (n d) -> p n d", d=D), factors.rearrange("p (n d) -> p n d", d=D),
                                 twice(span_max), ALU.subtract))
            dve.sem_inc(stage_of("merge diffs made"), 1)
            dve.wait_ge(*stage("merge factors made"))
            step(v.tensor_tensor(so, so, twice(fB), ALU.mult))
            step(v.tensor_tensor(tso, tail[:, D:3 * D].rearrange("p (n d) -> p n d", d=D), twice(fA), ALU.mult))
            dve.sem_inc(stage_of("L1 tail merged"), 1)
            step(v.tensor_tensor(so, so, tso, ALU.add))
            step(v.reciprocal(so[:, 0, :], so[:, 0, :]))
            step(v.tensor_tensor(span_max, so[:, 1, :], so[:, 0, :], ALU.mult))
            step(v.tensor_tensor(tmp[:, 0:NB, :], span_max.unsqueeze(1).to_broadcast([128, NB, D]), bc(span[:, :]),
                                 ALU.mult))
            step(v.tensor_tensor(x[:, 0:NB, :], x[:, 0:NB, :], tmp[:, 0:NB, :], ALU.add))
            g = agg.rearrange("p (b d) -> p b d", d=3 * D)
            sB, oB = g[:, :, D:2 * D], g[:, :, 2 * D:3 * D]
            for part, r in PARTS.items():
                dve.wait_ge(S(f"last rows {part}"), n_last_rows(1, part))
                step(v.reciprocal(sB[:, r, :], sB[:, r, :]))
                step(v.tensor_tensor(oB[:, r, :], oB[:, r, :], sB[:, r, :], ALU.mult))
                step(v.tensor_tensor(oB[:, r, :], oB[:, r, :], bc(solo[:, :], r), ALU.mult))
                step(v.tensor_tensor(x[:, r, :], x[:, r, :], oB[:, r, :], ALU.add))
                layernorm_relu(h, f"h2 made {part}", r)

            def split_features(layer, table, done):
                rest = tmp[:, 0:NB, :]
                for n in range(3):
                    step(v.tensor_copy(split[layer][:, :, n, :], rest if n else table))
                    if n < 2:
                        step(v.tensor_tensor(rest, rest if n else table, split[layer][:, :, n, :], ALU.subtract))
                dve.sem_inc(stage_of(done), 1)

            def pick_onehots(layer, i, k):
                dve.wait_ge(S("src spread", k), n_picked(layer, i + 1, 16))
                dve.wait_ge(S("rows multiplied", k), n_picked(layer, i))
                v.tensor_tensor(pick[layer][k], srcb[layer][k][:, J - 1::J].unsqueeze(1).to_broadcast([128, NB, 128]),
                                node_i[:, :].unsqueeze(2).to_broadcast([128, NB, 128]), ALU.is_equal) \
                    .then_inc(S("pick onehots made", k), 1)

            def add_parts(layer, i, k, bank):
                dve.wait_ge(S("rows multiplied", k), n_picked(layer, i + 1))
                v.reduce_sum(Gw(k, D)[:, J - 1, 1, :], P[:, bank, 0:3 * D].rearrange("p (n d) -> p d n", n=3),
                             axis=AX).then_inc(S("rows picked", k), 1)

            dve.wait_ge(*stage("w1a copied b"))
            dve.wait_ge(S("w1 stored"), 16)
            split_features(2, tabs[:, 0:NB, 0:D], "w1a split")
            dve.wait_ge(S("table stored", 2), 32)

            def l2_body(i, picking, more=True):
                for k in range(2):
                    if picking and (k == 0 or more):
                        pick_onehots(2, i + k, 1 - k)
                    if picking:
                        dve.wait_ge(S("hidden made", k), past(i))
                        add_parts(2, i, k, 4 + k)
                    dve.wait_ge(S("hidden made", k), past(i + 1))
                    v.bn_stats(stats[:, bass.ds(i * 12 + k * 6, 6)], arena[:, at(i, k)]).then_inc(S("stats made"), 1)

            pick_onehots(2, 0, 0)
            with dve.Fori(0, NPICK - 1) as i:
                l2_body(i, True)
            l2_body(NPICK - 1, True, more=False)
            with dve.Fori(NPICK, NIT) as i:
                l2_body(i, False)
            dve.wait_ge(S("stats made"), NCH)
            step(v.bn_stats(stats[0:64, (NCH - 1) * 6:NCH * 6], arena[0:64, (NCH - 1) * CH:(NCH - 1) * CH + LASTA]))
            step(v.bn_aggr(bn[:, 0:2], stats[:, :]))

            def batchnorm(tag, wcol, gcol, bcol):
                share = bnw[:, wcol:wcol + 1]
                step(v.tensor_tensor(bn[:, 2:3], bn[:, 0:1], share, ALU.mult))
                dve.sem_inc(stage_of(f"{tag} mean part made"), 1)
                dve.wait_ge(*stage(f"{tag} mean summed"))
                step(v.tensor_copy(bn[:, 4:5], P[:, 7, 0:1]))
                step(v.tensor_tensor(bn[:, 7:8], bn[:, 0:1], bn[:, 4:5], ALU.subtract))
                step(v.tensor_tensor(bn[:, 7:8], bn[:, 7:8], bn[:, 7:8], ALU.mult))
                step(v.tensor_tensor(bn[:, 7:8], bn[:, 7:8], bn[:, 1:2], ALU.add))
                step(v.tensor_tensor(bn[:, 3:4], bn[:, 7:8], share, ALU.mult))
                dve.sem_inc(stage_of(f"{tag} var part made"), 1)
                dve.wait_ge(*stage(f"{tag} var summed"))
                step(v.tensor_scalar(rs[:, 0, 0:1], P[:, 7, 1:2], EPS, None, ALU.add))
                rsqrt(slice(0, 1), step)
                step(v.tensor_tensor(bn[:, 5:6], rs[:, 1, 0:1], cols[:, gcol:gcol + 1], ALU.mult))
                step(v.tensor_tensor(bn[:, 7:8], bn[:, 5:6], bn[:, 4:5], ALU.mult))
                step(v.tensor_tensor(bn[:, 6:7], cols[:, bcol:bcol + 1], bn[:, 7:8], ALU.subtract))
                dve.sem_inc(stage_of(f"{tag} ready"), 1)

            batchnorm("edge bn", 0, LG1, LBE1)

            step(v.memset(scanb[1][:, CH - 1:CH], 0.0))
            with dve.Fori(0, NIT) as i:
                for k in range(2):
                    if k == 0:
                        dve.wait_ge(S("edges activated"), i + 1)
                    dve.wait_ge(S("scanned", 1 - k), n_scanned(2, i + k))
                    dve.wait_ge(S("out transposed", k), n_out_transposed(2, i))
                    v.tensor_tensor_scan(scanb[k][:, :], keep[:, at(i, k)], arena[:, at(i, k)],
                                         scanb[1 - k][:, CH - 1:CH], ALU.mult, ALU.add).then_inc(S("scanned", k), 1)

            merge_sum(2, invdeg[:, :], "L2 merged")
            dve.wait_ge(*stage("z copied"))
            z = tabs[:, 0:NPAIR, :].rearrange("p b d -> p (b d)")
            for n in range(3):
                step(v.bn_stats(stats[:, n * 6:(n + 1) * 6], z[:, n * 512:(n + 1) * 512]))
            step(v.bn_stats(stats[0:64, 18:24], z[0:64, 1536:1536 + NLAST]))
            step(v.bn_aggr(bn[0:64, 0:2], stats[0:64, 0:24]))
            step(v.bn_aggr(bn[64:128, 0:2], stats[64:128, 0:18]))
            batchnorm("node bn", 1, LG2, LBE2)
            step(v.memset(h[:, NB:NBP, :], 0.0))
            for part, r in PARTS.items():
                dve.wait_ge(*stage(f"z transposed {part}"))
                add_to_x(0, r)
                layernorm_relu(h, f"h3 made {part}", r)

            split_features(3, h[:, 0:NB, :], "h3 split")

            def l3_body(i, more=True):
                for k in range(2):
                    if k == 0 or more:
                        pick_onehots(3, i + k, 1 - k)
                    dve.wait_ge(S("in transposed", k), n_in_transposed(3, i))
                    add_parts(3, i, k, k)
                    dve.wait_ge(S("in transposed", k), n_in_transposed(3, i + 1))
                    dve.wait_ge(S("scanned", 1 - k), n_scanned(3, i + k))
                    dve.wait_ge(S("out transposed", k), n_out_transposed(3, i))
                    v.tensor_tensor_scan(scanb[k][:, :], keep[:, at(i, k)], P[:, 4 + k, :],
                                         scanb[1 - k][:, CH - 1:CH], ALU.mult, ALU.add).then_inc(S("scanned", k), 1)

            step(v.memset(scanb[1][:, CH - 1:CH], 0.0))
            pick_onehots(3, 0, 0)
            with dve.Fori(0, NIT - 1) as i:
                l3_body(i)
            l3_body(NIT - 1, more=False)

            def finish(part, r):
                step(v.tensor_tensor(x[:, r, :], x[:, r, :], tmp[:, r, :], ALU.add))
                dve.sem_inc(stage_of(f"x4 made {part}"), 1)

            merge_sum(3, degpos[:, :], then=finish)

        for names in stages.values():
            got = [n for n in counted if n in names]
            assert got == list(names), [(a, b) for a, b in zip(got + [None] * 9, names) if a != b][:3]


def kernel(**inputs):
    import concourse.bacc as bacc
    from concourse.bass_utils import run_bass_kernel_spmd as run

    nc = bacc.Bacc("TRN2", target_bir_lowering=False, num_devices=1)
    arrays, args = {}, {}
    for name, value in inputs.items():
        value = np.ascontiguousarray(value)
        arrays[f"in_{name}"] = value
        args[name] = nc.dram_tensor(f"in_{name}", value.shape, mybir.dt.from_np(value.dtype),
                                    kind="ExternalInput").ap()
    out = nc.dram_tensor("out_x", (N, D), F32, kind="ExternalOutput").ap()
    build(nc, args, out)
    return run(nc, [arrays], core_ids=[0]).results[0]["out_x"]
```
